# Optimizing a Trainium2 kernel written in Bass

```python
import numpy as np
import jax
import jax.numpy as jnp

def _softmax(x, axis=-1):
    return jax.nn.softmax(x, axis=axis)

def _gelu(x):
    return jax.nn.gelu(x, approximate=True)

def _silu(x):
    return jax.nn.silu(x)

def _sigmoid(x):
    return jax.nn.sigmoid(x)

def _layernorm(x, axis=-1, eps=1e-05):
    m = jnp.mean(x, axis=axis, keepdims=True)
    v = jnp.var(x, axis=axis, keepdims=True)
    return (x - m) / jnp.sqrt(v + eps)

def _scatter_add(tgt, idx, src, axis=0):
    return tgt.at[idx].add(src)

def _segment_sum(src, seg, n):
    return jax.ops.segment_sum(src, seg, n)
kernel_name = 'mk_gnn_resnorm_d4_gnn_r8_a7d604'

def setup_inputs(seed: int=0):
    np.random.seed(seed)
    _w = jnp.asarray

    def _rec_inputs():
        import jax
        import jax.numpy as jnp
        _gk = jax.random.key(seed)
        x = -0.0001126 + 1 * jax.random.normal(jax.random.fold_in(_gk, 1), (1250, 768), jnp.float32)
        _s = jax.random.randint(jax.random.fold_in(_gk, 2), (10000,), 0, 1250, jnp.int32)
        _d = jax.random.randint(jax.random.fold_in(_gk, 3), (10000,), 0, 1250, jnp.int32)
        _loop = jnp.arange(1250, dtype=jnp.int32)
        src = jnp.concatenate([_s, _d, _loop])
        dst = jnp.concatenate([_d, _s, _loop])
        _o = jnp.argsort(dst, stable=True)
        src = src[_o]
        dst = dst[_o]
        return (x, src, dst)
    x, src, dst = _rec_inputs()

    def _L0_gnn_setup():
        import jax, jax.numpy as jnp
        import numpy as np
        N = 1250
        E = 12500
        D = 768
        H = 1536
        EPS_MSG = 1e-07
        EPS_BN = 1e-05

        def segment_softmax(logits, seg, num_segments):
            m = jax.ops.segment_max(logits, seg, num_segments=num_segments)
            m = jnp.where(jnp.isfinite(m), m, 0.0)
            e = jnp.exp(logits - m[seg])
            s = jax.ops.segment_sum(e, seg, num_segments=num_segments)
            return e / (s[seg] + 1e-16)
        key = jax.random.key(seed)
        ks = jax.random.split(key, 8)
        x = jax.random.normal(ks[0], (N, D), dtype=jnp.float32)
        edge_index = jax.random.randint(ks[1], (2, E), 0, N, dtype=jnp.int32)
        batch = jnp.zeros((N,), dtype=jnp.int32)
        t = jnp.asarray(1.0, dtype=jnp.float32)
        s1 = 1.0 / np.sqrt(D)
        s2 = 1.0 / np.sqrt(H)
        W1 = jax.random.uniform(ks[2], (D, H), jnp.float32, -s1, s1)
        b1 = jax.random.uniform(ks[3], (H,), jnp.float32, -s1, s1)
        bn_gamma = jnp.ones((H,), jnp.float32)
        bn_beta = jnp.zeros((H,), jnp.float32)
        bn_mean = jnp.zeros((H,), jnp.float32)
        bn_var = jnp.ones((H,), jnp.float32)
        W2 = jax.random.uniform(ks[4], (H, D), jnp.float32, -s2, s2)
        b2 = jax.random.uniform(ks[5], (D,), jnp.float32, -s2, s2)
        return {'x': x, 'edge_index': edge_index, 'batch': batch, 't': t, 'W1': W1, 'b1': b1, 'bn_gamma': bn_gamma, 'bn_beta': bn_beta, 'bn_mean': bn_mean, 'bn_var': bn_var, 'W2': W2, 'b2': b2}
    _L0_gnn_all = _L0_gnn_setup()
    _L0_gnn_in = {k: v for k, v in _L0_gnn_all.items() if k in ('t', 'W1', 'b1', 'bn_gamma', 'bn_beta', 'bn_mean', 'bn_var', 'W2', 'b2')}
    del _L0_gnn_all

    def _L1_gnn_setup():
        import jax, jax.numpy as jnp
        import numpy as np
        N_NODES = 1250
        N_EDGES = 10000
        IN_DIM, HID, OUT_DIM, HEADS = (768, 512, 768, 4)
        NEG_SLOPE = 0.2

        def _gat_layer(x, src, dst, W, a_src, a_dst, b, heads, d_out, concat):
            N = x.shape[0]
            h = (x @ W).reshape(N, heads, d_out)
            as_n = jnp.einsum('nhd,hd->nh', h, a_src)
            ad_n = jnp.einsum('nhd,hd->nh', h, a_dst)
            e = jax.nn.leaky_relu(as_n[src] + ad_n[dst], NEG_SLOPE)
            e_max = jax.lax.stop_gradient(jax.ops.segment_max(e, dst, num_segments=N))
            ex = jnp.exp(e - e_max[dst])
            denom = jax.ops.segment_sum(ex, dst, num_segments=N)
            alpha = ex / (denom[dst] + 1e-16)
            msg = alpha[:, :, None] * h[src]
            out = jax.ops.segment_sum(msg, dst, num_segments=N)
            out = out.reshape(N, heads * d_out) if concat else out.mean(axis=1)
            return out + b
        key = jax.random.key(seed)
        ks = jax.random.split(key, 10)
        g = 0.05
        return {'x': jax.random.normal(ks[0], (N_NODES, IN_DIM), jnp.float32), 'edge_index': jax.random.randint(ks[1], (2, N_EDGES), 0, N_NODES, jnp.int64), 'W1': jax.random.normal(ks[2], (IN_DIM, HEADS * HID), jnp.float32) * g, 'a1_src': jax.random.normal(ks[3], (HEADS, HID), jnp.float32) * g, 'a1_dst': jax.random.normal(ks[4], (HEADS, HID), jnp.float32) * g, 'b1': jnp.zeros((HEADS * HID,), jnp.float32), 'W2': jax.random.normal(ks[5], (HEADS * HID, OUT_DIM), jnp.float32) * g, 'a2_src': jax.random.normal(ks[6], (1, OUT_DIM), jnp.float32) * g, 'a2_dst': jax.random.normal(ks[7], (1, OUT_DIM), jnp.float32) * g, 'b2': jnp.zeros((OUT_DIM,), jnp.float32)}
    _L1_gnn_all = _L1_gnn_setup()
    _L1_gnn_in = {k: v for k, v in _L1_gnn_all.items() if k in ('W1', 'a1_src', 'a1_dst', 'b1', 'W2', 'a2_src', 'a2_dst', 'b2')}
    del _L1_gnn_all

    def _L2_gnn_setup():
        import jax, jax.numpy as jnp
        import numpy as np
        N = 1250
        E = 20000
        D = 768
        H1, C1 = (4, 192)
        H2, C2 = (2, 96)
        EPS = 1e-05
        NEG_SLOPE = 0.2

        def layer_norm(x, g, b):
            mu = x.mean(-1, keepdims=True)
            var = ((x - mu) ** 2).mean(-1, keepdims=True)
            return (x - mu) * jax.lax.rsqrt(var + EPS) * g + b

        def gat_conv(x, src, dst, W, a_src, a_dst, bias, H, C, n):
            h = (x @ W).reshape(n, H, C)
            s_src = (h * a_src).sum(-1)
            s_dst = (h * a_dst).sum(-1)
            e = jax.nn.leaky_relu(s_src[src] + s_dst[dst], NEG_SLOPE)
            emax = jax.ops.segment_max(e, dst, num_segments=n)
            ee = jnp.exp(e - emax[dst])
            denom = jax.ops.segment_sum(ee, dst, num_segments=n)
            alpha = ee / denom[dst]
            out = jax.ops.segment_sum(alpha[:, :, None] * h[src], dst, num_segments=n)
            return out.reshape(n, H * C) + bias
        key = jax.random.key(seed)
        ks = jax.random.split(key, 16)
        sd = 1.0 / np.sqrt(D)
        inp = {'x': jax.random.normal(ks[0], (N, D), jnp.float32), 'edge_index': jax.random.randint(ks[1], (2, E), 0, N, jnp.int64), 'norm_g': jnp.ones((D,), jnp.float32), 'norm_b': jnp.zeros((D,), jnp.float32), 'W1': jax.random.normal(ks[2], (D, H1 * C1), jnp.float32) * sd, 'a_src1': jax.random.normal(ks[3], (H1, C1), jnp.float32) * sd, 'a_dst1': jax.random.normal(ks[4], (H1, C1), jnp.float32) * sd, 'b1': jnp.zeros((H1 * C1,), jnp.float32), 'W2': jax.random.normal(ks[5], (H1 * C1, H2 * C2), jnp.float32) * sd, 'a_src2': jax.random.normal(ks[6], (H2, C2), jnp.float32) * sd, 'a_dst2': jax.random.normal(ks[7], (H2, C2), jnp.float32) * sd, 'b2': jnp.zeros((H2 * C2,), jnp.float32), 'Wu': jax.random.normal(ks[8], (D + H2 * C2, D), jnp.float32) / np.sqrt(D + H2 * C2), 'bu': jnp.zeros((D,), jnp.float32)}
        return inp
    _L2_gnn_all = _L2_gnn_setup()
    _L2_gnn_in = {k: v for k, v in _L2_gnn_all.items() if k in ('norm_g', 'norm_b', 'W1', 'a_src1', 'a_dst1', 'b1', 'W2', 'a_src2', 'a_dst2', 'b2', 'Wu', 'bu')}
    del _L2_gnn_all

    def _L3_gnn_setup():
        import jax, jax.numpy as jnp
        import numpy as np
        N_NODES = 1250
        NEG_SLOPE = 0.2
        EPS = 1e-16

        def gat_layer(x, W, att_src, att_dst, bias, src, dst, heads, out_ch, concat):
            n = x.shape[0]
            h = (x @ W.T).reshape(n, heads, out_ch)
            a_src = jnp.einsum('nhc,hc->nh', h, att_src)
            a_dst = jnp.einsum('nhc,hc->nh', h, att_dst)
            e = a_src[src] + a_dst[dst]
            e = jax.nn.leaky_relu(e, NEG_SLOPE)
            m = jax.ops.segment_max(e, dst, num_segments=n)
            ex = jnp.exp(e - m[dst])
            denom = jax.ops.segment_sum(ex, dst, num_segments=n)
            alpha = ex / (denom[dst] + EPS)
            msg = alpha[:, :, None] * h[src]
            out = jax.ops.segment_sum(msg, dst, num_segments=n)
            if concat:
                out = out.reshape(n, heads * out_ch)
            else:
                out = out.mean(axis=1)
            return out + bias
        key = jax.random.key(seed)
        ks = jax.random.split(key, 12)
        x = jax.random.normal(ks[0], (N_NODES, 768), dtype=jnp.float32)
        edge_index = jax.random.randint(ks[1], (2, 20000), 0, N_NODES, dtype=jnp.int64)
        s1 = 1.0 / np.sqrt(768.0)
        W1 = jax.random.normal(ks[2], (8 * 128, 768), dtype=jnp.float32) * s1
        att_src1 = jax.random.normal(ks[3], (8, 128), dtype=jnp.float32) * (1.0 / np.sqrt(128.0))
        att_dst1 = jax.random.normal(ks[4], (8, 128), dtype=jnp.float32) * (1.0 / np.sqrt(128.0))
        b1 = jnp.zeros((8 * 128,), dtype=jnp.float32)
        s2 = 1.0 / np.sqrt(1024.0)
        W2 = jax.random.normal(ks[5], (1 * 768, 1024), dtype=jnp.float32) * s2
        att_src2 = jax.random.normal(ks[6], (1, 768), dtype=jnp.float32) * (1.0 / np.sqrt(768.0))
        att_dst2 = jax.random.normal(ks[7], (1, 768), dtype=jnp.float32) * (1.0 / np.sqrt(768.0))
        b2 = jnp.zeros((768,), dtype=jnp.float32)
        return {'x': x, 'edge_index': edge_index, 'W1': W1, 'att_src1': att_src1, 'att_dst1': att_dst1, 'b1': b1, 'W2': W2, 'att_src2': att_src2, 'att_dst2': att_dst2, 'b2': b2}
    _L3_gnn_all = _L3_gnn_setup()
    _L3_gnn_in = {k: v for k, v in _L3_gnn_all.items() if k in ('W1', 'att_src1', 'att_dst1', 'b1', 'W2', 'att_src2', 'att_dst2', 'b2')}
    del _L3_gnn_all
    return {'x': x, 'src': src, 'dst': dst, 'L0_gnn_t': _L0_gnn_in['t'], 'L0_gnn_W1': _L0_gnn_in['W1'], 'L0_gnn_b1': _L0_gnn_in['b1'], 'L0_gnn_bn_gamma': _L0_gnn_in['bn_gamma'], 'L0_gnn_bn_beta': _L0_gnn_in['bn_beta'], 'L0_gnn_bn_mean': _L0_gnn_in['bn_mean'], 'L0_gnn_bn_var': _L0_gnn_in['bn_var'], 'L0_gnn_W2': _L0_gnn_in['W2'], 'L0_gnn_b2': _L0_gnn_in['b2'], 'L1_gnn_W1': _L1_gnn_in['W1'], 'L1_gnn_a1_src': _L1_gnn_in['a1_src'], 'L1_gnn_a1_dst': _L1_gnn_in['a1_dst'], 'L1_gnn_b1': _L1_gnn_in['b1'], 'L1_gnn_W2': _L1_gnn_in['W2'], 'L1_gnn_a2_src': _L1_gnn_in['a2_src'], 'L1_gnn_a2_dst': _L1_gnn_in['a2_dst'], 'L1_gnn_b2': _L1_gnn_in['b2'], 'L2_gnn_norm_g': _L2_gnn_in['norm_g'], 'L2_gnn_norm_b': _L2_gnn_in['norm_b'], 'L2_gnn_W1': _L2_gnn_in['W1'], 'L2_gnn_a_src1': _L2_gnn_in['a_src1'], 'L2_gnn_a_dst1': _L2_gnn_in['a_dst1'], 'L2_gnn_b1': _L2_gnn_in['b1'], 'L2_gnn_W2': _L2_gnn_in['W2'], 'L2_gnn_a_src2': _L2_gnn_in['a_src2'], 'L2_gnn_a_dst2': _L2_gnn_in['a_dst2'], 'L2_gnn_b2': _L2_gnn_in['b2'], 'L2_gnn_Wu': _L2_gnn_in['Wu'], 'L2_gnn_bu': _L2_gnn_in['bu'], 'L3_gnn_W1': _L3_gnn_in['W1'], 'L3_gnn_att_src1': _L3_gnn_in['att_src1'], 'L3_gnn_att_dst1': _L3_gnn_in['att_dst1'], 'L3_gnn_b1': _L3_gnn_in['b1'], 'L3_gnn_W2': _L3_gnn_in['W2'], 'L3_gnn_att_src2': _L3_gnn_in['att_src2'], 'L3_gnn_att_dst2': _L3_gnn_in['att_dst2'], 'L3_gnn_b2': _L3_gnn_in['b2']}

def reference(x, src, dst, L0_gnn_t, L0_gnn_W1, L0_gnn_b1, L0_gnn_bn_gamma, L0_gnn_bn_beta, L0_gnn_bn_mean, L0_gnn_bn_var, L0_gnn_W2, L0_gnn_b2, L1_gnn_W1, L1_gnn_a1_src, L1_gnn_a1_dst, L1_gnn_b1, L1_gnn_W2, L1_gnn_a2_src, L1_gnn_a2_dst, L1_gnn_b2, L2_gnn_norm_g, L2_gnn_norm_b, L2_gnn_W1, L2_gnn_a_src1, L2_gnn_a_dst1, L2_gnn_b1, L2_gnn_W2, L2_gnn_a_src2, L2_gnn_a_dst2, L2_gnn_b2, L2_gnn_Wu, L2_gnn_bu, L3_gnn_W1, L3_gnn_att_src1, L3_gnn_att_dst1, L3_gnn_b1, L3_gnn_W2, L3_gnn_att_src2, L3_gnn_att_dst2, L3_gnn_b2):
    import jax
    import jax.numpy as jnp

    def _L0_gnn_ref(x, edge_index, batch, t, W1, b1, bn_gamma, bn_beta, bn_mean, bn_var, W2, b2):
        import jax, jax.numpy as jnp
        import numpy as np
        N = 1250
        E = 12500
        D = 768
        H = 1536
        EPS_MSG = 1e-07
        EPS_BN = 1e-05

        def segment_softmax(logits, seg, num_segments):
            m = jax.ops.segment_max(logits, seg, num_segments=num_segments)
            m = jnp.where(jnp.isfinite(m), m, 0.0)
            e = jnp.exp(logits - m[seg])
            s = jax.ops.segment_sum(e, seg, num_segments=num_segments)
            return e / (s[seg] + 1e-16)
        src, dst = (edge_index[0], edge_index[1])
        msg = jax.nn.relu(x[src]) + EPS_MSG
        alpha = segment_softmax(msg * t, dst, N)
        agg = jax.ops.segment_sum(msg * alpha, dst, num_segments=N)
        out = agg + x
        z = out @ W1 + b1
        z = (z - bn_mean) * jax.lax.rsqrt(bn_var + EPS_BN) * bn_gamma + bn_beta
        z = jax.nn.relu(z)
        z = z @ W2 + b2
        return x + z

    def _L1_gnn_ref(x, edge_index, W1, a1_src, a1_dst, b1, W2, a2_src, a2_dst, b2):
        import jax, jax.numpy as jnp
        import numpy as np
        N_NODES = 1250
        N_EDGES = 10000
        IN_DIM, HID, OUT_DIM, HEADS = (768, 512, 768, 4)
        NEG_SLOPE = 0.2

        def _gat_layer(x, src, dst, W, a_src, a_dst, b, heads, d_out, concat):
            N = x.shape[0]
            h = (x @ W).reshape(N, heads, d_out)
            as_n = jnp.einsum('nhd,hd->nh', h, a_src)
            ad_n = jnp.einsum('nhd,hd->nh', h, a_dst)
            e = jax.nn.leaky_relu(as_n[src] + ad_n[dst], NEG_SLOPE)
            e_max = jax.lax.stop_gradient(jax.ops.segment_max(e, dst, num_segments=N))
            ex = jnp.exp(e - e_max[dst])
            denom = jax.ops.segment_sum(ex, dst, num_segments=N)
            alpha = ex / (denom[dst] + 1e-16)
            msg = alpha[:, :, None] * h[src]
            out = jax.ops.segment_sum(msg, dst, num_segments=N)
            out = out.reshape(N, heads * d_out) if concat else out.mean(axis=1)
            return out + b
        N = x.shape[0]
        loops = jnp.arange(N, dtype=edge_index.dtype)
        src = jnp.concatenate([edge_index[0], loops])
        dst = jnp.concatenate([edge_index[1], loops])
        h = _gat_layer(x, src, dst, W1, a1_src, a1_dst, b1, HEADS, HID, True)
        h = jax.nn.elu(h)
        out = _gat_layer(h, src, dst, W2, a2_src, a2_dst, b2, 1, OUT_DIM, False)
        return out

    def _L2_gnn_ref(x, edge_index, norm_g, norm_b, W1, a_src1, a_dst1, b1, W2, a_src2, a_dst2, b2, Wu, bu):
        import jax, jax.numpy as jnp
        import numpy as np
        N = 1250
        E = 20000
        D = 768
        H1, C1 = (4, 192)
        H2, C2 = (2, 96)
        EPS = 1e-05
        NEG_SLOPE = 0.2

        def layer_norm(x, g, b):
            mu = x.mean(-1, keepdims=True)
            var = ((x - mu) ** 2).mean(-1, keepdims=True)
            return (x - mu) * jax.lax.rsqrt(var + EPS) * g + b

        def gat_conv(x, src, dst, W, a_src, a_dst, bias, H, C, n):
            h = (x @ W).reshape(n, H, C)
            s_src = (h * a_src).sum(-1)
            s_dst = (h * a_dst).sum(-1)
            e = jax.nn.leaky_relu(s_src[src] + s_dst[dst], NEG_SLOPE)
            emax = jax.ops.segment_max(e, dst, num_segments=n)
            ee = jnp.exp(e - emax[dst])
            denom = jax.ops.segment_sum(ee, dst, num_segments=n)
            alpha = ee / denom[dst]
            out = jax.ops.segment_sum(alpha[:, :, None] * h[src], dst, num_segments=n)
            return out.reshape(n, H * C) + bias
        loops = jnp.arange(N, dtype=edge_index.dtype)
        src = jnp.concatenate([edge_index[0], loops])
        dst = jnp.concatenate([edge_index[1], loops])
        x_norm = layer_norm(x, norm_g, norm_b)
        out1 = gat_conv(x_norm, src, dst, W1, a_src1, a_dst1, b1, H1, C1, N)
        out2 = gat_conv(out1, src, dst, W2, a_src2, a_dst2, b2, H2, C2, N)
        combined = jnp.concatenate([x, out2], axis=-1)
        return combined @ Wu + bu

    def _L3_gnn_ref(x, edge_index, W1, att_src1, att_dst1, b1, W2, att_src2, att_dst2, b2):
        import jax, jax.numpy as jnp
        import numpy as np
        N_NODES = 1250
        NEG_SLOPE = 0.2
        EPS = 1e-16

        def gat_layer(x, W, att_src, att_dst, bias, src, dst, heads, out_ch, concat):
            n = x.shape[0]
            h = (x @ W.T).reshape(n, heads, out_ch)
            a_src = jnp.einsum('nhc,hc->nh', h, att_src)
            a_dst = jnp.einsum('nhc,hc->nh', h, att_dst)
            e = a_src[src] + a_dst[dst]
            e = jax.nn.leaky_relu(e, NEG_SLOPE)
            m = jax.ops.segment_max(e, dst, num_segments=n)
            ex = jnp.exp(e - m[dst])
            denom = jax.ops.segment_sum(ex, dst, num_segments=n)
            alpha = ex / (denom[dst] + EPS)
            msg = alpha[:, :, None] * h[src]
            out = jax.ops.segment_sum(msg, dst, num_segments=n)
            if concat:
                out = out.reshape(n, heads * out_ch)
            else:
                out = out.mean(axis=1)
            return out + bias
        src, dst = (edge_index[0], edge_index[1])
        h = gat_layer(x, W1, att_src1, att_dst1, b1, src, dst, heads=8, out_ch=128, concat=True)
        h = jax.nn.relu(h)
        out = gat_layer(h, W2, att_src2, att_dst2, b2, src, dst, heads=1, out_ch=768, concat=True)
        return out
    edge_index = jnp.stack([src, dst])
    batch0 = jnp.zeros((1250,), jnp.int32)
    x = _layernorm(x + _L0_gnn_ref(x, edge_index, batch0, L0_gnn_t, L0_gnn_W1, L0_gnn_b1, L0_gnn_bn_gamma, L0_gnn_bn_beta, L0_gnn_bn_mean, L0_gnn_bn_var, L0_gnn_W2, L0_gnn_b2), axis=-1)
    x = _layernorm(x + _L1_gnn_ref(x, edge_index, L1_gnn_W1, L1_gnn_a1_src, L1_gnn_a1_dst, L1_gnn_b1, L1_gnn_W2, L1_gnn_a2_src, L1_gnn_a2_dst, L1_gnn_b2), axis=-1)
    x = _layernorm(x + _L2_gnn_ref(x, edge_index, L2_gnn_norm_g, L2_gnn_norm_b, L2_gnn_W1, L2_gnn_a_src1, L2_gnn_a_dst1, L2_gnn_b1, L2_gnn_W2, L2_gnn_a_src2, L2_gnn_a_dst2, L2_gnn_b2, L2_gnn_Wu, L2_gnn_bu), axis=-1)
    x = _layernorm(x + _L3_gnn_ref(x, edge_index, L3_gnn_W1, L3_gnn_att_src1, L3_gnn_att_dst1, L3_gnn_b1, L3_gnn_W2, L3_gnn_att_src2, L3_gnn_att_dst2, L3_gnn_b2), axis=-1)
    return x

_drawn_inputs = setup_inputs


def setup_inputs(seed=0):
    import zlib

    import numpy as np

    out = dict(_drawn_inputs(seed))
    spreads = {'L0_gnn_bn_gamma': (1.0, 0.2),
     'L0_gnn_bn_beta': (0.0, 0.1),
     'L0_gnn_bn_mean': (0.0, 0.1),
     'L0_gnn_bn_var': (1.0, 0.2),
     'L1_gnn_b1': (0.0, 0.1),
     'L1_gnn_b2': (0.0, 0.1),
     'L2_gnn_norm_g': (1.0, 0.2),
     'L2_gnn_norm_b': (0.0, 0.1),
     'L2_gnn_b1': (0.0, 0.1),
     'L2_gnn_b2': (0.0, 0.1),
     'L2_gnn_bu': (0.0, 0.1),
     'L3_gnn_b1': (0.0, 0.1),
     'L3_gnn_b2': (0.0, 0.1)}
    factors = {'L0_gnn_b1': 5.593,
     'L0_gnn_b2': 2.816,
     'L2_gnn_a_src1': 4.59,
     'L2_gnn_a_dst1': 8.0,
     'L2_gnn_a_src2': 8.0,
     'L2_gnn_a_dst2': 8.0,
     'L3_gnn_att_dst1': 5.015,
     'L3_gnn_att_src2': 8.0,
     'L3_gnn_att_dst2': 8.0}
    for name, (base, spread) in spreads.items():
        noise = np.random.default_rng([zlib.crc32(name.encode()), seed]).standard_normal(out[name].shape)
        drawn = base * np.exp(spread * noise) if base else spread * noise
        out[name] = jnp.asarray(drawn.astype(out[name].dtype))
    for name, factor in factors.items():
        out[name] = (out[name] * factor).astype(out[name].dtype)
    return out
```

```python
from contextlib import ExitStack

import concourse.bass as bass
from concourse import mybir

ALU = mybir.AluOpType
ACT = mybir.ActivationFunctionType
AX = mybir.AxisListType
F32 = mybir.dt.float32
F32R = mybir.dt.float32r
F16 = mybir.dt.float16
I32 = mybir.dt.int32
U16 = mybir.dt.uint16

P = 128
BANK = 512
NO_EDGE = -1.0e30
LN_EPS = 1e-5
EPS_MSG = 1e-7
W_SCALE = 64.0


def bass_gnn_kernel(nc: bass.Bass, ins, out: bass.AP):
    x_d, src_d, dst_d = ins["x"], ins["src"], ins["dst"]
    N, D = x_d.shape
    E = src_d.shape[0]
    T = -(-N // P)
    assert T % 2 == 0
    NP = T * P
    LAST = N - (T - 1) * P
    CHUNKS = [(a, min(a + BANK, NP)) for a in range(0, NP, BANK)]
    HALF = NP // 2
    HB = HALF // P

    root = ExitStack()
    with root:
        ps = root.enter_context(nc.psum_tensor("ps", [P, 8 * BANK], F32))

        def bank(b, width):
            return ps[:, b * BANK:b * BANK + width]

        def sb(ctx, name, shape, dt):
            return ctx.enter_context(nc.sbuf_tensor(name, shape, dt))

        in_use = []

        def sem(name):
            in_use.append(nc.alloc_semaphore(name))
            return in_use[-1]

        def recycle_semaphores():
            nc.clear_and_free_semaphores(in_use)
            in_use.clear()
            nc.all_engine_barrier()

        def over_partitions(ap):
            return ap.rearrange("(o f) -> o f", o=1).to_broadcast([P, ap.shape[0]])

        ident = sb(root, "ident", [P, P], F32)
        ones = sb(root, "ones", [P, P], F32)

        x_spill = nc.dram_tensor("x_spill", (NP, D), F32, kind="Internal").ap().rearrange("(t p) c -> p t c", p=P)
        logc_d = nc.dram_tensor("logc_d", (NP, NP), F32, kind="Internal").ap().rearrange("(t p) s -> p t s", p=P)
        logc_diag_d = nc.dram_tensor("logc_diag_d", (P, T, P), F32, kind="Internal").ap()
        src_rows_d = nc.dram_tensor("src_rows_d", (16, NP), F32, kind="Internal").ap()

        def count_edges(count):
            R, REM = divmod(E, P)
            G = -(-(R + 1) // P)
            PAIRS = -(-(R + 1) // 2)
            FULL = R - (G - 1) * P
            FAR = 1000.0
            assert REM and G == 2 and PAIRS < FAR
            with ExitStack() as ctx:
                edges = sb(ctx, "edges", [P, 2, G, P], I32)
                edges_f = sb(ctx, "edges_f", [P, 2, G, P], F32)
                edge_cols = sb(ctx, "edge_cols", [P, 2 * G * P], F32)
                iota = sb(ctx, "iota", [P, NP], F16)
                zeros = sb(ctx, "zeros", [P, P], F16)
                before = sb(ctx, "before", [T, T], F32)
                pair_no = sb(ctx, "pair_no", [T, PAIRS], F32)
                block_ends = sb(ctx, "block_ends", [T, 2], F32)
                tile_ends = sb(ctx, "tile_ends", [P, 2 * G], F32)
                diag = sb(ctx, "diag", [P, 2 * G * P], F32)
                pair_ends = sb(ctx, "pair_ends", [T, 2, P], F32)
                holds = sb(ctx, "holds", [T, 3, PAIRS], F32)
                span = sb(ctx, "span", [T, 3], F32)
                table = sb(ctx, "table", [1, 3 * T], I32)
                hot_dst = sb(ctx, "hot_dst", [P, 2, P], F16)
                hot_src = sb(ctx, "hot_src", [P, 2, NP], F16)
                consts, loaded = sem("g_consts"), sem("g_loaded")
                dve, pe_pre = sem("g_dve"), sem("g_pe_pre")
                hot_ready, hot_free = sem("g_hot_ready"), sem("g_hot_free")
                block_done, block_saved = sem("g_block_done"), sem("g_block_saved")
                N_CONST = 11

                with nc.Block() as block:
                    @block.gpsimd
                    def _(pool):
                        pool.memset(edges[:, 0], NP - 1).then_inc(consts, 1)
                        pool.memset(edges[:, 1], -1).then_inc(consts, 1)
                        pool.memset(ident[:], 0.0).then_inc(consts, 1)
                        pool.memset(ones[:], 1.0).then_inc(consts, 1)
                        pool.memset(zeros[:], 0.0).then_inc(consts, 1)
                        pool.iota(iota[:], [[1, NP]], base=0, channel_multiplier=0,
                                  allow_small_or_imprecise_dtypes=True).then_inc(consts, 1)
                        pool.iota(pair_no[:], [[1, PAIRS]], base=0, channel_multiplier=0,
                                  allow_small_or_imprecise_dtypes=True).then_inc(consts, 1)
                        pool.iota(block_ends[:], [[P, 2]], base=0, channel_multiplier=P,
                                  allow_small_or_imprecise_dtypes=True).then_inc(consts, 1)
                        pool.sem_inc(hot_free, 2)
                        pool.wait_ge(consts, 4)
                        pool.affine_select(out=ident[:], in_=ident[:], compare_op=ALU.not_equal, fill=1.0, base=0,
                                           pattern=[[-1, P]], channel_multiplier=1).then_inc(consts, 1)
                        pool.affine_select(out=before[:], in_=ones[0:T, 0:T], compare_op=ALU.is_gt, fill=0.0, base=0,
                                           pattern=[[1, T]], channel_multiplier=-1).then_inc(consts, 2)

                    @block.sync
                    def _(sp):
                        sp.wait_ge(consts, 2)
                        for k, a in ((0, dst_d), (1, src_d)):
                            first = (G - 1) * P * P
                            sp.dma_start(edges[:, k, 0, :],
                                         a[0:first].rearrange("(t e) -> t e", e=P)).then_inc(loaded, 16)
                            sp.dma_start(edges[0:FULL, k, 1, :],
                                         a[first:R * P].rearrange("(t e) -> t e", e=P)).then_inc(loaded, 16)
                            sp.dma_start(edges[FULL:FULL + 1, k, 1, 0:REM],
                                         a[R * P:E].rearrange("(t e) -> t e", e=REM)).then_inc(loaded, 16)

                    @block.vector
                    def _(v):
                        done = [0]

                        def step(ins):
                            done[0] += 1
                            ins.then_inc(dve, 1)
                            v.wait_ge(dve, done[0])

                        v.wait_ge(consts, N_CONST)
                        v.wait_ge(loaded, 6 * 16)
                        step(v.tensor_copy(edges_f[:], edges[:]))
                        step(v.tensor_reduce(tile_ends[:, 0:G], edges_f[:, 0], AX.X, ALU.min))
                        step(v.tensor_reduce(tile_ends[:, G:2 * G], edges_f[:, 0], AX.X, ALU.max))
                        for k in range(2 * G):
                            step(v.tensor_scalar(diag[:, k * P:(k + 1) * P], ident[:], tile_ends[:, k:k + 1], None,
                                                 ALU.mult))
                        v.wait_ge(pe_pre, 1)
                        step(v.tensor_copy(edge_cols[:], bank(0, 2 * G * P)))
                        v.wait_ge(pe_pre, 2)
                        for k, op in ((0, ALU.min), (1, ALU.max)):
                            step(v.tensor_reduce(
                                pair_ends[:, k],
                                bank(1, BANK)[0:T, k * G * P:(k + 1) * G * P].rearrange("b (j two) -> b j two", two=2),
                                AX.X, op))
                        step(v.tensor_scalar(holds[:, 0], pair_ends[:, 0, 0:PAIRS], block_ends[:, 1:2], None,
                                             ALU.is_lt))
                        step(v.scalar_tensor_tensor(out=holds[:, 1], in0=pair_ends[:, 1, 0:PAIRS],
                                                    scalar=block_ends[:, 0:1], in1=holds[:, 0], op0=ALU.is_ge,
                                                    op1=ALU.mult))
                        step(v.scalar_tensor_tensor(out=holds[:, 0], in0=holds[:, 1], scalar=-FAR, in1=pair_no[:],
                                                    op0=ALU.mult, op1=ALU.add))
                        step(v.tensor_reduce(span[:, 0:1], holds[:, 0], AX.X, ALU.min))
                        step(v.scalar_tensor_tensor(out=holds[:, 2], in0=pair_no[:], scalar=1.0, in1=holds[:, 1],
                                                    op0=ALU.add, op1=ALU.mult))
                        step(v.tensor_reduce(span[:, 1:2], holds[:, 2], AX.X, ALU.max))
                        step(v.tensor_scalar(span[:, 0:1], span[:, 0:1], FAR, float(PAIRS - 1), ALU.add, ALU.min))
                        step(v.tensor_scalar(span[:, 2:3], span[:, 1:2], span[:, 0:1], 1.0, ALU.subtract, ALU.max))
                        v.wait_ge(pe_pre, 3)
                        step(v.tensor_copy(table[:], bank(2, 3 * T)[0:1, :]))
                        with v.Fori(0, T) as b:
                            first = v.value_load(table[0:1, bass.ds(b, 1)], min_val=0, max_val=PAIRS - 1)
                            pairs = v.value_load(table[0:1, bass.ds(b + T, 1)], min_val=1, max_val=PAIRS)
                            past = v.value_load(table[0:1, bass.ds(b + 2 * T, 1)], min_val=0, max_val=T * PAIRS)
                            with v.Fori(0, pairs) as j:
                                t = ((first + j) * 2).with_bounds(min_val=0, max_val=2 * PAIRS - 2)
                                for k in range(2):
                                    v.wait_ge(hot_free, (past + j) * 2 + (k + 1))
                                    v.tensor_scalar(hot_dst[:, k], iota[:, bass.ds(b * P, P)],
                                                    edge_cols[:, bass.ds(t + k, 1)], None, ALU.is_equal)
                                    v.tensor_scalar(hot_src[:, k], iota[:], edge_cols[:, bass.ds(t + (k + G * P), 1)],
                                                    None, ALU.is_equal).then_inc(hot_ready, 1)

                    @block.tensor
                    def _(pe):
                        pe.wait_ge(consts, N_CONST)
                        pe.wait_ge(dve, 1)
                        flat = edges_f[:].rearrange("p a g e -> p (a g e)")
                        for k in range(2 * G):
                            mm = pe.transpose(bank(0, BANK)[:, k * P:(k + 1) * P], flat[:, k * P:(k + 1) * P], ident[:])
                        mm.then_inc(pe_pre, 1)
                        pe.wait_ge(dve, 3 + 2 * G)
                        pe.matmul(bank(1, BANK)[0:T, :], ones[:, 0:T], diag[:], start=True,
                                  stop=True).then_inc(pe_pre, 1)
                        pe.wait_ge(dve, 14 + 2 * G)
                        rows = bank(2, 3 * T)
                        pe.matmul(rows[0:1, 0:T], span[:, 0:1], ident[0:T, 0:T], start=True, stop=True)
                        pe.matmul(rows[0:1, T:2 * T], span[:, 2:3], ident[0:T, 0:T], start=True, stop=True)
                        pe.matmul(rows[0:1, 2 * T:3 * T], span[:, 2:3], before[:], start=True,
                                  stop=True).then_inc(pe_pre, 1)
                        pe.wait_ge(dve, 15 + 2 * G)
                        with pe.Fori(0, T // 2) as b2:
                            for r in range(2):
                                b = b2 * 2 + r
                                base = 4 * r
                                pairs = pe.value_load(table[0:1, bass.ds(b + T, 1)], min_val=1, max_val=PAIRS)
                                past = pe.value_load(table[0:1, bass.ds(b + 2 * T, 1)], min_val=0, max_val=T * PAIRS)
                                pe.wait_ge(block_saved, b + 1)
                                for a, z in CHUNKS:
                                    pe.matmul(ps[:, base * BANK + a:base * BANK + z], zeros[:], iota[:, a:z],
                                              start=True, stop=False, skip_group_check=True)
                                with pe.Fori(0, pairs) as j:
                                    for k in range(2):
                                        pe.wait_ge(hot_ready, (past + j) * 2 + (k + 1))
                                        for a, z in CHUNKS:
                                            mm = pe.matmul(ps[:, base * BANK + a:base * BANK + z], hot_dst[:, k],
                                                           hot_src[:, k, a:z], start=False, stop=False,
                                                           skip_group_check=True)
                                        mm.then_inc(hot_free, 1)
                                for a, z in CHUNKS:
                                    mm = pe.matmul(ps[:, base * BANK + a:base * BANK + z], zeros[:], iota[:, a:z],
                                                   start=False, stop=True, skip_group_check=True)
                                mm.then_inc(block_done, 1)

                    @block.scalar
                    def _(act):
                        act.sem_inc(block_saved, 2)
                        with act.Fori(0, T // 2) as b2:
                            for r in range(2):
                                b = b2 * 2 + r
                                act.wait_ge(block_done, b + 1)
                                act.activation(count[:, bass.ds(b, 1)].rearrange("p o s -> p (o s)"),
                                               ps[:, 4 * r * BANK:4 * r * BANK + NP], ACT.Copy).then_inc(block_saved, 1)

        def log_counts(count):
            WIDTH = NP + P
            with ExitStack() as ctx:
                counts = sb(ctx, "counts", [P, 2, WIDTH], F32)
                atleast = sb(ctx, "atleast", [P, 2, WIDTH], F32)
                missing = sb(ctx, "missing", [P, 2, WIDTH], F32)
                logs = sb(ctx, "logs", [P, 2, WIDTH], F32)
                taken, looped = sem("c_taken"), sem("c_looped")
                clipped, logged, summed = sem("c_clipped"), sem("c_logged"), sem("c_summed")
                stored = [sem("c_stored0"), sem("c_stored1")]
                with nc.Block() as block:
                    @block.gpsimd
                    def _(pool):
                        for i in range(T):
                            r = i % 2
                            if i >= 2:
                                pool.wait_ge(clipped, 2 * i - 2)
                            pool.tensor_copy(counts[:, r, 0:NP], count[:, i]).then_inc(taken, 1)
                            pool.tensor_copy(counts[:, r, NP:WIDTH], count[:, i, i * P:(i + 1) * P]).then_inc(taken, 1)
                            pool.wait_ge(taken, 2 * i + 1)
                            own = counts[:, r, i * P:(i + 1) * P]
                            pool.tensor_tensor(own, own, ident[:], ALU.add).then_inc(looped, 1)

                    @block.vector
                    def _(v):
                        def clip(i):
                            r = i % 2
                            v.wait_ge(looped, i + 1)
                            v.wait_ge(taken, 2 * i + 2)
                            v.tensor_scalar(atleast[:, r], counts[:, r], 1.0, None, ALU.max).then_inc(clipped, 1)
                            v.tensor_scalar(missing[:, r], counts[:, r], 0.0, NO_EDGE, ALU.is_equal,
                                            ALU.mult).then_inc(clipped, 1)

                        clip(0)
                        for i in range(T):
                            if i + 1 < T:
                                clip(i + 1)
                            v.wait_ge(clipped, 2 * i + 2)
                            v.wait_ge(logged, i + 1)
                            v.tensor_tensor(missing[:, i % 2], missing[:, i % 2], logs[:, i % 2],
                                            ALU.add).then_inc(summed, 1)
                            v.wait_ge(stored[i % 2], 32 * (i // 2 + 1))

                    @block.scalar
                    def _(act):
                        for i in range(T):
                            act.wait_ge(clipped, 2 * i + 1)
                            if i >= 2:
                                act.wait_ge(summed, i - 1)
                            act.activation(logs[:, i % 2], atleast[:, i % 2], ACT.Ln).then_inc(logged, 1)

                    @block.sync
                    def _(sp):
                        for i in range(T):
                            sp.wait_ge(summed, i + 1)
                            sp.dma_start(logc_d[:, i], missing[:, i % 2, 0:NP]).then_inc(stored[i % 2], 16)
                            sp.dma_start(logc_diag_d[:, i], missing[:, i % 2, NP:WIDTH]).then_inc(stored[i % 2], 16)

        def channel_softmax(x, count, t_d):
            WIDE = 2 * D
            wide_chunks = [(a, min(a + BANK, WIDE)) for a in range(0, WIDE, BANK)]
            OUT0 = 4
            with ExitStack() as ctx:
                hi = sb(ctx, "sm_hi", [P, T, WIDE], F32R)
                lo = sb(ctx, "sm_lo", [P, T, WIDE], F32R)
                tcol = sb(ctx, "tcol", [P, 1], F32)
                peak = sb(ctx, "peak", [P, T + 2], F32)
                peak_row = sb(ctx, "peak_row", [1, 2], F32)
                msg = sb(ctx, "msg", [P, D], F32)
                both = sb(ctx, "both", [P, WIDE], F32)
                countf = both
                count_t = sb(ctx, "count_t", [P, T, P], F32R)
                sums = sb(ctx, "sums", [P, WIDE], F32)
                x_in, t_in = sem("m_x_in"), sem("m_t_in")
                zeroed, dve, pe_pre = sem("m_zeroed"), sem("m_dve"), sem("m_pe_pre")
                exps, his, los = sem("m_exps"), sem("m_his"), sem("m_los")
                with nc.Block() as block:
                    @block.gpsimd
                    def _(pool):
                        pool.memset(x[:, T - 1], 0.0).then_inc(zeroed, 1)

                    @block.sync
                    def _(sp):
                        sp.dma_start(x[:, 0:T - 1], x_d[0:(T - 1) * P, :].rearrange("(t p) c -> p t c", p=P)
                                     ).then_inc(x_in, 16)
                        sp.wait_ge(zeroed, 1)
                        sp.dma_start(x[0:LAST, T - 1], x_d[(T - 1) * P:N, :]).then_inc(x_in, 16)
                        sp.dma_start(tcol[:], over_partitions(t_d)).then_inc(t_in, 16)

                    @block.vector
                    def _(v):
                        done = [0]

                        def step(ins):
                            done[0] += 1
                            ins.then_inc(dve, 1)
                            v.wait_ge(dve, done[0])

                        v.wait_ge(x_in, 32)
                        v.wait_ge(t_in, 16)
                        for i in range(T):
                            step(v.tensor_scalar(msg[:], x[:, i], 0.0, EPS_MSG, ALU.max, ALU.add))
                            step(v.tensor_scalar(msg[:], msg[:], tcol[:], None, ALU.mult))
                            step(v.tensor_reduce(peak[:, i:i + 1], msg[:], AX.X, ALU.max))
                        step(v.tensor_reduce(peak[:, T:T + 1], peak[:, 0:T], AX.X, ALU.max))
                        v.wait_ge(pe_pre, 1)
                        step(v.tensor_reduce(peak_row[:, 0:1], bank(0, P)[0:1, :], AX.X, ALU.max))
                        v.wait_ge(pe_pre, 2)
                        step(v.tensor_scalar(peak[:, T + 1:T + 2], bank(1, 1), -1.0, None, ALU.mult))
                        for i in range(T):
                            step(v.tensor_scalar(msg[:], x[:, i], 0.0, EPS_MSG, ALU.max, ALU.add))
                            v.wait_ge(exps, i + 1)
                            step(v.tensor_tensor(both[:, D:WIDE], both[:, 0:D], msg[:], ALU.mult))
                            v.wait_ge(his, i + 1)
                            v.tensor_tensor(lo[:, i], both[:], hi[:, i].bitcast(F32), ALU.subtract).then_inc(los, 1)

                    @block.tensor
                    def _(pe):
                        pe.wait_ge(dve, 3 * T + 1)
                        pe.transpose(bank(0, P)[0:1, :], peak[:, T:T + 1], ident[:]).then_inc(pe_pre, 1)
                        pe.wait_ge(dve, 3 * T + 2)
                        pe.matmul(bank(1, 1), ones[0:1, :], peak_row[:, 0:1], start=True, stop=True).then_inc(pe_pre, 1)

                    @block.scalar
                    def _(act):
                        for i in range(T):
                            act.wait_ge(dve, 3 * T + 3 + 2 * i + 1)
                            if i:
                                act.wait_ge(los, i)
                            act.activation(both[:, 0:D], msg[:], ACT.Exp, bias=peak[:, T + 1:T + 2],
                                           scale=tcol[:]).then_inc(exps, 1)
                            act.wait_ge(dve, 3 * T + 3 + 2 * i + 2)
                            act.activation(hi[:, i], both[:], ACT.Copy).then_inc(his, 1)

                copied, turned, turned_free = sem("m_copied"), sem("m_turned"), sem("m_turned_free")
                count_in, summed, saved, added = sem("m_count_in"), sem("m_summed"), sem("m_saved"), sem("m_added")
                chain = sem("m_chain")
                with nc.Block() as block:
                    @block.gpsimd
                    def _(pool):
                        for buffer in (turned, count_in, saved, summed, added):
                            pool.sem_inc(buffer, 1)
                        with pool.Fori(0, T) as i:
                            pool.wait_ge(turned, i * 2 + 1)
                            pool.tensor_copy(countf[:, 0:NP], count[:, bass.ds(i, 1)].rearrange("p o s -> p (o s)")
                                             ).then_inc(copied, 1)

                    @block.tensor
                    def _(pe):
                        with pe.Fori(0, T) as i:
                            pe.wait_ge(copied, i + 1)
                            pe.wait_ge(count_in, i * 2 + 1)
                            for g in range(2):
                                for k in range(HB):
                                    mm = pe.transpose(ps[:, 2 * g * BANK + k * P:2 * g * BANK + (k + 1) * P],
                                                      countf[:, (g * HB + k) * P:(g * HB + k + 1) * P], ident[:])
                                mm.then_inc(turned, 1)
                            pe.wait_ge(count_in, i * 2 + 3)
                            pe.wait_ge(saved, i + 1)
                            for a, z in wide_chunks:
                                for k in range(T):
                                    for h, half in enumerate((hi, lo)):
                                        mm = pe.matmul(ps[:, OUT0 * BANK + a:OUT0 * BANK + z], count_t[:, k],
                                                       half[:, k, a:z], start=(k == 0 and h == 0),
                                                       stop=(k == T - 1 and h == 1))
                            mm.then_inc(summed, 1)

                    @block.scalar
                    def _(act):
                        with act.Fori(0, T) as i:
                            act.wait_ge(summed, i + 1)
                            for g in range(2):
                                act.wait_ge(turned, i * 2 + (g + 2))
                                act.activation(count_t[:, g * HB:(g + 1) * HB].rearrange("p k s -> p (k s)"),
                                               ps[:, 2 * g * BANK:2 * g * BANK + HALF], ACT.Copy).then_inc(count_in, 1)
                            act.wait_ge(summed, i + 2)
                            act.wait_ge(added, i + 1)
                            act.activation(sums[:], ps[:, OUT0 * BANK:OUT0 * BANK + WIDE], ACT.Copy).then_inc(saved, 1)

                    @block.vector
                    def _(v):
                        with v.Fori(0, T) as i:
                            v.wait_ge(saved, i + 2)
                            v.tensor_scalar(sums[:, 0:D], sums[:, 0:D], 1e-37, None, ALU.max).then_inc(chain, 1)
                            v.wait_ge(chain, i * 3 + 1)
                            v.reciprocal(sums[:, 0:D], sums[:, 0:D]).then_inc(chain, 1)
                            v.wait_ge(chain, i * 3 + 2)
                            v.tensor_tensor(sums[:, D:WIDE], sums[:, D:WIDE], sums[:, 0:D], ALU.mult).then_inc(chain, 1)
                            v.wait_ge(chain, i * 3 + 3)
                            xi = x[:, bass.ds(i, 1)].rearrange("p o c -> p (o c)")
                            v.tensor_tensor(xi, xi, sums[:, D:WIDE], ALU.add).then_inc(added, 1)


        def in_pairs(eng, body, first, last):
            n = first
            if n % 2:
                body(n, 1)
                n += 1
            pairs = (last - n) // 2
            if pairs > 0:
                with eng.Fori(0, pairs) as q:
                    body(q * 2 + n, 0)
                    body(q * 2 + (n + 1), 1)
                n += 2 * pairs
            if n < last:
                body(n, 0)

        def tile_of(t, i):
            return t[:, bass.ds(i, 1)].rearrange("p o c -> p (o c)")

        def linear(name, pieces, K, w_d, F, *, out_hi=None, out_lo=None, finish=None, rows=(), turned_w=False,
                   elu=False, relu=False, heads=0, att=None, scores=None, room=None,
                   w_room=None):
            blocks = [(a, min(a + P, K)) for a in range(0, K, P)]
            KT = len(blocks)
            GROUP = 8
            groups = [range(g, min(g + GROUP, KT)) for g in range(0, KT, GROUP)]
            NG = len(groups)
            assert NG <= 2
            chunks = [(a, min(a + BANK, F)) for a in range(0, F, BANK)]
            NC = len(chunks) + bool(heads)
            RING = 4 if NC % 2 == 0 else 2
            OUT0 = 4
            S = 2 * heads
            C = F // heads if heads else 0
            with ExitStack() as ctx:
                w_hi = sb(ctx, f"{name}_w_hi", [P, KT, F], F16)
                w_lo = sb(ctx, f"{name}_w_lo", [P, KT, F], F16)
                if heads:
                    a_hi = sb(ctx, f"{name}_a_hi", [P, KT, S], F16)
                    a_lo = sb(ctx, f"{name}_a_lo", [P, KT, S], F16)
                splitting = ExitStack()
                if turned_w:
                    if w_room is not None:
                        w_nat = w_room[:, 0:F // P * K].rearrange("p (f k) -> p f k", k=K)
                    else:
                        w_nat = sb(splitting, f"{name}_w_nat", [P, F // P, K], F32)
                else:
                    w_in = sb(splitting, f"{name}_w_in", [P, 2, F], F32)
                if heads:
                    a_w = sb(splitting, f"{name}_a_w", [P, KT, S], F32)
                    att_row = sb(splitting, f"{name}_att_row", [P, 2, F], F32)
                    junk = sb(splitting, f"{name}_junk", [P, 2, C], F32)

                w_loaded = [sem(f"{name}_w_loaded{r}") for r in range(2)]
                rows_in, w_turned = sem(f"{name}_rows_in"), sem(f"{name}_w_turned")
                w_high, w_split = sem(f"{name}_w_high"), sem(f"{name}_w_split")
                a_step = sem(f"{name}_a_step")

                def raw(k):
                    a, z = blocks[k]
                    if turned_w:
                        return ps[:, 2 * (k % 2) * BANK:2 * (k % 2) * BANK + F]
                    return w_in[0:z - a, k % 2]

                with nc.Block() as block:
                    @block.sync
                    def _(sp):
                        if turned_w:
                            sp.dma_start(w_nat[:], w_d.rearrange("(t p) k -> p t k", p=P)).then_inc(w_loaded[0], 16)
                        else:
                            for k, (a, z) in enumerate(blocks):
                                if k >= 2:
                                    sp.wait_ge(w_split, k - 1)
                                sp.dma_start(w_in[0:z - a, k % 2], w_d[a:z, :]).then_inc(w_loaded[k % 2], 16)

                    @block.gpsimd
                    def _(pool):
                        n = 0
                        if heads:
                            for j in range(2):
                                pool.dma_start(att_row[:, j], over_partitions(att[j].rearrange("h c -> (h c)"))
                                               ).then_inc(rows_in, 16)
                                n += 16
                        for to, ap in rows:
                            pool.dma_start(to, over_partitions(ap)).then_inc(rows_in, 16)
                            n += 16
                        if n:
                            pool.wait_ge(rows_in, n)

                    @block.tensor
                    def _(pe):
                        if turned_w:
                            pe.wait_ge(w_loaded[0], 16)
                            for k in range(KT):
                                if k >= 2:
                                    pe.wait_ge(w_split, k - 1)
                                for f in range(F // P):
                                    mm = pe.transpose(raw(k)[:, f * P:(f + 1) * P], w_nat[:, f, k * P:(k + 1) * P],
                                                      ident[:])
                                mm.then_inc(w_turned, 1)

                    def weights_in(eng, k):
                        if turned_w:
                            eng.wait_ge(w_turned, k + 1)
                        else:
                            eng.wait_ge(w_loaded[k % 2], 16 * (k // 2 + 1))

                    @block.scalar
                    def _(act):
                        for k, (a, z) in enumerate(blocks):
                            weights_in(act, k)
                            act.activation(w_hi[0:z - a, k], raw(k), ACT.Copy, scale=W_SCALE).then_inc(w_high, 1)

                    @block.vector
                    def _(v):
                        if heads:
                            v.wait_ge(rows_in, 32)
                        for k, (a, z) in enumerate(blocks):
                            weights_in(v, k)
                            if turned_w:
                                v.wait_ge(w_high, k + 1)
                            for j in range(S):
                                h, n = j % heads, k * S + j
                                if n >= 2:
                                    v.wait_ge(a_step, n - 1)
                                v.tensor_tensor_reduce(junk[:, n % 2], raw(k)[:, h * C:(h + 1) * C],
                                                       att_row[:, j // heads, h * C:(h + 1) * C], 1.0, 0.0,
                                                       ALU.mult, ALU.add, a_w[:, k, j:j + 1]).then_inc(a_step, 1)
                            v.wait_ge(w_high, k + 1)
                            v.scalar_tensor_tensor(out=w_lo[0:z - a, k], in0=raw(k), scalar=W_SCALE,
                                                   in1=w_hi[0:z - a, k], op0=ALU.mult,
                                                   op1=ALU.subtract).then_inc(w_split, 1)
                        if heads:
                            v.wait_ge(a_step, KT * S)
                            v.tensor_scalar(a_hi[:], a_w[:], W_SCALE, None, ALU.mult).then_inc(a_step, 1)
                            v.wait_ge(a_step, KT * S + 1)
                            v.scalar_tensor_tensor(out=a_lo[:].rearrange("p k s -> p (k s)"),
                                                   in0=a_w[:].rearrange("p k s -> p (k s)"), scalar=W_SCALE,
                                                   in1=a_hi[:].rearrange("p k s -> p (k s)"), op0=ALU.mult,
                                                   op1=ALU.subtract).then_inc(a_step, 1)

                splitting.close()
                stage = sb(ctx, f"{name}_stage", [P, 2, K], F32)
                if room:
                    xt_hi, xt_lo = (part[:, 0:2 * KT * P].rearrange("p (r k n) -> p r k n", r=2, n=P) for part in room)
                else:
                    xt_hi = sb(ctx, f"{name}_xt_hi", [P, 2, KT, P], F16)
                    xt_lo = sb(ctx, f"{name}_xt_lo", [P, 2, KT, P], F16)
                staged, turned, slot_free = sem(f"{name}_staged"), sem(f"{name}_turned"), sem(f"{name}_slot_free")
                xt_high, summed = sem(f"{name}_xt_high"), sem(f"{name}_summed")
                out_high, out_free = sem(f"{name}_out_high"), sem(f"{name}_out_free")
                below, expd, seen = sem(f"{name}_below"), sem(f"{name}_expd"), sem(f"{name}_seen")
                SLOTS = 2

                def slot(r, g):
                    return ((r * NG + g) % SLOTS) * 2 * BANK

                def out_bank(r, c, width):
                    return bank(OUT0 + (r * NC + c) % RING, width)

                def turned_parts(r, g, ks):
                    whole = [k for k in ks if blocks[k][1] - blocks[k][0] == P]
                    runs = [(P, whole[0], whole[-1] + 1)] if whole else []
                    runs += [(blocks[k][1] - blocks[k][0], k, k + 1) for k in ks if k not in whole]
                    for n, ka, kz in runs:
                        at = slot(r, g) + (ka - ks[0]) * P
                        yield n, ka, kz, ps[0:n, at:at + (kz - ka) * P]

                def stage_is_free(eng, i):
                    eng.wait_ge(slot_free, i * NG + (SLOTS - NG))

                NPC = len(pieces(0))
                with nc.Block() as block:
                    @block.gpsimd
                    def _(pool):
                        pool.sem_inc(slot_free, SLOTS)
                        pool.sem_inc(out_free, RING)

                        def body(i, r):
                            if elu:
                                pool.wait_ge(expd, (i + 1) * NPC)
                                pool.sem_inc(seen, 1)
                                pool.tensor_scalar(stage[:, r], stage[:, r], 1.0, -1.0, ALU.min,
                                                   ALU.add).then_inc(below, 1)
                                return
                            stage_is_free(pool, i)
                            for a, z, part in pieces(i):
                                pool.tensor_copy(stage[:, r, a:z], part).then_inc(staged, 1)

                        in_pairs(pool, body, 0, T)

                    @block.tensor
                    def _(pe):
                        def turn(i, r):
                            pe.wait_ge(staged, (i + 1) * NPC)
                            for g, ks in enumerate(groups):
                                pe.wait_ge(slot_free, i * NG + (g + 1))
                                for k in ks:
                                    a, z = blocks[k]
                                    at = slot(r, g) + (k - ks[0]) * P
                                    mm = pe.transpose(ps[0:z - a, at:at + P], stage[:, r, a:z], ident[:])
                                mm.then_inc(turned, 1)

                        def products(i, r):
                            pe.wait_ge(slot_free, i * NG + (NG + SLOTS))
                            for c in range(NC):
                                pe.wait_ge(out_free, i * NC + (c + 1))
                                if c < len(chunks):
                                    a, z = chunks[c]
                                    hi_w, lo_w = w_hi[:, :, a:z], w_lo[:, :, a:z]
                                else:
                                    a, z = 0, S
                                    hi_w, lo_w = a_hi[:], a_lo[:]
                                into = out_bank(r, c, z - a)
                                for k, (ka, kz) in enumerate(blocks):
                                    n = kz - ka
                                    pe.matmul(into, xt_hi[0:n, r, k], hi_w[0:n, k], start=(k == 0), stop=False)
                                    pe.matmul(into, xt_hi[0:n, r, k], lo_w[0:n, k], start=False, stop=False)
                                    mm = pe.matmul(into, xt_lo[0:n, r, k], hi_w[0:n, k], start=False,
                                                   stop=(k == KT - 1))
                                mm.then_inc(summed, 1)

                        turn(0, 0)

                        def body(i, r):
                            turn(i + 1, 1 - r)
                            products(i, r)

                        in_pairs(pe, body, 0, T - 1)
                        products(T - 1, 1)

                    @block.scalar
                    def _(act):
                        def exps(i, r):
                            if elu:
                                stage_is_free(act, i)
                                for a, z, part in pieces(i):
                                    act.activation(stage[:, r, a:z], part, ACT.Exp).then_inc(expd, 1)

                        def high(i, r):
                            if not isinstance(i, int) or i >= 2:
                                act.wait_ge(summed, (i - 1) * NC)
                            for g, ks in enumerate(groups):
                                act.wait_ge(turned, i * NG + (g + 1))
                                for n, ka, kz, of in turned_parts(r, g, ks):
                                    to = xt_hi[0:n, r, ka:kz].rearrange("p k n -> p (k n)")
                                    if relu:
                                        ins = act.activation(to, of, ACT.Relu)
                                    else:
                                        ins = act.activation(to, of, ACT.Copy)
                                ins.then_inc(xt_high, 1)

                        def outs(i, r):
                            if out_hi:
                                for c, (a, z) in enumerate(chunks):
                                    act.wait_ge(summed, i * NC + (c + 1))
                                    act.activation(out_hi(i, a, z), out_bank(r, c, z - a), ACT.Copy,
                                                   scale=1.0 / W_SCALE).then_inc(out_high, 1)

                        exps(0, 0)
                        exps(1, 1)
                        high(0, 0)

                        def body(i, r):
                            high(i + 1, 1 - r)
                            outs(i, r)
                            exps(i + 2, r)

                        in_pairs(act, body, 0, T - 2)
                        high(T - 1, 1)
                        outs(T - 2, 0)
                        outs(T - 1, 1)

                    @block.vector
                    def _(v):
                        def join(i, r):
                            if elu:
                                v.wait_ge(below, i + 1)
                                for a, z, part in pieces(i):
                                    v.scalar_tensor_tensor(out=stage[:, r, a:z], in0=part, scalar=0.0,
                                                           in1=stage[:, r, a:z], op0=ALU.max,
                                                           op1=ALU.add).then_inc(staged, 1)

                        def split(i, r):
                            for g, ks in enumerate(groups):
                                v.wait_ge(xt_high, i * NG + (g + 1))
                                for n, ka, kz, of in turned_parts(r, g, ks):
                                    to = xt_lo[0:n, r, ka:kz].rearrange("p k n -> p (k n)")
                                    high = xt_hi[0:n, r, ka:kz].rearrange("p k n -> p (k n)")
                                    if relu:
                                        ins = v.scalar_tensor_tensor(out=to, in0=of, scalar=0.0, in1=high,
                                                                     op0=ALU.max, op1=ALU.subtract)
                                    else:
                                        ins = v.tensor_tensor(to, of, high, ALU.subtract)
                                ins.then_inc(slot_free, 1)

                        def outs(i, r):
                            for c, (a, z) in enumerate(chunks):
                                v.wait_ge(summed, i * NC + (c + 1))
                                of = out_bank(r, c, z - a)
                                if out_hi:
                                    v.wait_ge(out_high, i * len(chunks) + (c + 1))
                                    v.scalar_tensor_tensor(out=out_lo(i, a, z), in0=of, scalar=1.0 / W_SCALE,
                                                           in1=out_hi(i, a, z), op0=ALU.mult,
                                                           op1=ALU.subtract).then_inc(out_free, 1)
                                else:
                                    finish(v, i, a, z, of, out_free, i * NC + (c + 1 + RING))
                            if heads:
                                c = len(chunks)
                                v.wait_ge(summed, i * NC + (c + 1))
                                v.tensor_scalar(scores(i), out_bank(r, c, S).rearrange("p (e h) -> p e h", e=2),
                                                1.0 / W_SCALE, None, ALU.mult).then_inc(out_free, 1)

                        join(0, 0)
                        split(0, 0)

                        def body(i, r):
                            join(i + 1, 1 - r)
                            split(i + 1, 1 - r)
                            outs(i, r)

                        in_pairs(v, body, 0, T - 1)
                        outs(T - 1, 1)

        def each_unit(eng, body, last):
            H, left = divmod(last, T)
            if left == 0:
                H, left = H - 1, T
            if H:
                with eng.Fori(0, H) as h:
                    for i in range(1, T):
                        body(h, i)
                    body(h + 1, 0)
            for i in range(1, left):
                body(H, i)

        def attention(name, H, C, h_hi, h_lo, scores, logc, bias_d, put, *, load=None, residual=None):
            U = H * T
            ROWS = 2 * H
            acc_chunks = [(a, min(a + BANK, C)) for a in range(0, C, BANK)]
            with ExitStack() as ctx:
                s_row = sb(ctx, f"{name}_s_row", [P, 2, NP], F32)
                s_row_fifth = sb(ctx, f"{name}_s_row_fifth", [P, 2, NP], F32)
                d_most = sb(ctx, f"{name}_d_most", [P, H, T], F32)
                logit = sb(ctx, f"{name}_logit", [P, 2, NP], F32)
                src_rows = logit[0:ROWS, 0]
                peak = sb(ctx, f"{name}_peak", [P, 2], F32)
                denom = sb(ctx, f"{name}_denom", [P, U], F32)
                inv = sb(ctx, f"{name}_inv", [P, 2], F32)
                pt_hi = sb(ctx, f"{name}_pt_hi", [P, 2, T, P], F16)
                pt_lo = sb(ctx, f"{name}_pt_lo", [P, 2, T, P], F16)
                bias = sb(ctx, f"{name}_bias", [P, H * C], F32)

                rows_turned, rows_saved = sem(f"{name}_rows_turned"), sem(f"{name}_rows_saved")
                rows_out, d_scaled = sem(f"{name}_rows_out"), sem(f"{name}_d_scaled")
                logc_in, bias_in = sem(f"{name}_logc_in"), sem(f"{name}_bias_in")
                with nc.Block() as block:
                    @block.sync
                    def _(sp):
                        loads = load(sp, logc_in) if load else 0
                        sp.wait_ge(rows_saved, 1)
                        sp.dma_start(src_rows_d[0:H, :], src_rows[0:H]).then_inc(rows_out, 16)
                        sp.wait_ge(rows_out, 16)
                        if load:
                            sp.wait_ge(logc_in, loads)

                    @block.gpsimd
                    def _(pool):
                        pool.dma_start(bias[:], over_partitions(bias_d)).then_inc(bias_in, 16)
                        pool.wait_ge(bias_in, 16)

                    @block.tensor
                    def _(pe):
                        for i in range(T):
                            mm = pe.transpose(ps[0:ROWS, i * P:(i + 1) * P],
                                              scores[:, i].rearrange("p e h -> p (e h)"), ident[:])
                        mm.then_inc(rows_turned, 1)

                    @block.scalar
                    def _(act):
                        act.wait_ge(rows_turned, 1)
                        act.activation(src_rows, ps[0:ROWS, 0:NP], ACT.Copy).then_inc(rows_saved, 1)

                    @block.vector
                    def _(v):
                        v.tensor_scalar(d_most[:].rearrange("p h t -> p t h"), scores[:, :, 1], 0.8, None,
                                        ALU.mult).then_inc(d_scaled, 1)

                row_in = [sem(f"{name}_row_in{r}") for r in range(2)]
                row_ready = sem(f"{name}_row_ready")
                logit_up, logit_done, expd = sem(f"{name}_logit_up"), sem(f"{name}_logit_done"), sem(f"{name}_expd")
                turned, high, split = sem(f"{name}_turned"), sem(f"{name}_high"), sem(f"{name}_split")
                summed, acc_free, seen = sem(f"{name}_summed"), sem(f"{name}_acc_free"), sem(f"{name}_seen")
                inverted, biased = sem(f"{name}_inverted"), sem(f"{name}_biased")
                SETS = 2

                def acc(r, a, z):
                    return ps[:, (4 + 2 * r) * BANK + a:(4 + 2 * r) * BANK + z]

                with nc.Block() as block:
                    @block.sync
                    def _(sp):
                        for h in range(H):
                            if h >= 2:
                                sp.wait_ge(logit_up, (h - 1) * T)
                            sp.dma_start(s_row[:, h % 2], over_partitions(src_rows_d[h])).then_inc(row_in[h % 2], 16)

                    @block.gpsimd
                    def _(pool):
                        pool.sem_inc(summed, SETS)
                        pool.sem_inc(acc_free, SETS)
                        for h in range(H):
                            pool.wait_ge(row_in[h % 2], 16 * (h // 2 + 1))
                            pool.tensor_scalar(s_row_fifth[:, h % 2], s_row[:, h % 2], 0.2, None,
                                               ALU.mult).then_inc(row_ready, 1)
                            if residual is not None:
                                for i in range(T):
                                    pool.tensor_tensor(residual[:, i], residual[:, i], bias[:],
                                                       ALU.add).then_inc(biased, 1)

                    def after(h, i):
                        return (h, i + 1) if i + 1 < T else (h + 1, 0)

                    def before(h, i):
                        return (h, i - 1) if i else (h - 1, T - 1)

                    @block.vector
                    def _(v):
                        def logits(h, i):
                            u, r = h * T + i, i % 2
                            v.wait_ge(row_ready, h + 1)
                            if not isinstance(u, int) or u >= 2:
                                v.wait_ge(turned, (u - 1) * 2)
                            row = h % 2
                            v.scalar_tensor_tensor(out=logit[:, r], in0=tile_of(s_row, row),
                                                   scalar=d_most[:].rearrange("p h t -> p (h t)")[:, bass.ds(u, 1)],
                                                   in1=tile_of(s_row_fifth, row), op0=ALU.add,
                                                   op1=ALU.max).then_inc(logit_up, 1)
                            v.wait_ge(logit_up, u + 1)
                            v.sem_inc(seen, 1)
                            v.tensor_tensor_reduce(logit[:, r], logit[:, r], logc[:, i], -1.0, -NO_EDGE / 10,
                                                   ALU.add, ALU.min, peak[:, r:r + 1]).then_inc(logit_done, 1)

                        def low(h, i):
                            u, r = h * T + i, i % 2
                            for g in range(2):
                                v.wait_ge(high, u * 2 + (g + 1))
                                v.tensor_tensor(pt_lo[:, r, g * HB:(g + 1) * HB].rearrange("p k n -> p (k n)"),
                                                ps[:, 2 * g * BANK:2 * g * BANK + HALF],
                                                pt_hi[:, r, g * HB:(g + 1) * HB].rearrange("p k n -> p (k n)"),
                                                ALU.subtract).then_inc(split, 1)

                        def finish(h, i):
                            u, r = h * T + i, i % 2
                            v.wait_ge(summed, u + (1 + SETS))
                            v.tensor_scalar(inv[:, r:r + 1], denom[:, bass.ds(u, 1)], 1e-37, None,
                                            ALU.max).then_inc(inverted, 1)
                            v.wait_ge(inverted, u * 2 + 1)
                            v.reciprocal(inv[:, r:r + 1], inv[:, r:r + 1]).then_inc(inverted, 1)
                            v.wait_ge(inverted, u * 2 + 2)
                            if residual is not None:
                                v.wait_ge(biased, i + 1)
                                other = residual[:, i]
                            else:
                                other = bias[:, bass.ds(h * C, C)]
                            v.scalar_tensor_tensor(out=put(h, i), in0=acc(r, 0, C), scalar=inv[:, r:r + 1],
                                                   in1=other, op0=ALU.mult, op1=ALU.add).then_inc(acc_free, 1)

                        logits(0, 0)
                        logits(0, 1)
                        low(0, 0)

                        def body(h, i):
                            logits(*after(h, i))
                            low(h, i)
                            finish(*before(h, i))

                        each_unit(v, body, U - 1)
                        low(H - 1, T - 1)
                        finish(H - 1, T - 2)
                        finish(H - 1, T - 1)

                    @block.scalar
                    def _(act):
                        def exps(h, i):
                            u, r = h * T + i, i % 2
                            act.wait_ge(logit_done, u + 1)
                            act.activation(logit[:, r], logit[:, r], ACT.Exp, bias=peak[:, r:r + 1], scale=-1.0,
                                           accum_out=denom[:, bass.ds(u, 1)]).then_inc(expd, 1)

                        def highs(h, i):
                            u, r = h * T + i, i % 2
                            act.wait_ge(summed, u + 1)
                            for g in range(2):
                                act.wait_ge(turned, u * 2 + (g + 1))
                                act.activation(pt_hi[:, r, g * HB:(g + 1) * HB].rearrange("p k n -> p (k n)"),
                                               ps[:, 2 * g * BANK:2 * g * BANK + HALF], ACT.Copy).then_inc(high, 1)

                        def body(h, i):
                            exps(*after(h, i))
                            highs(h, i)

                        exps(0, 0)
                        body(0, 0)
                        each_unit(act, body, U - 1)
                        highs(H - 1, T - 1)

                    @block.tensor
                    def _(pe):
                        def turn(h, i):
                            u, r = h * T + i, i % 2
                            pe.wait_ge(expd, u + 1)
                            for g in range(2):
                                if not isinstance(u, int) or u > 0:
                                    pe.wait_ge(split, u * 2 + g - 1)
                                for k in range(HB):
                                    at = 2 * g * BANK + k * P
                                    mm = pe.transpose(ps[:, at:at + P],
                                                      logit[:, r, (g * HB + k) * P:(g * HB + k + 1) * P], ident[:])
                                mm.then_inc(turned, 1)

                        def sums(h, i):
                            u, r = h * T + i, i % 2
                            pe.wait_ge(split, u * 2 + 2)
                            pe.wait_ge(acc_free, u + 1)
                            for a, z in acc_chunks:
                                for k in range(T):
                                    into = acc(r, a, z)
                                    pe.matmul(into, pt_hi[:, r, k], h_hi(k, h, a, z), start=(k == 0), stop=False)
                                    pe.matmul(into, pt_hi[:, r, k], h_lo(k, h, a, z), start=False, stop=False)
                                    mm = pe.matmul(into, pt_lo[:, r, k], h_hi(k, h, a, z), start=False,
                                                   stop=(k == T - 1))
                            mm.then_inc(summed, 1)

                        def body(h, i):
                            turn(*after(h, i))
                            sums(h, i)

                        turn(0, 0)
                        body(0, 0)
                        each_unit(pe, body, U - 1)
                        sums(H - 1, T - 1)

        def layer_norm(name, x, to=None, affine=None, store=None):
            to = x if to is None else to
            HALF_D = D // 2
            with ExitStack() as ctx:
                stats = sb(ctx, f"{name}_stats", [P, T, 2, 6], F32)
                mean_var = sb(ctx, f"{name}_mean_var", [P, T, 2], F32)
                std = sb(ctx, f"{name}_std", [P, T], F32)
                rows = sb(ctx, f"{name}_rows", [P, 2, D], F32) if affine else None
                dve, rooted, rows_in = sem(f"{name}_dve"), sem(f"{name}_rooted"), sem(f"{name}_rows_in")
                normed, stored = sem(f"{name}_normed"), sem(f"{name}_stored")
                with nc.Block() as block:
                    @block.vector
                    def _(v):
                        for i in range(T):
                            for h in range(2):
                                v.bn_stats(stats[:, i, h], x[:, i, h * HALF_D:(h + 1) * HALF_D]).then_inc(dve, 1)
                        for i in range(T):
                            v.wait_ge(dve, 2 * T + i if i else 2 * T)
                            v.bn_aggr(mean_var[:, i], stats[:, i].rearrange("p a b -> p (a b)")).then_inc(dve, 1)
                        v.wait_ge(dve, 3 * T)
                        v.tensor_scalar(std[:], mean_var[:, :, 1], LN_EPS, None, ALU.add).then_inc(dve, 1)
                        v.wait_ge(rooted, 1)
                        v.reciprocal(std[:], std[:]).then_inc(dve, 1)
                        v.wait_ge(dve, 3 * T + 2)
                        if affine:
                            v.wait_ge(rows_in, 32)
                        for i in range(T):
                            done = v.tensor_scalar(to[:, i], x[:, i], mean_var[:, i, 0:1], std[:, i:i + 1],
                                                   ALU.subtract, ALU.mult)
                            if affine:
                                done.then_inc(dve, 1)
                                v.wait_ge(dve, 3 * T + 2 + 2 * i + 1)
                                v.tensor_tensor(to[:, i], to[:, i], rows[:, 0], ALU.mult).then_inc(dve, 1)
                                v.wait_ge(dve, 3 * T + 2 + 2 * i + 2)
                                done = v.tensor_tensor(to[:, i], to[:, i], rows[:, 1], ALU.add)
                            done.then_inc(normed, 1)

                    @block.scalar
                    def _(act):
                        act.wait_ge(dve, 3 * T + 1)
                        act.activation(std[:], std[:], ACT.Sqrt).then_inc(rooted, 1)

                    @block.gpsimd
                    def _(pool):
                        if affine:
                            for k in range(2):
                                pool.dma_start(rows[:, k], over_partitions(affine[k])).then_inc(rows_in, 16)
                            pool.wait_ge(rows_in, 32)

                    @block.sync
                    def _(sp):
                        if store:
                            sp.wait_ge(normed, T)
                            sp.wait_ge(stored, store(sp, stored))

        early = ExitStack()
        x = sb(early, "x0", [P, T, D], F32)
        with ExitStack() as counting:
            count = sb(counting, "count", [P, T, NP], U16)
            count_edges(count)
            log_counts(count)
            channel_softmax(x, count, ins["L0_gnn_t"])

        F0 = ins["L0_gnn_W1"].shape[1]
        with ExitStack() as ctx:
            z = sb(ctx, "z", [P, T, F0], F32)
            with ExitStack() as ctx2:
                bn = sb(ctx2, "bn", [P, 5, F0], F32)
                bn_in, bn_step, bn_root = sem("bn_in"), sem("bn_step"), sem("bn_root")
                with nc.Block() as block:
                    @block.gpsimd
                    def _(pool):
                        for k, key in enumerate(("bn_var", "bn_gamma", "b1", "bn_mean", "bn_beta")):
                            pool.dma_start(bn[:, k], over_partitions(ins[f"L0_gnn_{key}"])).then_inc(bn_in, 16)

                    @block.scalar
                    def _(act):
                        act.wait_ge(bn_step, 1)
                        act.activation(bn[:, 0], bn[:, 0], ACT.Sqrt).then_inc(bn_root, 1)

                    @block.vector
                    def _(v):
                        done = [0]

                        def step(ins_):
                            done[0] += 1
                            ins_.then_inc(bn_step, 1)
                            v.wait_ge(bn_step, done[0])

                        v.wait_ge(bn_in, 5 * 16)
                        step(v.tensor_scalar(bn[:, 0], bn[:, 0], LN_EPS, None, ALU.add))
                        v.wait_ge(bn_root, 1)
                        step(v.reciprocal(bn[:, 0], bn[:, 0]))
                        step(v.tensor_tensor(bn[:, 0], bn[:, 0], bn[:, 1], ALU.mult))
                        step(v.tensor_tensor(bn[:, 2], bn[:, 2], bn[:, 3], ALU.subtract))
                        step(v.tensor_tensor(bn[:, 2], bn[:, 2], bn[:, 0], ALU.mult))
                        step(v.tensor_tensor(bn[:, 2], bn[:, 2], bn[:, 4], ALU.add))
                        step(v.tensor_scalar(bn[:, 0], bn[:, 0], 1.0 / W_SCALE, None, ALU.mult))

                def batch_norm(v, i, a, z_, of, of_free, first_done):
                    to = z[:, bass.ds(i, 1), a:z_].rearrange("p o c -> p (o c)")
                    v.tensor_tensor(to, of, bn[:, 0, a:z_], ALU.mult).then_inc(of_free, 1)
                    v.wait_ge(of_free, first_done)
                    v.tensor_tensor(to, to, bn[:, 2, a:z_], ALU.add)

                linear("l0a", lambda i: [(0, D, tile_of(x, i))], D, ins["L0_gnn_W1"], F0, finish=batch_norm)

            b2 = sb(ctx, "b2_0", [P, D], F32)
            summand = sb(ctx, "summand0", [P, 2, BANK], F32)
            again = sem("x_again")
            with nc.Block() as block:
                @block.sync
                def _(sp):
                    sp.dma_start(x[:, 0:T - 1], x_d[0:(T - 1) * P, :].rearrange("(t p) c -> p t c", p=P)
                                 ).then_inc(again, 16)
                    sp.dma_start(x[0:LAST, T - 1], x_d[(T - 1) * P:N, :]).then_inc(again, 16)
                    sp.wait_ge(again, 32)

            def add_twice(times):
                def finish(v, i, a, z_, of, of_free, first_done):
                    tmp = summand[:, (a // BANK) % 2, 0:z_ - a]
                    v.scalar_tensor_tensor(out=tmp, in0=of, scalar=1.0 / W_SCALE, in1=b2[:, a:z_], op0=ALU.mult,
                                           op1=ALU.add).then_inc(of_free, 1)
                    v.wait_ge(of_free, first_done)
                    to = x[:, bass.ds(i, 1), a:z_].rearrange("p o c -> p (o c)")
                    v.scalar_tensor_tensor(out=to, in0=to, scalar=times, in1=tmp, op0=ALU.mult, op1=ALU.add)
                return finish

            linear("l0b", lambda i: [(0, F0, tile_of(z, i))], F0, ins["L0_gnn_W2"], D, finish=add_twice(2.0),
                   rows=[(b2[:], ins["L0_gnn_b2"])], relu=True)

        def spill(sp, stored):
            sp.dma_start(x_spill, x[:]).then_inc(stored, 16)
            return 16

        layer_norm("n0", x, store=spill)

        recycle_semaphores()

        H1, C1 = ins["L1_gnn_a1_src"].shape
        wide = ExitStack()
        slots = wide.enter_context(nc.sbuf_tensor("slots", [P, H1 + 1, T, C1], F32, side="right"))
        halves = slots[:].bitcast(F16).rearrange("p h t c -> p h (t c)")
        halves = halves.rearrange("p h (e t c) -> p h e t c", e=2, t=T)
        scores1 = wide.enter_context(nc.sbuf_tensor("scores1", [P, T, 2, H1], F32, side="right"))
        HH = H1 // 2

        def slot_half(e, first):
            def where(i, a, z_):
                h = first + a // C1
                return halves[:, h + 1, e, bass.ds(i, 1), :].rearrange("p o c -> p (o c)")
            return where

        for part in range(2):
            first = part * HH
            linear(f"l1a{part}", lambda i: [(0, D, tile_of(x, i))], D,
                   ins["L1_gnn_W1"][:, first * C1:(first + HH) * C1], HH * C1, out_hi=slot_half(0, first),
                   out_lo=slot_half(1, first), heads=HH,
                   att=[ins["L1_gnn_a1_src"][first:first + HH, :], ins["L1_gnn_a1_dst"][first:first + HH, :]],
                   scores=lambda i, first=first: scores1[:, bass.ds(i, 1), :, first:first + HH]
                   .rearrange("p o e h -> p (o e) h"))
        early.close()

        def load_logs(logc):
            def load(sp, loaded):
                sp.dma_start(logc[:], logc_d).then_inc(loaded, 16)
                return 16
            return load

        def load_diagonal(sp, loaded):
            for i in range(T):
                sp.dma_start(logc[:, i, i * P:(i + 1) * P], logc_diag_d[:, i]).then_inc(loaded, 16)
            return 16 * T

        def head_half(e):
            return lambda k, h, a, z_: halves[:, bass.ds(h + 1, 1), e, k, a:z_].rearrange("p o c -> p (o c)")

        with ExitStack() as ctx:
            logc = sb(ctx, "logc1", [P, T, NP], F32)
            attention("t1a", H1, C1, head_half(0), head_half(1), scores1, logc, ins["L1_gnn_b1"],
                      lambda h, i: slots[:, bass.ds(h, 1), bass.ds(i, 1), :].rearrange("p a b c -> p (a b c)"),
                      load=load_logs(logc))

        mid = ExitStack()
        feat_hi = sb(mid, "feat1_hi", [P, T, D], F16)
        feat_lo = sb(mid, "feat1_lo", [P, T, D], F16)
        scores2 = sb(mid, "scores2", [P, T, 2, 1], F32)

        def tile_half(t):
            return lambda i, a, z_: t[:, bass.ds(i, 1), a:z_].rearrange("p o c -> p (o c)")

        def feature_half(t, C):
            return lambda k, h, a, z_: (t[:, k, a:z_] if isinstance(h, int) and h == 0 else
                                        t[:, k, bass.ds(h * C + a, z_ - a)])

        def tile_scores(s):
            return lambda i: s[:, bass.ds(i, 1)].rearrange("p o e h -> p (o e) h")

        linear("l1b", lambda i: [(h * C1, (h + 1) * C1, slots[:, h, bass.ds(i, 1), :].rearrange("p o c -> p (o c)"))
                                 for h in range(H1)],
               H1 * C1, ins["L1_gnn_W2"], D, out_hi=tile_half(feat_hi), out_lo=tile_half(feat_lo), elu=True, heads=1,
               att=[ins["L1_gnn_a2_src"], ins["L1_gnn_a2_dst"]], scores=tile_scores(scores2),
               room=[halves[:, H1, e].rearrange("p t c -> p (t c)") for e in range(2)])
        wide.close()

        x = root.enter_context(nc.sbuf_tensor("x1", [P, T, D], F32, side="right"))
        logc = root.enter_context(nc.sbuf_tensor("logc", [P, T, NP], F32, side="right"))
        back = sem("x_back")
        with nc.Block() as block:
            @block.sync
            def _(sp):
                sp.dma_start(x[:], x_spill).then_inc(back, 16)
                sp.wait_ge(back, 16)

        attention("t1b", 1, D, feature_half(feat_hi, D), feature_half(feat_lo, D), scores2, logc, ins["L1_gnn_b2"],
                  lambda h, i: tile_of(x, i), load=load_logs(logc), residual=x)
        mid.close()
        layer_norm("n1", x)

        recycle_semaphores()

        H2, C2 = ins["L2_gnn_a_src1"].shape
        H3, C3 = ins["L2_gnn_a_src2"].shape
        FB = H3 * C3
        with ExitStack() as ctx:
            out2 = sb(ctx, "out2", [P, T, FB], F32)
            with ExitStack() as ctx2:
                out1 = sb(ctx2, "out1", [P, T, H2 * C2], F32)
                with ExitStack() as ctx3:
                    layer_norm("n2", x, to=out1, affine=[ins["L2_gnn_norm_g"], ins["L2_gnn_norm_b"]])
                    f_hi = sb(ctx3, "feat2_hi", [P, T, H2 * C2], F16)
                    f_lo = sb(ctx3, "feat2_lo", [P, T, H2 * C2], F16)
                    sc = sb(ctx3, "scores3", [P, T, 2, H2], F32)
                    linear("l2a", lambda i: [(0, D, tile_of(out1, i))], D, ins["L2_gnn_W1"], H2 * C2,
                           out_hi=tile_half(f_hi), out_lo=tile_half(f_lo), heads=H2,
                           att=[ins["L2_gnn_a_src1"], ins["L2_gnn_a_dst1"]], scores=tile_scores(sc))
                    attention("t2a", H2, C2, feature_half(f_hi, C2), feature_half(f_lo, C2), sc, logc,
                              ins["L2_gnn_b1"],
                              lambda h, i: out1[:, bass.ds(i, 1), bass.ds(h * C2, C2)].rearrange("p o c -> p (o c)"))
                f_hi = sb(ctx2, "feat3_hi", [P, T, FB], F16)
                f_lo = sb(ctx2, "feat3_lo", [P, T, FB], F16)
                sc = sb(ctx2, "scores4", [P, T, 2, H3], F32)
                linear("l2b", lambda i: [(0, H2 * C2, tile_of(out1, i))], H2 * C2, ins["L2_gnn_W2"], FB,
                       out_hi=tile_half(f_hi), out_lo=tile_half(f_lo), heads=H3,
                       att=[ins["L2_gnn_a_src2"], ins["L2_gnn_a_dst2"]], scores=tile_scores(sc))
                attention("t2b", H3, C3, feature_half(f_hi, C3), feature_half(f_lo, C3), sc, logc,
                          ins["L2_gnn_b2"],
                          lambda h, i: out2[:, bass.ds(i, 1), bass.ds(h * C3, C3)].rearrange("p o c -> p (o c)"))
            b2 = sb(ctx, "b2_2", [P, D], F32)
            summand = sb(ctx, "summand2", [P, 2, BANK], F32)
            linear("l2c", lambda i: [(0, D, tile_of(x, i)), (D, D + FB, tile_of(out2, i))], D + FB,
                   ins["L2_gnn_Wu"], D, finish=add_twice(1.0), rows=[(b2[:], ins["L2_gnn_bu"])])
        layer_norm("n3", x)

        recycle_semaphores()

        H4, C4 = ins["L3_gnn_att_src1"].shape
        with ExitStack() as ctx:
            out3 = sb(ctx, "out3", [P, T, H4 * C4], F32)
            with ExitStack() as ctx2:
                f_hi = sb(ctx2, "feat4_hi", [P, T, H4 * C4], F16)
                f_lo = sb(ctx2, "feat4_lo", [P, T, H4 * C4], F16)
                sc = sb(ctx2, "scores5", [P, T, 2, H4], F32)
                linear("l3a", lambda i: [(0, D, tile_of(x, i))], D, ins["L3_gnn_W1"], H4 * C4,
                       out_hi=tile_half(f_hi), out_lo=tile_half(f_lo), turned_w=True, heads=H4,
                       att=[ins["L3_gnn_att_src1"], ins["L3_gnn_att_dst1"]], scores=tile_scores(sc),
                       w_room=out3[:].rearrange("p t c -> p (t c)"))
                attention("t3a", H4, C4, feature_half(f_hi, C4), feature_half(f_lo, C4), sc, logc,
                          ins["L3_gnn_b1"],
                          lambda h, i: out3[:, bass.ds(i, 1), bass.ds(h * C4, C4)].rearrange("p o c -> p (o c)"),
                          load=load_diagonal)
            feat = sb(ctx, "feat5", [P, 2, T, D], F16)
            f_hi, f_lo = feat[:, 0], feat[:, 1]
            sc = sb(ctx, "scores6", [P, T, 2, 1], F32)
            linear("l3b", lambda i: [(0, H4 * C4, tile_of(out3, i))], H4 * C4, ins["L3_gnn_W2"], D,
                   out_hi=tile_half(f_hi), out_lo=tile_half(f_lo), turned_w=True, relu=True, heads=1,
                   att=[ins["L3_gnn_att_src2"], ins["L3_gnn_att_dst2"]], scores=tile_scores(sc),
                   w_room=feat[:].rearrange("p e t c -> p (e t c)").bitcast(F32))
            attention("t3b", 1, D, feature_half(f_hi, D), feature_half(f_lo, D), sc, logc, ins["L3_gnn_b2"],
                      lambda h, i: tile_of(x, i), residual=x)

        def store_out(sp, stored):
            sp.dma_start(out[0:(T - 1) * P, :].rearrange("(t p) c -> p t c", p=P), x[:, 0:T - 1]).then_inc(stored, 16)
            sp.dma_start(out[(T - 1) * P:N, :], x[0:LAST, T - 1]).then_inc(stored, 16)
            return 32

        layer_norm("n4", x, store=store_out)


_INS = ["x", "src", "dst", "L0_gnn_t", "L0_gnn_W1", "L0_gnn_b1", "L0_gnn_bn_gamma", "L0_gnn_bn_beta",
        "L0_gnn_bn_mean", "L0_gnn_bn_var", "L0_gnn_W2", "L0_gnn_b2", "L1_gnn_W1", "L1_gnn_a1_src", "L1_gnn_a1_dst",
        "L1_gnn_b1", "L1_gnn_W2", "L1_gnn_a2_src", "L1_gnn_a2_dst", "L1_gnn_b2", "L2_gnn_norm_g", "L2_gnn_norm_b",
        "L2_gnn_W1", "L2_gnn_a_src1", "L2_gnn_a_dst1", "L2_gnn_b1", "L2_gnn_W2", "L2_gnn_a_src2", "L2_gnn_a_dst2",
        "L2_gnn_b2", "L2_gnn_Wu", "L2_gnn_bu", "L3_gnn_W1", "L3_gnn_att_src1", "L3_gnn_att_dst1", "L3_gnn_b1",
        "L3_gnn_W2", "L3_gnn_att_src2", "L3_gnn_att_dst2", "L3_gnn_b2"]


def kernel(**inputs):
    import numpy as _np
    import concourse.bacc as _bacc
    from concourse import mybir as _mybir
    from concourse.bass_utils import run_bass_kernel_spmd as _run

    nc = _bacc.Bacc("TRN2", target_bir_lowering=False, num_devices=1)
    arrays, args = {}, {}
    for name in _INS:
        a = _np.ascontiguousarray(inputs[name])
        if a.ndim == 0:
            a = a.reshape(1)
        arrays[f"in_{name}_dram"] = a
        args[name] = nc.dram_tensor(f"in_{name}_dram", a.shape, _mybir.dt.from_np(a.dtype), kind="ExternalInput").ap()
    out = nc.dram_tensor("out_dram", inputs["x"].shape, _mybir.dt.float32, kind="ExternalOutput").ap()
    bass_gnn_kernel(nc, args, out)
    r = _run(nc, [arrays], core_ids=[0])
    return r.results[0]["out_dram"]
```

```python
from contextlib import ExitStack

import concourse.bass as bass
from concourse import mybir

ALU = mybir.AluOpType
ACT = mybir.ActivationFunctionType
AX = mybir.AxisListType
F32 = mybir.dt.float32
F32R = mybir.dt.float32r
F16 = mybir.dt.float16
I32 = mybir.dt.int32
U16 = mybir.dt.uint16

P = 128
BANK = 512
NO_EDGE = -1.0e30
LN_EPS = 1e-5
EPS_MSG = 1e-7
W_SCALE = 64.0


def bass_gnn_kernel(nc: bass.Bass, ins, out: bass.AP):
    x_d, src_d, dst_d = ins["x"], ins["src"], ins["dst"]
    N, D = x_d.shape
    E = src_d.shape[0]
    T = -(-N // P)
    assert T % 2 == 0
    NP = T * P
    LAST = N - (T - 1) * P
    CHUNKS = [(a, min(a + BANK, NP)) for a in range(0, NP, BANK)]
    HALF = NP // 2
    HB = HALF // P

    root = ExitStack()
    with root:
        ps = root.enter_context(nc.psum_tensor("ps", [P, 8 * BANK], F32))

        def bank(b, width):
            return ps[:, b * BANK:b * BANK + width]

        def sb(ctx, name, shape, dt):
            return ctx.enter_context(nc.sbuf_tensor(name, shape, dt))

        in_use = []

        def sem(name):
            in_use.append(nc.alloc_semaphore(name))
            return in_use[-1]

        def recycle_semaphores():
            nc.clear_and_free_semaphores(in_use)
            in_use.clear()
            nc.all_engine_barrier()

        def tile_of(t, i):
            return t[:, bass.ds(i, 1)].rearrange("p o c -> p (o c)")

        def over_partitions(ap):
            return ap.rearrange("(o f) -> o f", o=1).to_broadcast([P, ap.shape[0]])

        ident = sb(root, "ident", [P, P], F32)
        ones = sb(root, "ones", [P, P], F32)
        stats = sb(root, "stats", [P, T, 2, 6], F32)

        x_spill = nc.dram_tensor("x_spill", (NP, D), F32, kind="Internal").ap().rearrange("(t p) c -> p t c", p=P)
        logc_d = nc.dram_tensor("logc_d", (NP, NP), F32, kind="Internal").ap().rearrange("(t p) s -> p t s", p=P)
        logc_diag_d = nc.dram_tensor("logc_diag_d", (P, T, P), F32, kind="Internal").ap()
        src_rows_d = nc.dram_tensor("src_rows_d", (16, NP), F32, kind="Internal").ap()


        def in_pairs(eng, body, first, last):
            n = first
            if n % 2:
                body(n, 1)
                n += 1
            pairs = (last - n) // 2
            if pairs > 0:
                with eng.Fori(0, pairs) as q:
                    body(q * 2 + n, 0)
                    body(q * 2 + (n + 1), 1)
                n += 2 * pairs
            if n < last:
                body(n, 0)

        WIDE = 2 * D

        def count_and_weigh(count, hi, lo, t_d):
            R, REM = divmod(E, P)
            G = -(-(R + 1) // P)
            BATCH = 4
            BATCHES = -(-(R + 1) // BATCH)
            ENDS = P * G // BATCH
            FULL = R - (G - 1) * P
            FAR = 1000.0
            assert REM and G == 2 and BATCHES < FAR
            with ExitStack() as ctx:
                edges = sb(ctx, "edges", [P, 2, G, P], I32)
                edges_f = sb(ctx, "edges_f", [P, 2, G, P], F32)
                edge_cols = sb(ctx, "edge_cols", [P, 2 * G * P], F32)
                iota = sb(ctx, "iota", [P, NP], F16)
                zeros = sb(ctx, "zeros", [P, P], F16)
                before = sb(ctx, "before", [T, T], F32)
                batch_no = sb(ctx, "batch_no", [T, BATCHES], F32)
                block_ends = sb(ctx, "block_ends", [T, 2], F32)
                tile_ends = sb(ctx, "tile_ends", [P, 2 * G], F32)
                diag = sb(ctx, "diag", [P, 2 * G * P], F32)
                batch_ends = sb(ctx, "batch_ends", [T, 2, ENDS], F32)
                holds = sb(ctx, "holds", [T, 3, BATCHES], F32)
                span = sb(ctx, "span", [T, 3], F32)
                table = sb(ctx, "table", [1, 3 * T], I32)
                hot_dst = sb(ctx, "hot_dst", [P, BATCH, P], F16)
                hot_src = sb(ctx, "hot_src", [P, BATCH, NP], F16)
                WITH_LOOPS = NP + P
                logs = sb(ctx, "logs", [P, WITH_LOOPS], F32)
                tiny = sb(ctx, "tiny", [P, 1], F32)
                mask = sb(ctx, "mask", [P, WITH_LOOPS], F32)
                looped = sb(ctx, "looped", [P, P], F32)
                xr = sb(ctx, "xr", [P, 2, D], F32)
                tcol = sb(ctx, "tcol", [P, 1], F32)
                ends = sb(ctx, "ends", [P, 2, T], F32)
                peak = sb(ctx, "peak", [P, 3], F32)
                peak_row = sb(ctx, "peak_row", [1, 1], F32)
                msg = sb(ctx, "msg", [P, D], F32)
                both = sb(ctx, "both", [P, WIDE], F32)
                consts, loaded = sem("g_consts"), sem("g_loaded")
                dve, pe_pre = sem("g_dve"), sem("g_pe_pre")
                hot_ready, hot_free = sem("g_hot_ready"), sem("g_hot_free")
                block_done = sem("g_block_done")
                counted, logged = sem("g_counted"), sem("g_logged")
                masked, loops_in, rows_stored = sem("g_masked"), sem("g_loops_in"), sem("g_rows_stored")
                x_in = [sem("g_x_in0"), sem("g_x_in1")]
                t_in, x_seen, peak_step, peak_pe = sem("g_t_in"), sem("g_x_seen"), sem("g_peak_step"), sem("g_peak_pe")
                msgs, exps, prods = sem("g_msgs"), sem("g_exps"), sem("g_prods")
                his, los = sem("g_his"), sem("g_los")
                N_CONST = 12
                TABLE = 15 + 2 * G
                PEAK = 5

                with nc.Block() as block:
                    @block.gpsimd
                    def _(pool):
                        pool.memset(edges[:, 0], NP - 1).then_inc(consts, 1)
                        pool.memset(edges[:, 1], -1).then_inc(consts, 1)
                        pool.memset(ident[:], 0.0).then_inc(consts, 1)
                        pool.memset(ones[:], 1.0).then_inc(consts, 1)
                        pool.memset(zeros[:], 0.0).then_inc(consts, 1)
                        pool.memset(tiny[:], 1e-30).then_inc(consts, 1)
                        pool.iota(iota[:], [[1, NP]], base=0, channel_multiplier=0,
                                  allow_small_or_imprecise_dtypes=True).then_inc(consts, 1)
                        pool.iota(batch_no[:], [[1, BATCHES]], base=0, channel_multiplier=0,
                                  allow_small_or_imprecise_dtypes=True).then_inc(consts, 1)
                        pool.iota(block_ends[:], [[P, 2]], base=0, channel_multiplier=P,
                                  allow_small_or_imprecise_dtypes=True).then_inc(consts, 1)
                        pool.sem_inc(hot_free, BATCH)
                        pool.wait_ge(consts, 4)
                        pool.affine_select(out=ident[:], in_=ident[:], compare_op=ALU.not_equal, fill=1.0, base=0,
                                           pattern=[[-1, P]], channel_multiplier=1).then_inc(consts, 1)
                        pool.affine_select(out=before[:], in_=ones[0:T, 0:T], compare_op=ALU.is_gt, fill=0.0, base=0,
                                           pattern=[[1, T]], channel_multiplier=-1).then_inc(consts, 2)
                        for i in range(T):
                            r = i % 2
                            pool.wait_ge(x_in[r], 16 * (T // 2 + i // 2 + 1))
                            pool.tensor_scalar(msg[:], xr[:, r], 0.0, EPS_MSG, ALU.max, ALU.add).then_inc(msgs, 1)
                            pool.wait_ge(exps, i + 1)
                            pool.wait_ge(msgs, i + 1)
                            pool.tensor_tensor(both[:, D:WIDE], both[:, 0:D], msg[:], ALU.mult).then_inc(prods, 1)
                            pool.wait_ge(his, i + 1)
                            pool.tensor_tensor(lo[:, i], both[:], hi[:, i].bitcast(F32), ALU.subtract).then_inc(los, 1)
                            pool.wait_ge(counted, i + 1)
                            pool.tensor_tensor(looped[:], looped[:], ident[:], ALU.add).then_inc(loops_in, 1)

                    @block.sync
                    def _(sp):
                        def load_x(n):
                            i, r = n % T, n % 2
                            rows = P if i < T - 1 else LAST
                            sp.dma_start(xr[0:rows, r], x_d[i * P:i * P + rows, :]).then_inc(x_in[r], 16)

                        sp.wait_ge(consts, 2)
                        for k, a in ((0, dst_d), (1, src_d)):
                            first = (G - 1) * P * P
                            sp.dma_start(edges[:, k, 0, :],
                                         a[0:first].rearrange("(t e) -> t e", e=P)).then_inc(loaded, 16)
                            sp.dma_start(edges[0:FULL, k, 1, :],
                                         a[first:R * P].rearrange("(t e) -> t e", e=P)).then_inc(loaded, 16)
                            sp.dma_start(edges[FULL:FULL + 1, k, 1, 0:REM],
                                         a[R * P:E].rearrange("(t e) -> t e", e=REM)).then_inc(loaded, 16)
                        sp.dma_start(tcol[:], over_partitions(t_d)).then_inc(t_in, 16)
                        for n in range(T):
                            if n >= 2:
                                sp.wait_ge(x_seen, 2 * (n - 1))
                            load_x(n)
                        for i in range(2):
                            sp.wait_ge(x_seen, 2 * (T - 1 + i))
                            load_x(T + i)
                        for i in range(T):
                            if i + 2 < T:
                                sp.wait_ge(msgs, i + 1)
                                load_x(T + i + 2)
                            sp.wait_ge(masked, i + 1)
                            sp.dma_start(logc_diag_d[:, i], logs[:, i * P:(i + 1) * P]).then_inc(rows_stored, 16)
                            sp.dma_start(logc_d[:, i], logs[:, 0:NP]).then_inc(rows_stored, 16)
                            sp.wait_ge(rows_stored, 48 * i + 32)
                            sp.dma_start(logc_d[:, i, i * P:(i + 1) * P], logs[:, NP:WITH_LOOPS]
                                         ).then_inc(rows_stored, 16)
                        sp.wait_ge(rows_stored, 48 * T)

                    @block.vector
                    def _(v):
                        done = [0, 0]

                        def step(ins, k=0):
                            done[k] += 1
                            ins.then_inc((dve, peak_step)[k], 1)
                            v.wait_ge((dve, peak_step)[k], done[k])

                        v.wait_ge(consts, N_CONST)
                        v.wait_ge(loaded, 6 * 16)
                        step(v.tensor_copy(edges_f[:], edges[:]))
                        step(v.tensor_reduce(tile_ends[:, 0:G], edges_f[:, 0], AX.X, ALU.min))
                        step(v.tensor_reduce(tile_ends[:, G:2 * G], edges_f[:, 0], AX.X, ALU.max))
                        for k in range(2 * G):
                            step(v.tensor_scalar(diag[:, k * P:(k + 1) * P], ident[:], tile_ends[:, k:k + 1], None,
                                                 ALU.mult))
                        v.wait_ge(pe_pre, 1)
                        step(v.tensor_copy(edge_cols[:], bank(0, 2 * G * P)))
                        v.wait_ge(pe_pre, 2)
                        for k, op in ((0, ALU.min), (1, ALU.max)):
                            step(v.tensor_reduce(
                                batch_ends[:, k],
                                bank(1, BANK)[0:T, k * G * P:(k + 1) * G * P].rearrange("b (j m) -> b j m", m=BATCH),
                                AX.X, op))
                        step(v.tensor_scalar(holds[:, 0], batch_ends[:, 0, 0:BATCHES], block_ends[:, 1:2], None,
                                             ALU.is_lt))
                        step(v.scalar_tensor_tensor(out=holds[:, 1], in0=batch_ends[:, 1, 0:BATCHES],
                                                    scalar=block_ends[:, 0:1], in1=holds[:, 0], op0=ALU.is_ge,
                                                    op1=ALU.mult))
                        step(v.scalar_tensor_tensor(out=holds[:, 0], in0=holds[:, 1], scalar=-FAR, in1=batch_no[:],
                                                    op0=ALU.mult, op1=ALU.add))
                        step(v.tensor_reduce(span[:, 0:1], holds[:, 0], AX.X, ALU.min))
                        step(v.scalar_tensor_tensor(out=holds[:, 2], in0=batch_no[:], scalar=1.0, in1=holds[:, 1],
                                                    op0=ALU.add, op1=ALU.mult))
                        step(v.tensor_reduce(span[:, 1:2], holds[:, 2], AX.X, ALU.max))
                        step(v.tensor_scalar(span[:, 0:1], span[:, 0:1], FAR, float(BATCHES - 1), ALU.add, ALU.min))
                        step(v.tensor_scalar(span[:, 2:3], span[:, 1:2], span[:, 0:1], 1.0, ALU.subtract, ALU.max))
                        v.wait_ge(pe_pre, 3)
                        step(v.tensor_copy(table[:], bank(2, 3 * T)[0:1, :]))
                        assert done[0] == TABLE

                        for i in range(T):
                            v.wait_ge(x_in[i % 2], 16 * (i // 2 + 1))
                            v.tensor_reduce(ends[:, 0, i:i + 1], xr[:, i % 2], AX.X, ALU.max).then_inc(x_seen, 1)
                            v.tensor_reduce(ends[:, 1, i:i + 1], xr[:, i % 2], AX.X, ALU.min).then_inc(x_seen, 1)
                        v.wait_ge(x_seen, 2 * T)
                        v.wait_ge(t_in, 16)
                        v.tensor_reduce(peak[:, 0:1], ends[:, 0], AX.X, ALU.max)
                        step(v.tensor_reduce(peak[:, 1:2], ends[:, 1], AX.X, ALU.min), 1)
                        step(v.tensor_scalar(peak[:, 0:2], peak[:, 0:2], 0.0, EPS_MSG, ALU.max, ALU.add), 1)
                        step(v.tensor_scalar(peak[:, 0:2], peak[:, 0:2], tcol[:], None, ALU.mult), 1)
                        v.wait_ge(peak_pe, 1)
                        step(v.tensor_reduce(peak_row[:], bank(3, 2 * P)[0:1, :], AX.X, ALU.max), 1)
                        v.wait_ge(peak_pe, 2)
                        step(v.tensor_scalar(peak[:, 2:3], bank(3, 1), -1.0, None, ALU.mult), 1)
                        assert done[1] == PEAK

                        def one_hots(b):
                            first = v.value_load(table[0:1, bass.ds(b, 1)], min_val=0, max_val=BATCHES - 1)
                            batches = v.value_load(table[0:1, bass.ds(b + T, 1)], min_val=1, max_val=BATCHES)
                            past = v.value_load(table[0:1, bass.ds(b + 2 * T, 1)], min_val=0, max_val=T * BATCHES)
                            with v.Fori(0, batches) as j:
                                t = ((first + j) * BATCH).with_bounds(min_val=0, max_val=BATCH * (BATCHES - 1))
                                for k in range(BATCH):
                                    v.wait_ge(hot_free, (past + j) * BATCH + (k + 1))
                                    v.tensor_scalar(hot_dst[:, k], iota[:, bass.ds(b * P, P)],
                                                    edge_cols[:, bass.ds(t + k, 1)], None, ALU.is_equal)
                                    v.tensor_scalar(hot_src[:, k], iota[:], edge_cols[:, bass.ds(t + (k + G * P), 1)],
                                                    None, ALU.is_equal).then_inc(hot_ready, 1)

                        def mask_logs(b):
                            v.wait_ge(logged, b * 2 + 6)
                            v.tensor_tensor(logs[:], logs[:], mask[:], ALU.min).then_inc(masked, 1)

                        one_hots(0)
                        with v.Fori(1, T) as b:
                            one_hots(b)
                            mask_logs(b - 1)
                        mask_logs(T - 1)

                    @block.tensor
                    def _(pe):
                        pe.wait_ge(consts, N_CONST)
                        pe.wait_ge(dve, 1)
                        flat = edges_f[:].rearrange("p a g e -> p (a g e)")
                        for k in range(2 * G):
                            mm = pe.transpose(bank(0, BANK)[:, k * P:(k + 1) * P], flat[:, k * P:(k + 1) * P], ident[:])
                        mm.then_inc(pe_pre, 1)
                        pe.wait_ge(dve, 3 + 2 * G)
                        pe.matmul(bank(1, BANK)[0:T, :], ones[:, 0:T], diag[:], start=True,
                                  stop=True).then_inc(pe_pre, 1)
                        pe.wait_ge(dve, 14 + 2 * G)
                        rows = bank(2, 3 * T)
                        pe.matmul(rows[0:1, 0:T], span[:, 0:1], ident[0:T, 0:T], start=True, stop=True)
                        pe.matmul(rows[0:1, T:2 * T], span[:, 2:3], ident[0:T, 0:T], start=True, stop=True)
                        pe.matmul(rows[0:1, 2 * T:3 * T], span[:, 2:3], before[:], start=True,
                                  stop=True).then_inc(pe_pre, 1)
                        pe.wait_ge(peak_step, 3)
                        for k in range(2):
                            mm = pe.transpose(bank(3, 2 * P)[0:1, k * P:(k + 1) * P], peak[:, k:k + 1], ident[:])
                        mm.then_inc(peak_pe, 1)
                        pe.wait_ge(peak_step, 4)
                        pe.matmul(bank(3, 1), ones[0:1, :], peak_row[:], start=True, stop=True).then_inc(peak_pe, 1)
                        pe.wait_ge(peak_step, PEAK)
                        pe.wait_ge(dve, TABLE)
                        with pe.Fori(0, T // 2) as b2:
                            for r in range(2):
                                b = b2 * 2 + r
                                base = 4 * r
                                batches = pe.value_load(table[0:1, bass.ds(b + T, 1)], min_val=1, max_val=BATCHES)
                                past = pe.value_load(table[0:1, bass.ds(b + 2 * T, 1)], min_val=0,
                                                     max_val=T * BATCHES)
                                pe.wait_ge(logged, b * 2 + 2)
                                for a, z in CHUNKS:
                                    pe.matmul(ps[:, base * BANK + a:base * BANK + z], zeros[:], iota[:, a:z],
                                              start=True, stop=False, skip_group_check=True)
                                with pe.Fori(0, batches) as j:
                                    for k in range(BATCH):
                                        pe.wait_ge(hot_ready, (past + j) * BATCH + (k + 1))
                                        for a, z in CHUNKS:
                                            mm = pe.matmul(ps[:, base * BANK + a:base * BANK + z], hot_dst[:, k],
                                                           hot_src[:, k, a:z], start=False, stop=False,
                                                           skip_group_check=True)
                                        mm.then_inc(hot_free, 1)
                                for a, z in CHUNKS:
                                    mm = pe.matmul(ps[:, base * BANK + a:base * BANK + z], zeros[:], iota[:, a:z],
                                                   start=False, stop=True, skip_group_check=True)
                                mm.then_inc(block_done, 1)

                    @block.scalar
                    def _(act):
                        def weigh(i):
                            if i == 0:
                                act.wait_ge(peak_step, PEAK)
                            act.wait_ge(msgs, i + 1)
                            if i:
                                act.wait_ge(los, i)
                            act.activation(both[:, 0:D], msg[:], ACT.Exp, bias=peak[:, 2:3],
                                           scale=tcol[:]).then_inc(exps, 1)
                            act.wait_ge(prods, i + 1)
                            act.activation(hi[:, i], both[:], ACT.Copy).then_inc(his, 1)

                        act.sem_inc(logged, 4)
                        weigh(0)
                        for b in range(T):
                            of = ps[:, 4 * (b % 2) * BANK:4 * (b % 2) * BANK + NP]
                            act.wait_ge(block_done, b + 1)
                            act.activation(count[:, b], of, ACT.Copy)
                            act.activation(looped[:], of[:, b * P:(b + 1) * P], ACT.Copy).then_inc(counted, 1)
                            act.wait_ge(loops_in, b + 1)
                            if b:
                                act.wait_ge(rows_stored, 48 * b)
                            act.activation(mask[:, NP:WITH_LOOPS], looped[:], ACT.Copy, scale=-2 * NO_EDGE,
                                           bias=NO_EDGE)
                            act.activation(mask[:, 0:NP], of, ACT.Copy, scale=-2 * NO_EDGE,
                                           bias=NO_EDGE).then_inc(logged, 1)
                            act.activation(logs[:, NP:WITH_LOOPS], looped[:], ACT.Ln, bias=tiny[:])
                            act.activation(logs[:, 0:NP], of, ACT.Ln, bias=tiny[:]).then_inc(logged, 1)
                            if b + 1 < T:
                                weigh(b + 1)

        def channel_softmax(x, count, hi, lo):
            wide_chunks = [(a, min(a + BANK, WIDE)) for a in range(0, WIDE, BANK)]
            NC = len(wide_chunks)
            OUT0 = 4
            with ExitStack() as ctx:
                countf = sb(ctx, "countf", [P, NP], F32)
                count_t = sb(ctx, "count_t", [P, 2, T, P], F32R)
                sums = sb(ctx, "sums", [P, WIDE], F32)
                x_in, zeroed = sem("m_x_in"), sem("m_zeroed")
                copied, turned, count_in = sem("m_copied"), sem("m_turned"), sem("m_count_in")
                summed, saved, added, chain = sem("m_summed"), sem("m_saved"), sem("m_added"), sem("m_chain")
                with nc.Block() as block:
                    @block.gpsimd
                    def _(pool):
                        pool.sem_inc(added, 1)
                        pool.sem_inc(saved, NC)
                        pool.sem_inc(turned, 2)
                        pool.memset(x[:, T - 1], 0.0).then_inc(zeroed, 1)
                        with pool.Fori(0, T) as i:
                            pool.wait_ge(turned, i * 2 + 2)
                            pool.tensor_copy(countf[:], tile_of(count, i)).then_inc(copied, 1)

                    @block.sync
                    def _(sp):
                        sp.dma_start(x[:, 0:T - 1], x_d[0:(T - 1) * P, :].rearrange("(t p) c -> p t c", p=P)
                                     ).then_inc(x_in, 16)
                        sp.wait_ge(zeroed, 1)
                        sp.dma_start(x[0:LAST, T - 1], x_d[(T - 1) * P:N, :]).then_inc(x_in, 16)

                    @block.tensor
                    def _(pe):
                        def turn(i, r):
                            pe.wait_ge(copied, i + 1)
                            if not isinstance(i, int) or i > 0:
                                pe.wait_ge(count_in, i * 2)
                            for g in range(2):
                                for k in range(HB):
                                    mm = pe.transpose(ps[:, 2 * g * BANK + k * P:2 * g * BANK + (k + 1) * P],
                                                      countf[:, (g * HB + k) * P:(g * HB + k + 1) * P], ident[:])
                                mm.then_inc(turned, 1)

                        def products(i, r):
                            pe.wait_ge(count_in, i * 2 + 2)
                            for c, (a, z) in enumerate(wide_chunks):
                                pe.wait_ge(saved, i * NC + (c + 1))
                                for k in range(T):
                                    for h, half in enumerate((hi, lo)):
                                        mm = pe.matmul(ps[:, OUT0 * BANK + a:OUT0 * BANK + z], count_t[:, r, k],
                                                       half[:, k, a:z], start=(k == 0 and h == 0),
                                                       stop=(k == T - 1 and h == 1))
                                mm.then_inc(summed, 1)

                        def body(i, r):
                            turn(i + 1, 1 - r)
                            products(i, r)

                        turn(0, 0)
                        body(0, 0)
                        in_pairs(pe, body, 1, T - 1)
                        products(T - 1, 1)

                    @block.scalar
                    def _(act):
                        def take(i, r):
                            if not isinstance(i, int) or i >= 2:
                                act.wait_ge(summed, (i - 1) * NC)
                            for g in range(2):
                                act.wait_ge(turned, i * 2 + (g + 3))
                                act.activation(count_t[:, r, g * HB:(g + 1) * HB].rearrange("p k s -> p (k s)"),
                                               ps[:, 2 * g * BANK:2 * g * BANK + HALF], ACT.Copy).then_inc(count_in, 1)

                        def save(i, r):
                            act.wait_ge(added, i + 1)
                            for c, (a, z) in enumerate(wide_chunks):
                                act.wait_ge(summed, i * NC + (c + 1))
                                act.activation(sums[:, a:z], ps[:, OUT0 * BANK + a:OUT0 * BANK + z],
                                               ACT.Copy).then_inc(saved, 1)

                        def body(i, r):
                            take(i + 1, 1 - r)
                            save(i, r)

                        take(0, 0)
                        body(0, 0)
                        in_pairs(act, body, 1, T - 1)
                        save(T - 1, 1)

                    @block.vector
                    def _(v):
                        v.wait_ge(x_in, 32)
                        with v.Fori(0, T) as i:
                            v.wait_ge(saved, i * NC + 2 * NC)
                            v.tensor_scalar(sums[:, 0:D], sums[:, 0:D], 1e-37, None, ALU.max).then_inc(chain, 1)
                            v.wait_ge(chain, i * 3 + 1)
                            v.reciprocal(sums[:, 0:D], sums[:, 0:D]).then_inc(chain, 1)
                            v.wait_ge(chain, i * 3 + 2)
                            v.tensor_tensor(sums[:, D:WIDE], sums[:, D:WIDE], sums[:, 0:D], ALU.mult).then_inc(chain, 1)
                            v.wait_ge(chain, i * 3 + 3)
                            v.tensor_tensor(tile_of(x, i), tile_of(x, i), sums[:, D:WIDE], ALU.add).then_inc(added, 1)

        def linear(name, pieces, K, w_d, F, *, out_hi=None, out_lo=None, out=None, finish=None, rows=(), turned_w=False,
                   elu=False, relu=False, heads=0, att=None, scores=None, room=None,
                   w_room=None, w_ring=4, beside=None, apart=False):
            blocks = [(a, min(a + P, K)) for a in range(0, K, P)]
            KT = len(blocks)
            GROUP = 8
            groups = [range(g, min(g + GROUP, KT)) for g in range(0, KT, GROUP)]
            NG = len(groups)
            assert NG <= 2
            chunks = [(a, min(a + BANK, F)) for a in range(0, F, BANK)]
            NC = len(chunks) + bool(heads)
            RING = 4 if NC % 2 == 0 else 2
            OUT0 = 4
            S = 2 * heads
            C = F // heads if heads else 0
            with ExitStack() as ctx:
                w_hi = sb(ctx, f"{name}_w_hi", [P, KT, F], F16)
                w_lo = sb(ctx, f"{name}_w_lo", [P, KT, F], F16)
                if heads:
                    a_hi = sb(ctx, f"{name}_a_hi", [P, KT, S], F16)
                    a_lo = sb(ctx, f"{name}_a_lo", [P, KT, S], F16)
                splitting = ExitStack()
                if not apart:
                    ctx.enter_context(splitting)
                if turned_w:
                    if w_room is not None:
                        w_nat = w_room[:, 0:F // P * K].rearrange("p (f k) -> p f k", k=K)
                    else:
                        w_nat = sb(splitting, f"{name}_w_nat", [P, F // P, K], F32)
                elif w_room is not None:
                    w_in = w_room[:, 0:w_ring * F].rearrange("p (r f) -> p r f", f=F)
                else:
                    w_in = sb(splitting, f"{name}_w_in", [P, w_ring, F], F32)
                if heads:
                    a_w = sb(splitting, f"{name}_a_w", [P, KT, S], F32)
                    att_row = sb(splitting, f"{name}_att_row", [P, 2, F], F32)
                    junk = sb(splitting, f"{name}_junk", [P, 2, C], F32)

                w_loaded = [sem(f"{name}_w_loaded{r}") for r in range(1 if turned_w else w_ring)]
                rows_in, w_turned = sem(f"{name}_rows_in"), sem(f"{name}_w_turned")
                w_high, w_split = sem(f"{name}_w_high"), sem(f"{name}_w_split")
                a_step = sem(f"{name}_a_step")

                def raw(k):
                    a, z = blocks[k]
                    if turned_w:
                        at = (OUT0 + 2 * (k % 2)) * BANK
                        return ps[:, at:at + F]
                    return w_in[0:z - a, k % w_ring]

                def load_weights(sp):
                    if turned_w:
                        sp.dma_start(w_nat[:], w_d.rearrange("(t p) k -> p t k", p=P)).then_inc(w_loaded[0], 16)
                    else:
                        for k, (a, z) in enumerate(blocks):
                            if k >= w_ring:
                                sp.wait_ge(w_split, k - w_ring + 1)
                            sp.dma_start(w_in[0:z - a, k % w_ring], w_d[a:z, :]
                                         ).then_inc(w_loaded[k % w_ring], 16)

                    if beside and "sync" in beside:
                        beside["sync"](sp)

                def load_rows(pool):
                    if beside and "gpsimd" in beside:
                        beside["gpsimd"](pool)
                    if heads:
                        for j in range(2):
                            pool.dma_start(att_row[:, j], over_partitions(att[j].rearrange("h c -> (h c)"))
                                           ).then_inc(rows_in, 16)
                    for to, ap in rows:
                        pool.dma_start(to, over_partitions(ap)).then_inc(rows_in, 16)

                def turn_weights(pe):
                    if turned_w:
                        pe.wait_ge(w_loaded[0], 16)
                        for k in range(KT):
                            if k >= 2:
                                pe.wait_ge(w_split, k - 1)
                            for f in range(F // P):
                                mm = pe.transpose(raw(k)[:, f * P:(f + 1) * P], w_nat[:, f, k * P:(k + 1) * P],
                                                  ident[:])
                            mm.then_inc(w_turned, 1)

                def weights_in(eng, k):
                    if turned_w:
                        eng.wait_ge(w_turned, k + 1)
                    else:
                        eng.wait_ge(w_loaded[k % w_ring], 16 * (k // w_ring + 1))

                def high_weights(act):
                    for k, (a, z) in enumerate(blocks):
                        weights_in(act, k)
                        act.activation(w_hi[0:z - a, k], raw(k), ACT.Copy, scale=W_SCALE).then_inc(w_high, 1)
                    if beside and "scalar" in beside:
                        beside["scalar"](act)

                def split_weights(v):
                    if heads or rows:
                        v.wait_ge(rows_in, 16 * (2 * bool(heads) + len(rows)))
                    for k, (a, z) in enumerate(blocks):
                        weights_in(v, k)
                        if turned_w:
                            v.wait_ge(w_high, k + 1)
                        for j in range(S):
                            h, n = j % heads, k * S + j
                            if n >= 2:
                                v.wait_ge(a_step, n - 1)
                            v.tensor_tensor_reduce(junk[:, n % 2], raw(k)[:, h * C:(h + 1) * C],
                                                   att_row[:, j // heads, h * C:(h + 1) * C], 1.0, 0.0,
                                                   ALU.mult, ALU.add, a_w[:, k, j:j + 1]).then_inc(a_step, 1)
                        v.wait_ge(w_high, k + 1)
                        v.scalar_tensor_tensor(out=w_lo[0:z - a, k], in0=raw(k), scalar=W_SCALE,
                                               in1=w_hi[0:z - a, k], op0=ALU.mult,
                                               op1=ALU.subtract).then_inc(w_split, 1)
                    if heads:
                        v.wait_ge(a_step, KT * S)
                        v.tensor_scalar(a_hi[:], a_w[:], W_SCALE, None, ALU.mult).then_inc(a_step, 1)
                        v.wait_ge(a_step, KT * S + 1)
                        v.scalar_tensor_tensor(out=a_lo[:].rearrange("p k s -> p (k s)"),
                                               in0=a_w[:].rearrange("p k s -> p (k s)"), scalar=W_SCALE,
                                               in1=a_hi[:].rearrange("p k s -> p (k s)"), op0=ALU.mult,
                                               op1=ALU.subtract).then_inc(a_step, 1)
                    if beside and "vector" in beside:
                        beside["vector"](v)

                if apart:
                    with nc.Block() as block:
                        @block.sync
                        def _(sp):
                            load_weights(sp)

                        @block.gpsimd
                        def _(pool):
                            load_rows(pool)

                        @block.scalar
                        def _(act):
                            high_weights(act)

                        @block.vector
                        def _(v):
                            split_weights(v)

                    splitting.close()
                stage = sb(ctx, f"{name}_stage", [P, 2, K], F32)
                if room:
                    xt_hi, xt_lo = (part[:, 0:2 * KT * P].rearrange("p (r k n) -> p r k n", r=2, n=P) for part in room)
                else:
                    xt_hi = sb(ctx, f"{name}_xt_hi", [P, 2, KT, P], F16)
                    xt_lo = sb(ctx, f"{name}_xt_lo", [P, 2, KT, P], F16)
                staged, turned, slot_free = sem(f"{name}_staged"), sem(f"{name}_turned"), sem(f"{name}_slot_free")
                xt_high, summed = sem(f"{name}_xt_high"), sem(f"{name}_summed")
                out_high, out_free = sem(f"{name}_out_high"), sem(f"{name}_out_free")
                below, expd, seen = sem(f"{name}_below"), sem(f"{name}_expd"), sem(f"{name}_seen")
                SLOTS = 2

                def slot(r, g):
                    return ((r * NG + g) % SLOTS) * 2 * BANK

                def out_bank(r, c, width):
                    return bank(OUT0 + (r * NC + c) % RING, width)

                def turned_parts(r, g, ks):
                    whole = [k for k in ks if blocks[k][1] - blocks[k][0] == P]
                    runs = [(P, whole[0], whole[-1] + 1)] if whole else []
                    runs += [(blocks[k][1] - blocks[k][0], k, k + 1) for k in ks if k not in whole]
                    for n, ka, kz in runs:
                        at = slot(r, g) + (ka - ks[0]) * P
                        yield n, ka, kz, ps[0:n, at:at + (kz - ka) * P]

                def stage_is_free(eng, i):
                    eng.wait_ge(slot_free, i * NG + (SLOTS - NG))

                NPC = len(pieces(0))
                with nc.Block() as block:
                    @block.sync
                    def _(sp):
                        if not apart:
                            load_weights(sp)

                    @block.gpsimd
                    def _(pool):
                        if not apart:
                            load_rows(pool)
                        pool.sem_inc(slot_free, SLOTS)
                        pool.sem_inc(out_free, RING)

                        def body(i, r):
                            if elu:
                                pool.wait_ge(expd, (i + 1) * NPC)
                                pool.sem_inc(seen, 1)
                                pool.tensor_scalar(stage[:, r], stage[:, r], 1.0, -1.0, ALU.min,
                                                   ALU.add).then_inc(below, 1)
                                return
                            stage_is_free(pool, i)
                            for a, z, part in pieces(i):
                                pool.tensor_copy(stage[:, r, a:z], part).then_inc(staged, 1)

                        in_pairs(pool, body, 0, T)

                    @block.tensor
                    def _(pe):
                        def turn(i, r):
                            pe.wait_ge(staged, (i + 1) * NPC)
                            for g, ks in enumerate(groups):
                                pe.wait_ge(slot_free, i * NG + (g + 1))
                                for k in ks:
                                    a, z = blocks[k]
                                    at = slot(r, g) + (k - ks[0]) * P
                                    mm = pe.transpose(ps[0:z - a, at:at + P], stage[:, r, a:z], ident[:])
                                mm.then_inc(turned, 1)

                        def products(i, r):
                            pe.wait_ge(slot_free, i * NG + (NG + SLOTS))
                            for c in range(NC):
                                pe.wait_ge(out_free, i * NC + (c + 1))
                                if c < len(chunks):
                                    a, z = chunks[c]
                                    hi_w, lo_w = w_hi[:, :, a:z], w_lo[:, :, a:z]
                                else:
                                    a, z = 0, S
                                    hi_w, lo_w = a_hi[:], a_lo[:]
                                into = out_bank(r, c, z - a)
                                at_first = isinstance(i, int) and i == 0
                                if at_first and c == len(chunks):
                                    pe.wait_ge(a_step, KT * S + 2)
                                for k, (ka, kz) in enumerate(blocks):
                                    n = kz - ka
                                    if at_first and c == 0:
                                        pe.wait_ge(w_split, KT if turned_w else k + 1)
                                    pe.matmul(into, xt_hi[0:n, r, k], hi_w[0:n, k], start=(k == 0), stop=False)
                                    pe.matmul(into, xt_hi[0:n, r, k], lo_w[0:n, k], start=False, stop=False)
                                    mm = pe.matmul(into, xt_lo[0:n, r, k], hi_w[0:n, k], start=False,
                                                   stop=(k == KT - 1))
                                mm.then_inc(summed, 1)

                        def body(i, r):
                            turn(i + 1, 1 - r)
                            products(i, r)

                        turn(0, 0)
                        turn_weights(pe)
                        body(0, 0)
                        in_pairs(pe, body, 1, T - 1)
                        products(T - 1, 1)

                    @block.scalar
                    def _(act):
                        def exps(i, r):
                            if elu:
                                stage_is_free(act, i)
                                for a, z, part in pieces(i):
                                    act.activation(stage[:, r, a:z], part, ACT.Exp).then_inc(expd, 1)

                        def high(i, r):
                            if not isinstance(i, int) or i >= 2:
                                act.wait_ge(summed, (i - 1) * NC)
                            for g, ks in enumerate(groups):
                                act.wait_ge(turned, i * NG + (g + 1))
                                for n, ka, kz, of in turned_parts(r, g, ks):
                                    to = xt_hi[0:n, r, ka:kz].rearrange("p k n -> p (k n)")
                                    if relu:
                                        ins = act.activation(to, of, ACT.Relu)
                                    else:
                                        ins = act.activation(to, of, ACT.Copy)
                                ins.then_inc(xt_high, 1)

                        def outs(i, r):
                            if out_hi:
                                for c, (a, z) in enumerate(chunks):
                                    act.wait_ge(summed, i * NC + (c + 1))
                                    act.activation(out_hi(i, a, z), out_bank(r, c, z - a), ACT.Copy,
                                                   scale=1.0 / W_SCALE).then_inc(out_high, 1)
                            if out:
                                for c, (a, z) in enumerate(chunks):
                                    act.wait_ge(summed, i * NC + (c + 1))
                                    act.activation(out(i, a, z), out_bank(r, c, z - a), ACT.Copy,
                                                   scale=1.0 / W_SCALE).then_inc(out_free, 1)
                                act.wait_ge(summed, i * NC + NC)
                                act.activation(scores(i), out_bank(r, NC - 1, S).rearrange("p (e h) -> p e h", e=2),
                                               ACT.Copy, scale=1.0 / W_SCALE).then_inc(out_free, 1)

                        exps(0, 0)
                        exps(1, 1)
                        high(0, 0)
                        if not apart:
                            high_weights(act)

                        def body(i, r):
                            exps(i + 2, r)
                            high(i + 1, 1 - r)
                            outs(i, r)

                        in_pairs(act, body, 0, T - 2)
                        high(T - 1, 1)
                        outs(T - 2, 0)
                        outs(T - 1, 1)

                    @block.vector
                    def _(v):
                        def join(i, r):
                            if elu:
                                v.wait_ge(below, i + 1)
                                for a, z, part in pieces(i):
                                    v.scalar_tensor_tensor(out=stage[:, r, a:z], in0=part, scalar=0.0,
                                                           in1=stage[:, r, a:z], op0=ALU.max,
                                                           op1=ALU.add).then_inc(staged, 1)

                        def split(i, r):
                            for g, ks in enumerate(groups):
                                v.wait_ge(xt_high, i * NG + (g + 1))
                                for n, ka, kz, of in turned_parts(r, g, ks):
                                    to = xt_lo[0:n, r, ka:kz].rearrange("p k n -> p (k n)")
                                    high = xt_hi[0:n, r, ka:kz].rearrange("p k n -> p (k n)")
                                    if relu:
                                        ins = v.scalar_tensor_tensor(out=to, in0=of, scalar=0.0, in1=high,
                                                                     op0=ALU.max, op1=ALU.subtract)
                                    else:
                                        ins = v.tensor_tensor(to, of, high, ALU.subtract)
                                ins.then_inc(slot_free, 1)

                        def outs(i, r):
                            if out:
                                return
                            for c, (a, z) in enumerate(chunks):
                                v.wait_ge(summed, i * NC + (c + 1))
                                of = out_bank(r, c, z - a)
                                if out_hi:
                                    v.wait_ge(out_high, i * len(chunks) + (c + 1))
                                    v.scalar_tensor_tensor(out=out_lo(i, a, z), in0=of, scalar=1.0 / W_SCALE,
                                                           in1=out_hi(i, a, z), op0=ALU.mult,
                                                           op1=ALU.subtract).then_inc(out_free, 1)
                                else:
                                    finish(v, i, a, z, of, out_free, i * NC + (c + 1 + RING))
                            if heads:
                                c = len(chunks)
                                v.wait_ge(summed, i * NC + (c + 1))
                                v.tensor_scalar(scores(i), out_bank(r, c, S).rearrange("p (e h) -> p e h", e=2),
                                                1.0 / W_SCALE, None, ALU.mult).then_inc(out_free, 1)

                        join(0, 0)
                        join(1, 1)
                        split(0, 0)
                        if not apart:
                            split_weights(v)

                        def body(i, r):
                            split(i + 1, 1 - r)
                            join(i + 2, r)
                            outs(i, r)

                        in_pairs(v, body, 0, T - 2)
                        split(T - 1, 1)
                        outs(T - 2, 0)
                        outs(T - 1, 1)

        def each_unit(eng, body, first, last):
            H, left = divmod(last, T)
            if left < first:
                H, left = H - 1, left + T
            if H:
                with eng.Fori(0, H) as h:
                    for i in range(first, T):
                        body(h, i)
                    for i in range(first):
                        body(h + 1, i)
            for i in range(first, left):
                body(H + i // T, i % T)

        def attention(name, H, C, h_hi, h_lo, scores, logc, bias_d, put, *, load=None, residual=None, stats=None):
            U = H * T
            ROWS = 2 * H
            acc_chunks = [(a, min(a + BANK, C)) for a in range(0, C, BANK)]
            with ExitStack() as ctx:
                s_row = sb(ctx, f"{name}_s_row", [P, 2, NP], F32)
                s_row_fifth = sb(ctx, f"{name}_s_row_fifth", [P, 2, NP], F32)
                d_most = sb(ctx, f"{name}_d_most", [P, H, T], F32)
                logit = sb(ctx, f"{name}_logit", [P, 2, NP], F32)
                src_rows = logit[0:ROWS, 0]
                peak = sb(ctx, f"{name}_peak", [P, 2], F32)
                denom = sb(ctx, f"{name}_denom", [P, U], F32)
                inv = sb(ctx, f"{name}_inv", [P, 2], F32)
                pt_hi = sb(ctx, f"{name}_pt_hi", [P, 2, T, P], F16 if h_lo else F32)
                pt_lo = sb(ctx, f"{name}_pt_lo", [P, 2, T, P], F16) if h_lo else None
                bias = sb(ctx, f"{name}_bias", [P, H * C], F32)

                rows_turned, rows_saved = sem(f"{name}_rows_turned"), sem(f"{name}_rows_saved")
                rows_out, d_scaled = sem(f"{name}_rows_out"), sem(f"{name}_d_scaled")
                logc_in, bias_in = sem(f"{name}_logc_in"), sem(f"{name}_bias_in")
                with nc.Block() as block:
                    @block.sync
                    def _(sp):
                        loads = load(sp, logc_in) if load else 0
                        sp.wait_ge(rows_saved, 1)
                        sp.dma_start(src_rows_d[0:H, :], src_rows[0:H]).then_inc(rows_out, 16)
                        sp.wait_ge(rows_out, 16)
                        if load:
                            sp.wait_ge(logc_in, loads)

                    @block.gpsimd
                    def _(pool):
                        pool.dma_start(bias[:], over_partitions(bias_d)).then_inc(bias_in, 16)
                        pool.wait_ge(bias_in, 16)

                    @block.tensor
                    def _(pe):
                        for i in range(T):
                            mm = pe.transpose(ps[0:ROWS, i * P:(i + 1) * P],
                                              scores[:, i].rearrange("p e h -> p (e h)"), ident[:])
                        mm.then_inc(rows_turned, 1)

                    @block.scalar
                    def _(act):
                        act.wait_ge(rows_turned, 1)
                        act.activation(src_rows, ps[0:ROWS, 0:NP], ACT.Copy).then_inc(rows_saved, 1)

                    @block.vector
                    def _(v):
                        v.tensor_scalar(d_most[:].rearrange("p h t -> p t h"), scores[:, :, 1], 0.8, None,
                                        ALU.mult).then_inc(d_scaled, 1)

                row_in = [sem(f"{name}_row_in{r}") for r in range(2)]
                row_ready = sem(f"{name}_row_ready")
                logit_up, logit_done, expd = sem(f"{name}_logit_up"), sem(f"{name}_logit_done"), sem(f"{name}_expd")
                turned, high, split = sem(f"{name}_turned"), sem(f"{name}_high"), sem(f"{name}_split")
                summed, acc_free, seen = sem(f"{name}_summed"), sem(f"{name}_acc_free"), sem(f"{name}_seen")
                inverted, biased = sem(f"{name}_inverted"), sem(f"{name}_biased")
                SETS = 2
                taken = split if h_lo else high

                def acc(r, a, z):
                    return ps[:, (4 + 2 * r) * BANK + a:(4 + 2 * r) * BANK + z]

                with nc.Block() as block:
                    @block.sync
                    def _(sp):
                        for h in range(H):
                            if h >= 2:
                                sp.wait_ge(logit_up, (h - 1) * T)
                            sp.dma_start(s_row[:, h % 2], over_partitions(src_rows_d[h])).then_inc(row_in[h % 2], 16)

                    @block.gpsimd
                    def _(pool):
                        pool.sem_inc(summed, SETS)
                        pool.sem_inc(acc_free, SETS)
                        for h in range(H):
                            pool.wait_ge(row_in[h % 2], 16 * (h // 2 + 1))
                            pool.tensor_scalar(s_row_fifth[:, h % 2], s_row[:, h % 2], 0.2, None,
                                               ALU.mult).then_inc(row_ready, 1)
                            if residual is not None:
                                for i in range(T):
                                    pool.tensor_tensor(residual[:, i], residual[:, i], bias[:],
                                                       ALU.add).then_inc(biased, 1)

                    def after(h, i):
                        return (h, i + 1) if i + 1 < T else (h + 1, 0)

                    def before(h, i, n):
                        return (h, i - n) if i >= n else (h - 1, i + T - n)

                    @block.vector
                    def _(v):
                        def logits(h, i):
                            u, r = h * T + i, i % 2
                            v.wait_ge(row_ready, h + 1)
                            if not isinstance(u, int) or u >= 2:
                                v.wait_ge(turned, (u - 1) * 2)
                            row = h % 2
                            v.scalar_tensor_tensor(out=logit[:, r], in0=tile_of(s_row, row),
                                                   scalar=d_most[:].rearrange("p h t -> p (h t)")[:, bass.ds(u, 1)],
                                                   in1=tile_of(s_row_fifth, row), op0=ALU.add,
                                                   op1=ALU.max).then_inc(logit_up, 1)
                            v.wait_ge(logit_up, u + 1)
                            v.sem_inc(seen, 1)
                            v.tensor_tensor_reduce(logit[:, r], logit[:, r], logc[:, i], -1.0, -NO_EDGE / 10,
                                                   ALU.add, ALU.min, peak[:, r:r + 1]).then_inc(logit_done, 1)

                        def low(h, i):
                            u, r = h * T + i, i % 2
                            for g in range(2 if h_lo else 0):
                                v.wait_ge(high, u * 2 + (g + 1))
                                v.tensor_tensor(pt_lo[:, r, g * HB:(g + 1) * HB].rearrange("p k n -> p (k n)"),
                                                ps[:, 2 * g * BANK:2 * g * BANK + HALF],
                                                pt_hi[:, r, g * HB:(g + 1) * HB].rearrange("p k n -> p (k n)"),
                                                ALU.subtract).then_inc(split, 1)

                        def finish(h, i):
                            u, r = h * T + i, i % 2
                            v.wait_ge(summed, u + (1 + SETS))
                            v.tensor_scalar(inv[:, r:r + 1], denom[:, bass.ds(u, 1)], 1e-37, None,
                                            ALU.max).then_inc(inverted, 1)
                            v.wait_ge(inverted, u * 2 + 1)
                            v.reciprocal(inv[:, r:r + 1], inv[:, r:r + 1]).then_inc(inverted, 1)
                            v.wait_ge(inverted, u * 2 + 2)
                            if residual is not None:
                                v.wait_ge(biased, i + 1)
                                other = residual[:, i]
                            else:
                                other = bias[:, bass.ds(h * C, C)]
                            v.scalar_tensor_tensor(out=put(h, i), in0=acc(r, 0, C), scalar=inv[:, r:r + 1],
                                                   in1=other, op0=ALU.mult, op1=ALU.add).then_inc(acc_free, 1)
                            if stats is not None:
                                v.wait_ge(acc_free, u + (1 + SETS))
                                row_stats(v, stats, i, put(h, i))

                        logits(0, 0)
                        logits(0, 1)
                        low(0, 0)

                        def body(h, i):
                            logits(*after(h, i))
                            finish(*before(h, i, 2))
                            low(h, i)

                        logits(0, 2)
                        low(0, 1)
                        each_unit(v, body, 2, U - 1)
                        finish(*before(H - 1, T - 1, 2))
                        low(H - 1, T - 1)
                        finish(H - 1, T - 2)
                        finish(H - 1, T - 1)

                    @block.scalar
                    def _(act):
                        def exps(h, i):
                            u, r = h * T + i, i % 2
                            act.wait_ge(logit_done, u + 1)
                            act.activation(logit[:, r], logit[:, r], ACT.Exp, bias=peak[:, r:r + 1], scale=-1.0,
                                           accum_out=denom[:, bass.ds(u, 1)]).then_inc(expd, 1)

                        def highs(h, i):
                            u, r = h * T + i, i % 2
                            act.wait_ge(summed, u + 1)
                            for g in range(2):
                                act.wait_ge(turned, u * 2 + (g + 1))
                                act.activation(pt_hi[:, r, g * HB:(g + 1) * HB].rearrange("p k n -> p (k n)"),
                                               ps[:, 2 * g * BANK:2 * g * BANK + HALF], ACT.Copy).then_inc(high, 1)

                        def body(h, i):
                            if h_lo:
                                highs(h, i)
                                exps(*after(h, i))
                            else:
                                exps(*after(h, i))
                                highs(h, i)

                        exps(0, 0)
                        body(0, 0)
                        each_unit(act, body, 1, U - 1)
                        highs(H - 1, T - 1)

                    @block.tensor
                    def _(pe):
                        def turn(h, i):
                            u, r = h * T + i, i % 2
                            pe.wait_ge(expd, u + 1)
                            for g in range(2):
                                if not isinstance(u, int) or u > 0:
                                    pe.wait_ge(taken, u * 2 + g - 1)
                                for k in range(HB):
                                    at = 2 * g * BANK + k * P
                                    mm = pe.transpose(ps[:, at:at + P],
                                                      logit[:, r, (g * HB + k) * P:(g * HB + k + 1) * P], ident[:])
                                mm.then_inc(turned, 1)

                        def sums(h, i):
                            u, r = h * T + i, i % 2
                            pe.wait_ge(acc_free, u + 1)
                            for a, z in acc_chunks:
                                for k in range(T):
                                    if a == 0 and k in (0, HB):
                                        pe.wait_ge(taken, u * 2 + (k // HB + 1))
                                    into = acc(r, a, z)
                                    if not h_lo:
                                        mm = pe.matmul(into, pt_hi[:, r, k], h_hi(k, h, a, z), start=(k == 0),
                                                       stop=(k == T - 1))
                                        continue
                                    pe.matmul(into, pt_hi[:, r, k], h_hi(k, h, a, z), start=(k == 0), stop=False)
                                    pe.matmul(into, pt_hi[:, r, k], h_lo(k, h, a, z), start=False, stop=False)
                                    mm = pe.matmul(into, pt_lo[:, r, k], h_hi(k, h, a, z), start=False,
                                                   stop=(k == T - 1))
                            mm.then_inc(summed, 1)

                        def body(h, i):
                            turn(*after(h, i))
                            sums(h, i)

                        turn(0, 0)
                        body(0, 0)
                        each_unit(pe, body, 1, U - 1)
                        sums(H - 1, T - 1)

        def row_stats(v, stats, i, row):
            for h in range(2):
                ins_ = v.bn_stats(stats[:, bass.ds(i, 1), h].rearrange("p o s -> p (o s)"),
                                  row[:, h * (D // 2):(h + 1) * (D // 2)])
            return ins_

        def layer_norm(name, x, to=None, affine=None, store=None, stats=None):
            to = x if to is None else to
            with ExitStack() as ctx:
                known = stats is not None
                if not known:
                    stats = sb(ctx, f"{name}_stats", [P, T, 2, 6], F32)
                mean_var = sb(ctx, f"{name}_mean_var", [P, T, 2], F32)
                std = sb(ctx, f"{name}_std", [P, T], F32)
                offset = sb(ctx, f"{name}_offset", [P, T], F32)
                rows = sb(ctx, f"{name}_rows", [P, 2, D], F32) if affine else None
                dve, rooted, rows_in = sem(f"{name}_dve"), sem(f"{name}_rooted"), sem(f"{name}_rows_in")
                known_stats = sem(f"{name}_known_stats")
                on_act = [i for i in range(T) if i % 2 and not affine]
                on_dve = [i for i in range(T) if i not in on_act]
                act_normed, dve_normed = sem(f"{name}_act_normed"), sem(f"{name}_dve_normed")
                with nc.Block() as block:
                    @block.vector
                    def _(v):
                        if not known:
                            for i in range(T):
                                row_stats(v, stats, i, x[:, i]).then_inc(known_stats, 1)
                            v.wait_ge(known_stats, T)
                        for i in range(T):
                            v.bn_aggr(mean_var[:, i], stats[:, i].rearrange("p a b -> p (a b)")).then_inc(dve, 1)
                        v.wait_ge(dve, T)
                        v.tensor_scalar(std[:], mean_var[:, :, 1], LN_EPS, None, ALU.add).then_inc(dve, 1)
                        v.wait_ge(rooted, 1)
                        v.reciprocal(std[:], std[:]).then_inc(dve, 1)
                        v.wait_ge(dve, T + 2)
                        v.scalar_tensor_tensor(out=offset[:], in0=mean_var[:, :, 0], scalar=-1.0, in1=std[:],
                                               op0=ALU.mult, op1=ALU.mult).then_inc(dve, 1)
                        if affine:
                            v.wait_ge(rows_in, 32)
                            for i in on_dve:
                                v.scalar_tensor_tensor(out=to[:, i], in0=x[:, i], scalar=mean_var[:, i, 0:1],
                                                       in1=rows[:, 0], op0=ALU.subtract,
                                                       op1=ALU.mult).then_inc(dve, 1)
                            for i in on_dve:
                                v.wait_ge(dve, T + 4 + i)
                                v.scalar_tensor_tensor(out=to[:, i], in0=to[:, i], scalar=std[:, i:i + 1],
                                                       in1=rows[:, 1], op0=ALU.mult,
                                                       op1=ALU.add).then_inc(dve_normed, 1)
                        else:
                            for i in on_dve:
                                v.tensor_scalar(to[:, i], x[:, i], mean_var[:, i, 0:1], std[:, i:i + 1],
                                                ALU.subtract, ALU.mult).then_inc(dve_normed, 1)

                    @block.scalar
                    def _(act):
                        act.wait_ge(dve, T + 1)
                        act.activation(std[:], std[:], ACT.Sqrt).then_inc(rooted, 1)
                        act.wait_ge(dve, T + 3)
                        for i in on_act:
                            act.activation(to[:, i], x[:, i], ACT.Identity, bias=offset[:, i:i + 1],
                                           scale=std[:, i:i + 1]).then_inc(act_normed, 1)

                    @block.gpsimd
                    def _(pool):
                        if affine:
                            for k in range(2):
                                pool.dma_start(rows[:, k], over_partitions(affine[k])).then_inc(rows_in, 16)
                            pool.wait_ge(rows_in, 32)

                    @block.sync
                    def _(sp):
                        if store:
                            for i in range(T):
                                if i in on_act:
                                    sp.wait_ge(act_normed, on_act.index(i) + 1)
                                else:
                                    sp.wait_ge(dve_normed, on_dve.index(i) + 1)
                                store(sp, i)

        early = ExitStack()
        with ExitStack() as counting:
            count = counting.enter_context(nc.sbuf_tensor("count", [P, T, NP], U16, side="right"))
            hi = counting.enter_context(nc.sbuf_tensor("sm_hi", [P, T, WIDE], F32R, side="right"))
            lo = counting.enter_context(nc.sbuf_tensor("sm_lo", [P, T, WIDE], F32R, side="right"))
            count_and_weigh(count, hi, lo, ins["L0_gnn_t"])
            x = sb(early, "x0", [P, T, D], F32)
            channel_softmax(x, count, hi, lo)

        F0 = ins["L0_gnn_W1"].shape[1]
        with ExitStack() as ctx:
            z = sb(ctx, "z", [P, T, F0], F32)
            with ExitStack() as ctx2:
                bn = sb(ctx2, "bn", [P, 5, F0], F32)
                bn_in, bn_step, bn_root = sem("bn_in"), sem("bn_step"), sem("bn_root")

                def bn_load(pool):
                    for k, key in enumerate(("bn_var", "bn_gamma", "b1", "bn_mean", "bn_beta")):
                        pool.dma_start(bn[:, k], over_partitions(ins[f"L0_gnn_{key}"])).then_inc(bn_in, 16)

                def bn_sqrt(act):
                    act.wait_ge(bn_step, 1)
                    act.activation(bn[:, 0], bn[:, 0], ACT.Sqrt).then_inc(bn_root, 1)

                def bn_rows(v):
                    done = [0]

                    def step(ins_):
                        done[0] += 1
                        ins_.then_inc(bn_step, 1)
                        v.wait_ge(bn_step, done[0])

                    v.wait_ge(bn_in, 5 * 16)
                    step(v.tensor_scalar(bn[:, 0], bn[:, 0], LN_EPS, None, ALU.add))
                    v.wait_ge(bn_root, 1)
                    step(v.reciprocal(bn[:, 0], bn[:, 0]))
                    step(v.tensor_tensor(bn[:, 0], bn[:, 0], bn[:, 1], ALU.mult))
                    step(v.tensor_tensor(bn[:, 2], bn[:, 2], bn[:, 3], ALU.subtract))
                    step(v.tensor_tensor(bn[:, 2], bn[:, 2], bn[:, 0], ALU.mult))
                    step(v.tensor_tensor(bn[:, 2], bn[:, 2], bn[:, 4], ALU.add))
                    step(v.tensor_scalar(bn[:, 0], bn[:, 0], 1.0 / W_SCALE, None, ALU.mult))

                def batch_norm(v, i, a, z_, of, of_free, first_done):
                    to = z[:, bass.ds(i, 1), a:z_].rearrange("p o c -> p (o c)")
                    v.tensor_tensor(to, of, bn[:, 0, a:z_], ALU.mult).then_inc(of_free, 1)
                    v.wait_ge(of_free, first_done)
                    v.tensor_tensor(to, to, bn[:, 2, a:z_], ALU.add)

                linear("l0a", lambda i: [(0, D, tile_of(x, i))], D, ins["L0_gnn_W1"], F0, finish=batch_norm,
                       beside={"gpsimd": bn_load, "scalar": bn_sqrt, "vector": bn_rows}, w_ring=2)

            b2 = sb(ctx, "b2_0", [P, D], F32)
            summand = sb(ctx, "summand0", [P, 2, BANK], F32)
            again = sem("x_again")

            def x_again(sp):
                sp.dma_start(x[:, 0:T - 1], x_d[0:(T - 1) * P, :].rearrange("(t p) c -> p t c", p=P)
                             ).then_inc(again, 16)
                sp.dma_start(x[0:LAST, T - 1], x_d[(T - 1) * P:N, :]).then_inc(again, 16)

            def add_twice(times, row_done):
                def finish(v, i, a, z_, of, of_free, first_done):
                    tmp = summand[:, (a // BANK) % 2, 0:z_ - a]
                    v.scalar_tensor_tensor(out=tmp, in0=of, scalar=1.0 / W_SCALE, in1=b2[:, a:z_], op0=ALU.mult,
                                           op1=ALU.add).then_inc(of_free, 1)
                    v.wait_ge(of_free, first_done)
                    to = x[:, bass.ds(i, 1), a:z_].rearrange("p o c -> p (o c)")
                    ins_ = v.scalar_tensor_tensor(out=to, in0=to, scalar=times, in1=tmp, op0=ALU.mult, op1=ALU.add)
                    ins_.then_inc(row_done, 1)
                    if z_ == D:
                        v.wait_ge(row_done, (i + 1) * -(-D // BANK))
                        row_stats(v, stats, i, tile_of(x, i))
                return finish

            linear("l0b", lambda i: [(0, F0, tile_of(z, i))], F0, ins["L0_gnn_W2"], D, finish=add_twice(2.0, sem("row_done0")),
                   rows=[(b2[:], ins["L0_gnn_b2"])], relu=True, beside={"sync": x_again, "vector": lambda v: v.wait_ge(again, 32)})

        x_away = nc.alloc_semaphore("x_away")

        def spill(sp, i):
            sp.dma_start(x_spill[:, i], x[:, i]).then_inc(x_away, 16)

        layer_norm("n0", x, store=spill, stats=stats)

        recycle_semaphores()

        H1, C1 = ins["L1_gnn_a1_src"].shape
        wide = ExitStack()
        slots = wide.enter_context(nc.sbuf_tensor("slots", [P, H1 + 1, T, C1], F32, side="right"))
        halves = slots[:].bitcast(F16).rearrange("p h t c -> p h (t c)")
        halves = halves.rearrange("p h (e t c) -> p h e t c", e=2, t=T)
        scores1 = wide.enter_context(nc.sbuf_tensor("scores1", [P, T, 2, H1], F32, side="right"))
        HH = H1 // 2

        def slot_half(e, first):
            def where(i, a, z_):
                h = first + a // C1
                return halves[:, h + 1, e, bass.ds(i, 1), :].rearrange("p o c -> p (o c)")
            return where

        for part in range(2):
            first = part * HH
            linear(f"l1a{part}", lambda i: [(0, D, tile_of(x, i))], D,
                   ins["L1_gnn_W1"][:, first * C1:(first + HH) * C1], HH * C1, out_hi=slot_half(0, first),
                   out_lo=slot_half(1, first), heads=HH,
                   att=[ins["L1_gnn_a1_src"][first:first + HH, :], ins["L1_gnn_a1_dst"][first:first + HH, :]],
                   scores=lambda i, first=first: scores1[:, bass.ds(i, 1), :, first:first + HH]
                   .rearrange("p o e h -> p (o e) h"))
        early.close()

        def load_logs(logc):
            def load(sp, loaded):
                sp.dma_start(logc[:], logc_d).then_inc(loaded, 16)
                return 16
            return load

        def load_diagonal(sp, loaded):
            for i in range(T):
                sp.dma_start(logc[:, i, i * P:(i + 1) * P], logc_diag_d[:, i]).then_inc(loaded, 16)
            return 16 * T

        def head_half(e):
            return lambda k, h, a, z_: halves[:, bass.ds(h + 1, 1), e, k, a:z_].rearrange("p o c -> p (o c)")

        with ExitStack() as ctx:
            logc = sb(ctx, "logc1", [P, T, NP], F32)
            attention("t1a", H1, C1, head_half(0), head_half(1), scores1, logc, ins["L1_gnn_b1"],
                      lambda h, i: slots[:, bass.ds(h, 1), bass.ds(i, 1), :].rearrange("p a b c -> p (a b c)"),
                      load=load_logs(logc))

        mid = ExitStack()
        feat_hi = sb(mid, "feat1_hi", [P, T, D], F16)
        feat_lo = sb(mid, "feat1_lo", [P, T, D], F16)
        scores2 = sb(mid, "scores2", [P, T, 2, 1], F32)

        def tile_half(t):
            return lambda i, a, z_: t[:, bass.ds(i, 1), a:z_].rearrange("p o c -> p (o c)")

        def feature_half(t, C):
            return lambda k, h, a, z_: (t[:, k, a:z_] if isinstance(h, int) and h == 0 else
                                        t[:, k, bass.ds(h * C + a, z_ - a)])

        def tile_scores(s):
            return lambda i: s[:, bass.ds(i, 1)].rearrange("p o e h -> p (o e) h")

        linear("l1b", lambda i: [(h * C1, (h + 1) * C1, slots[:, h, bass.ds(i, 1), :].rearrange("p o c -> p (o c)"))
                                 for h in range(H1)],
               H1 * C1, ins["L1_gnn_W2"], D, out_hi=tile_half(feat_hi), out_lo=tile_half(feat_lo), elu=True, heads=1,
               att=[ins["L1_gnn_a2_src"], ins["L1_gnn_a2_dst"]], scores=tile_scores(scores2),
               w_room=slots[:, H1].rearrange("p t c -> p (t c)"), w_ring=6, apart=True,
               room=[halves[:, H1, e].rearrange("p t c -> p (t c)") for e in range(2)])
        wide.close()

        x = root.enter_context(nc.sbuf_tensor("x1", [P, T, D], F32, side="right"))
        logc = root.enter_context(nc.sbuf_tensor("logc", [P, T, NP], F32, side="right"))

        def load_logs_and_x(sp, loaded):
            sp.wait_ge(x_away, 16 * T)
            sp.dma_start(x[:], x_spill).then_inc(loaded, 16)
            return 16 + load_logs(logc)(sp, loaded)

        attention("t1b", 1, D, feature_half(feat_hi, D), feature_half(feat_lo, D), scores2, logc, ins["L1_gnn_b2"],
                  lambda h, i: tile_of(x, i), load=load_logs_and_x, residual=x, stats=stats)
        mid.close()
        layer_norm("n1", x, stats=stats)

        recycle_semaphores()

        H2, C2 = ins["L2_gnn_a_src1"].shape
        H3, C3 = ins["L2_gnn_a_src2"].shape
        FB = H3 * C3
        with ExitStack() as ctx:
            out2 = sb(ctx, "out2", [P, T, FB], F32)
            with ExitStack() as ctx2:
                out1 = sb(ctx2, "out1", [P, T, H2 * C2], F32)
                with ExitStack() as ctx3:
                    layer_norm("n2", x, to=out1, affine=[ins["L2_gnn_norm_g"], ins["L2_gnn_norm_b"]])
                    feat = sb(ctx3, "feat2", [P, T, H2 * C2], F32)
                    sc = sb(ctx3, "scores3", [P, T, 2, H2], F32)
                    linear("l2a", lambda i: [(0, D, tile_of(out1, i))], D, ins["L2_gnn_W1"], H2 * C2,
                           out=tile_half(feat), heads=H2,
                           att=[ins["L2_gnn_a_src1"], ins["L2_gnn_a_dst1"]], scores=tile_scores(sc))
                    attention("t2a", H2, C2, feature_half(feat, C2), None, sc, logc,
                              ins["L2_gnn_b1"],
                              lambda h, i: out1[:, bass.ds(i, 1), bass.ds(h * C2, C2)].rearrange("p o c -> p (o c)"))
                feat = sb(ctx2, "feat3", [P, T, FB], F32)
                sc = sb(ctx2, "scores4", [P, T, 2, H3], F32)
                linear("l2b", lambda i: [(0, H2 * C2, tile_of(out1, i))], H2 * C2, ins["L2_gnn_W2"], FB,
                       out=tile_half(feat), heads=H3,
                       att=[ins["L2_gnn_a_src2"], ins["L2_gnn_a_dst2"]], scores=tile_scores(sc))
                attention("t2b", H3, C3, feature_half(feat, C3), None, sc, logc,
                          ins["L2_gnn_b2"],
                          lambda h, i: out2[:, bass.ds(i, 1), bass.ds(h * C3, C3)].rearrange("p o c -> p (o c)"))
            b2 = sb(ctx, "b2_2", [P, D], F32)
            summand = sb(ctx, "summand2", [P, 2, BANK], F32)
            linear("l2c", lambda i: [(0, D, tile_of(x, i)), (D, D + FB, tile_of(out2, i))], D + FB,
                   ins["L2_gnn_Wu"], D, finish=add_twice(1.0, sem("row_done2")), rows=[(b2[:], ins["L2_gnn_bu"])])
        layer_norm("n3", x, stats=stats)

        recycle_semaphores()

        H4, C4 = ins["L3_gnn_att_src1"].shape
        with ExitStack() as ctx:
            out3 = sb(ctx, "out3", [P, T, H4 * C4], F32)
            with ExitStack() as ctx2:
                feat = sb(ctx2, "feat4", [P, T, H4 * C4], F32)
                sc = sb(ctx2, "scores5", [P, T, 2, H4], F32)
                linear("l3a", lambda i: [(0, D, tile_of(x, i))], D, ins["L3_gnn_W1"], H4 * C4,
                       out=tile_half(feat), turned_w=True, heads=H4,
                       att=[ins["L3_gnn_att_src1"], ins["L3_gnn_att_dst1"]], scores=tile_scores(sc),
                       w_room=out3[:].rearrange("p t c -> p (t c)"))
                attention("t3a", H4, C4, feature_half(feat, C4), None, sc, logc,
                          ins["L3_gnn_b1"],
                          lambda h, i: out3[:, bass.ds(i, 1), bass.ds(h * C4, C4)].rearrange("p o c -> p (o c)"),
                          load=load_diagonal)
            feat = sb(ctx, "feat5", [P, 2, T, D], F16)
            f_hi, f_lo = feat[:, 0], feat[:, 1]
            sc = sb(ctx, "scores6", [P, T, 2, 1], F32)
            linear("l3b", lambda i: [(0, H4 * C4, tile_of(out3, i))], H4 * C4, ins["L3_gnn_W2"], D,
                   out_hi=tile_half(f_hi), out_lo=tile_half(f_lo), turned_w=True, relu=True, heads=1,
                   att=[ins["L3_gnn_att_src2"], ins["L3_gnn_att_dst2"]], scores=tile_scores(sc),
                   w_room=feat[:].rearrange("p e t c -> p (e t c)").bitcast(F32))
            attention("t3b", 1, D, feature_half(f_hi, D), feature_half(f_lo, D), sc, logc, ins["L3_gnn_b2"],
                      lambda h, i: tile_of(x, i), residual=x, stats=stats)

        out_stored = sem("out_stored")

        def store_out(sp, i):
            rows = P if i < T - 1 else LAST
            sp.dma_start(out[i * P:i * P + rows, :], x[0:rows, i]).then_inc(out_stored, 16)
            if i == T - 1:
                sp.wait_ge(out_stored, 16 * T)

        layer_norm("n4", x, store=store_out, stats=stats)


_INS = ["x", "src", "dst", "L0_gnn_t", "L0_gnn_W1", "L0_gnn_b1", "L0_gnn_bn_gamma", "L0_gnn_bn_beta",
        "L0_gnn_bn_mean", "L0_gnn_bn_var", "L0_gnn_W2", "L0_gnn_b2", "L1_gnn_W1", "L1_gnn_a1_src", "L1_gnn_a1_dst",
        "L1_gnn_b1", "L1_gnn_W2", "L1_gnn_a2_src", "L1_gnn_a2_dst", "L1_gnn_b2", "L2_gnn_norm_g", "L2_gnn_norm_b",
        "L2_gnn_W1", "L2_gnn_a_src1", "L2_gnn_a_dst1", "L2_gnn_b1", "L2_gnn_W2", "L2_gnn_a_src2", "L2_gnn_a_dst2",
        "L2_gnn_b2", "L2_gnn_Wu", "L2_gnn_bu", "L3_gnn_W1", "L3_gnn_att_src1", "L3_gnn_att_dst1", "L3_gnn_b1",
        "L3_gnn_W2", "L3_gnn_att_src2", "L3_gnn_att_dst2", "L3_gnn_b2"]


def kernel(**inputs):
    import numpy as _np
    import concourse.bacc as _bacc
    from concourse import mybir as _mybir
    from concourse.bass_utils import run_bass_kernel_spmd as _run

    nc = _bacc.Bacc("TRN2", target_bir_lowering=False, num_devices=1)
    arrays, args = {}, {}
    for name in _INS:
        a = _np.ascontiguousarray(inputs[name])
        if a.ndim == 0:
            a = a.reshape(1)
        arrays[f"in_{name}_dram"] = a
        args[name] = nc.dram_tensor(f"in_{name}_dram", a.shape, _mybir.dt.from_np(a.dtype), kind="ExternalInput").ap()
    out = nc.dram_tensor("out_dram", inputs["x"].shape, _mybir.dt.float32, kind="ExternalOutput").ap()
    bass_gnn_kernel(nc, args, out)
    r = _run(nc, [arrays], core_ids=[0])
    return r.results[0]["out_dram"]
```

```python
from contextlib import ExitStack

import numpy as np
import concourse.bass as bass
from concourse import mybir

ALU = mybir.AluOpType
ACT = mybir.ActivationFunctionType
AX = mybir.AxisListType
F32 = mybir.dt.float32
F32R = mybir.dt.float32r
F16 = mybir.dt.float16
I32 = mybir.dt.int32
U16 = mybir.dt.uint16

P = 128
BANK = 512
NO_EDGE = -1.0e30
LN_EPS = 1e-5
EPS_MSG = 1e-7
BAND = 60.0
W_SCALE = 64.0


def bass_gnn_kernel(nc: bass.Bass, ins, out: bass.AP):
    x_d, src_d, dst_d = ins["x"], ins["src"], ins["dst"]
    N, D = x_d.shape
    E = src_d.shape[0]
    T = -(-N // P)
    assert T % 2 == 0
    NP = T * P
    LAST = N - (T - 1) * P
    CHUNKS = [(a, min(a + BANK, NP)) for a in range(0, NP, BANK)]
    HALF = NP // 2
    HB = HALF // P

    root = ExitStack()
    with root:
        ps = root.enter_context(nc.psum_tensor("ps", [P, 8 * BANK], F32))

        def bank(b, width):
            return ps[:, b * BANK:b * BANK + width]

        def sb(ctx, name, shape, dt):
            return ctx.enter_context(nc.sbuf_tensor(name, shape, dt))

        in_use = []

        def sem(name):
            in_use.append(nc.alloc_semaphore(name))
            return in_use[-1]

        def recycle_semaphores(first=0):
            nc.clear_and_free_semaphores(in_use[first:])
            del in_use[first:]
            nc.all_engine_barrier()

        def tile_of(t, i):
            return t[:, bass.ds(i, 1)].rearrange("p o c -> p (o c)")

        def over_partitions(ap):
            return ap.rearrange("(o f) -> o f", o=1).to_broadcast([P, ap.shape[0]])

        ident = sb(root, "ident", [P, P], F32)
        ones = sb(root, "ones", [P, P], F32)
        stats = sb(root, "stats", [P, T, 2, 6], F32)

        x_spill = nc.dram_tensor("x_spill", (NP, D), F32, kind="Internal").ap().rearrange("(t p) c -> p t c", p=P)
        logc_d = nc.dram_tensor("logc_d", (NP, NP), F32, kind="Internal").ap().rearrange("(t p) s -> p t s", p=P)
        logc_diag_d = nc.dram_tensor("logc_diag_d", (P, T, P), F32, kind="Internal").ap()
        bn_d = nc.dram_tensor("bn_d", (2, ins["L0_gnn_W1"].shape[1]), F32, kind="Internal").ap()
        open_d = nc.dram_tensor("open_d", (P, T, D), F32, kind="Internal").ap()
        src_rows_d = nc.dram_tensor("src_rows_d", (16, NP), F32, kind="Internal").ap()


        def in_pairs(eng, body, first, last):
            n = first
            if n % 2:
                body(n, 1)
                n += 1
            pairs = (last - n) // 2
            if pairs > 0:
                with eng.Fori(0, pairs) as q:
                    body(q * 2 + n, 0)
                    body(q * 2 + (n + 1), 1)
                n += 2 * pairs
            if n < last:
                body(n, 0)

        WIDE = 2 * D

        def count_and_weigh(count, hi, lo, tcol, shift, bands, t_d):
            R, REM = divmod(E, P)
            G = -(-(R + 1) // P)
            BATCH = 4
            BATCHES = -(-(R + 1) // BATCH)
            ENDS = P * G // BATCH
            FULL = R - (G - 1) * P
            FAR = 1000.0
            assert REM and G == 2 and BATCHES < FAR
            with ExitStack() as ctx:
                edges = sb(ctx, "edges", [P, 2, G, P], I32)
                edges_f = sb(ctx, "edges_f", [P, 2, G, P], F32)
                edge_cols = sb(ctx, "edge_cols", [P, 2 * G * P], F32)
                iota = sb(ctx, "iota", [P, NP], F16)
                zeros = sb(ctx, "zeros", [P, P], F16)
                before = sb(ctx, "before", [T, T], F32)
                batch_no = sb(ctx, "batch_no", [T, BATCHES], F32)
                block_ends = sb(ctx, "block_ends", [T, 2], F32)
                tile_ends = sb(ctx, "tile_ends", [P, 2 * G], F32)
                diag = sb(ctx, "diag", [P, 2 * G * P], F32)
                batch_ends = sb(ctx, "batch_ends", [T, 2, ENDS], F32)
                holds = sb(ctx, "holds", [T, 3, BATCHES], F32)
                span = sb(ctx, "span", [T, 3], F32)
                table = sb(ctx, "table", [1, 3 * T], I32)
                hot_dst = sb(ctx, "hot_dst", [P, BATCH, P], F16)
                hot_src = sb(ctx, "hot_src", [P, BATCH, NP], F16)
                WITH_LOOPS = NP + P
                logs = sb(ctx, "logs", [P, WITH_LOOPS], F32)
                tiny = sb(ctx, "tiny", [P, 1], F32)
                mask = sb(ctx, "mask", [P, WITH_LOOPS], F32)
                looped = sb(ctx, "looped", [P, P], F32)
                xr = sb(ctx, "xr", [P, 2, D], F32)
                greatest = sb(ctx, "greatest", [P, T], F32)
                peak = sb(ctx, "peak", [P, 2], F32)
                peak_row = sb(ctx, "peak_row", [1, 4], F32)
                msg = sb(ctx, "msg", [P, D], F32)
                both = sb(ctx, "both", [P, WIDE], F32)
                consts, loaded = sem("g_consts"), sem("g_loaded")
                dve, pe_pre = sem("g_dve"), sem("g_pe_pre")
                hot_ready, hot_free = sem("g_hot_ready"), sem("g_hot_free")
                block_done = sem("g_block_done")
                counted, logged = sem("g_counted"), sem("g_logged")
                masked, loops_in, rows_stored = sem("g_masked"), sem("g_loops_in"), sem("g_rows_stored")
                x_first = [sem(f"g_x_first{r}") for r in range(4)]
                x_in = [sem(f"g_x_in{r}") for r in range(2)]
                first_room = [xr[:, 0], xr[:, 1], both[:, 0:D], both[:, D:WIDE]]
                t_in, x_seen, peak_step, peak_pe = sem("g_t_in"), sem("g_x_seen"), sem("g_peak_step"), sem("g_peak_pe")
                msgs, exps, prods, band_step = sem("g_msgs"), sem("g_exps"), sem("g_prods"), sem("g_band_step")
                his, los = sem("g_his"), sem("g_los")
                N_CONST = 12
                TABLE = 15 + 2 * G
                PEAK = 6

                with nc.Block() as block:
                    @block.gpsimd
                    def _(pool):
                        pool.memset(edges[:, 0], NP - 1).then_inc(consts, 1)
                        pool.memset(edges[:, 1], -1).then_inc(consts, 1)
                        pool.memset(ident[:], 0.0).then_inc(consts, 1)
                        pool.memset(ones[:], 1.0).then_inc(consts, 1)
                        pool.memset(zeros[:], 0.0).then_inc(consts, 1)
                        pool.memset(tiny[:], 1e-30).then_inc(consts, 1)
                        pool.iota(iota[:], [[1, NP]], base=0, channel_multiplier=0,
                                  allow_small_or_imprecise_dtypes=True).then_inc(consts, 1)
                        pool.iota(batch_no[:], [[1, BATCHES]], base=0, channel_multiplier=0,
                                  allow_small_or_imprecise_dtypes=True).then_inc(consts, 1)
                        pool.iota(block_ends[:], [[P, 2]], base=0, channel_multiplier=P,
                                  allow_small_or_imprecise_dtypes=True).then_inc(consts, 1)
                        pool.sem_inc(hot_free, BATCH)
                        pool.wait_ge(consts, 4)
                        pool.affine_select(out=ident[:], in_=ident[:], compare_op=ALU.not_equal, fill=1.0, base=0,
                                           pattern=[[-1, P]], channel_multiplier=1).then_inc(consts, 1)
                        pool.affine_select(out=before[:], in_=ones[0:T, 0:T], compare_op=ALU.is_gt, fill=0.0, base=0,
                                           pattern=[[1, T]], channel_multiplier=-1).then_inc(consts, 2)

                        def weigh(i):
                            r = i % 2
                            pool.wait_ge(x_in[r], 16 * (i // 2 + 1))
                            pool.tensor_scalar(msg[:], xr[:, r], 0.0, EPS_MSG, ALU.max, ALU.add).then_inc(msgs, 1)
                            pool.wait_ge(exps, i + 1)
                            pool.wait_ge(msgs, i + 1)
                            pool.tensor_tensor(both[:, D:WIDE], both[:, 0:D], msg[:], ALU.mult).then_inc(prods, 1)
                            pool.wait_ge(his, i + 1)
                            pool.tensor_tensor(lo[:, i], both[:], hi[:, i].bitcast(F32), ALU.subtract).then_inc(los, 1)

                        weigh(0)
                        weigh(1)
                        for b in range(T):
                            pool.wait_ge(counted, b + 1)
                            pool.tensor_tensor(looped[:], looped[:], ident[:], ALU.add).then_inc(loops_in, 1)
                            if b + 2 < T:
                                weigh(b + 2)

                    @block.sync
                    def _(sp):
                        def load_x(i, to, loaded):
                            rows = P if i < T - 1 else LAST
                            sp.dma_start(to[0:rows], x_d[i * P:i * P + rows, :]).then_inc(loaded, 16)

                        sp.wait_ge(consts, 2)
                        for k, a in ((0, dst_d), (1, src_d)):
                            first = (G - 1) * P * P
                            sp.dma_start(edges[:, k, 0, :],
                                         a[0:first].rearrange("(t e) -> t e", e=P)).then_inc(loaded, 16)
                            sp.dma_start(edges[0:FULL, k, 1, :],
                                         a[first:R * P].rearrange("(t e) -> t e", e=P)).then_inc(loaded, 16)
                            sp.dma_start(edges[FULL:FULL + 1, k, 1, 0:REM],
                                         a[R * P:E].rearrange("(t e) -> t e", e=REM)).then_inc(loaded, 16)
                        sp.dma_start(tcol[:], over_partitions(t_d)).then_inc(t_in, 16)
                        for i in range(T):
                            if i >= 4:
                                sp.wait_ge(x_seen, i - 3)
                            load_x(i, first_room[i % 4], x_first[i % 4])
                        sp.wait_ge(x_seen, T)
                        for i in range(2):
                            load_x(i, xr[:, i], x_in[i])
                        for i in range(T):
                            if i + 2 < T:
                                sp.wait_ge(msgs, i + 1)
                                load_x(i + 2, xr[:, i % 2], x_in[i % 2])
                            sp.wait_ge(masked, i + 1)
                            sp.dma_start(logc_diag_d[:, i], logs[:, i * P:(i + 1) * P]).then_inc(rows_stored, 16)
                            sp.dma_start(logc_d[:, i], logs[:, 0:NP]).then_inc(rows_stored, 16)
                            sp.wait_ge(rows_stored, 48 * i + 32)
                            sp.dma_start(logc_d[:, i, i * P:(i + 1) * P], logs[:, NP:WITH_LOOPS]
                                         ).then_inc(rows_stored, 16)
                        sp.wait_ge(rows_stored, 48 * T)

                    @block.vector
                    def _(v):
                        done = [0, 0, 0]

                        def step(ins, k=0):
                            done[k] += 1
                            ins.then_inc((dve, peak_step, band_step)[k], 1)
                            v.wait_ge((dve, peak_step, band_step)[k], done[k])

                        v.wait_ge(consts, N_CONST)
                        v.wait_ge(loaded, 6 * 16)
                        step(v.tensor_copy(edges_f[:], edges[:]))
                        step(v.tensor_reduce(tile_ends[:, 0:G], edges_f[:, 0], AX.X, ALU.min))
                        step(v.tensor_reduce(tile_ends[:, G:2 * G], edges_f[:, 0], AX.X, ALU.max))
                        for k in range(2 * G):
                            step(v.tensor_scalar(diag[:, k * P:(k + 1) * P], ident[:], tile_ends[:, k:k + 1], None,
                                                 ALU.mult))
                        v.wait_ge(pe_pre, 1)
                        step(v.tensor_copy(edge_cols[:], bank(0, 2 * G * P)))
                        v.wait_ge(pe_pre, 2)
                        for k, op in ((0, ALU.min), (1, ALU.max)):
                            step(v.tensor_reduce(
                                batch_ends[:, k],
                                bank(1, BANK)[0:T, k * G * P:(k + 1) * G * P].rearrange("b (j m) -> b j m", m=BATCH),
                                AX.X, op))
                        step(v.tensor_scalar(holds[:, 0], batch_ends[:, 0, 0:BATCHES], block_ends[:, 1:2], None,
                                             ALU.is_lt))
                        step(v.scalar_tensor_tensor(out=holds[:, 1], in0=batch_ends[:, 1, 0:BATCHES],
                                                    scalar=block_ends[:, 0:1], in1=holds[:, 0], op0=ALU.is_ge,
                                                    op1=ALU.mult))
                        step(v.scalar_tensor_tensor(out=holds[:, 0], in0=holds[:, 1], scalar=-FAR, in1=batch_no[:],
                                                    op0=ALU.mult, op1=ALU.add))
                        step(v.tensor_reduce(span[:, 0:1], holds[:, 0], AX.X, ALU.min))
                        step(v.scalar_tensor_tensor(out=holds[:, 2], in0=batch_no[:], scalar=1.0, in1=holds[:, 1],
                                                    op0=ALU.add, op1=ALU.mult))
                        step(v.tensor_reduce(span[:, 1:2], holds[:, 2], AX.X, ALU.max))
                        step(v.tensor_scalar(span[:, 0:1], span[:, 0:1], FAR, float(BATCHES - 1), ALU.add, ALU.min))
                        step(v.tensor_scalar(span[:, 2:3], span[:, 1:2], span[:, 0:1], 1.0, ALU.subtract, ALU.max))
                        v.wait_ge(pe_pre, 3)
                        step(v.tensor_copy(table[:], bank(2, 3 * T)[0:1, :]))
                        assert done[0] == TABLE

                        for i in range(T):
                            v.wait_ge(x_first[i % 4], 16 * (i // 4 + 1))
                            v.tensor_reduce(greatest[:, i:i + 1], first_room[i % 4], AX.X, ALU.max).then_inc(x_seen, 1)
                        v.wait_ge(x_seen, T)
                        v.wait_ge(t_in, 16)
                        step(v.tensor_reduce(peak[:, 0:1], greatest[:], AX.X, ALU.max), 1)
                        step(v.memset(peak[:, 1:2], 0.0), 1)
                        step(v.tensor_scalar(peak[:, 0:2], peak[:, 0:2], 0.0, EPS_MSG, ALU.max, ALU.add), 1)
                        step(v.tensor_scalar(peak[:, 0:2], peak[:, 0:2], tcol[:], None, ALU.mult), 1)
                        v.wait_ge(peak_pe, 1)
                        step(v.tensor_reduce(peak_row[:, 0:1], bank(3, 2 * P)[0:1, :], AX.X, ALU.max), 1)
                        v.wait_ge(peak_pe, 2)
                        step(v.tensor_scalar(shift[:], bank(4, 1), -1.0, None, ALU.mult), 1)
                        step(v.tensor_reduce(peak_row[:, 1:2], bank(3, 2 * P)[0:1, :], AX.X, ALU.min), 2)
                        step(v.tensor_scalar(peak_row[:, 2:3], peak_row[:, 0:1], peak_row[:, 1:2], 1.0 / BAND,
                                             ALU.subtract, ALU.mult), 2)
                        step(v.tensor_scalar(bands[:], peak_row[:, 2:3], 1.0, 1e6, ALU.add, ALU.min), 2)
                        assert done[1] == PEAK

                        def one_hots(b):
                            first = v.value_load(table[0:1, bass.ds(b, 1)], min_val=0, max_val=BATCHES - 1)
                            batches = v.value_load(table[0:1, bass.ds(b + T, 1)], min_val=1, max_val=BATCHES)
                            past = v.value_load(table[0:1, bass.ds(b + 2 * T, 1)], min_val=0, max_val=T * BATCHES)
                            with v.Fori(0, batches) as j:
                                t = ((first + j) * BATCH).with_bounds(min_val=0, max_val=BATCH * (BATCHES - 1))
                                for k in range(BATCH):
                                    v.wait_ge(hot_free, (past + j) * BATCH + (k + 1))
                                    v.tensor_scalar(hot_dst[:, k], iota[:, bass.ds(b * P, P)],
                                                    edge_cols[:, bass.ds(t + k, 1)], None, ALU.is_equal)
                                    v.tensor_scalar(hot_src[:, k], iota[:], edge_cols[:, bass.ds(t + (k + G * P), 1)],
                                                    None, ALU.is_equal).then_inc(hot_ready, 1)

                        def mask_logs(b):
                            v.wait_ge(logged, b * 2 + 6)
                            v.tensor_tensor(logs[:], logs[:], mask[:], ALU.min).then_inc(masked, 1)

                        one_hots(0)
                        with v.Fori(1, T) as b:
                            one_hots(b)
                            mask_logs(b - 1)
                        mask_logs(T - 1)

                    @block.tensor
                    def _(pe):
                        pe.wait_ge(consts, N_CONST)
                        pe.wait_ge(dve, 1)
                        flat = edges_f[:].rearrange("p a g e -> p (a g e)")
                        for k in range(2 * G):
                            mm = pe.transpose(bank(0, BANK)[:, k * P:(k + 1) * P], flat[:, k * P:(k + 1) * P], ident[:])
                        mm.then_inc(pe_pre, 1)
                        pe.wait_ge(dve, 3 + 2 * G)
                        pe.matmul(bank(1, BANK)[0:T, :], ones[:, 0:T], diag[:], start=True,
                                  stop=True).then_inc(pe_pre, 1)
                        pe.wait_ge(dve, 14 + 2 * G)
                        rows = bank(2, 3 * T)
                        pe.matmul(rows[0:1, 0:T], span[:, 0:1], ident[0:T, 0:T], start=True, stop=True)
                        pe.matmul(rows[0:1, T:2 * T], span[:, 2:3], ident[0:T, 0:T], start=True, stop=True)
                        pe.matmul(rows[0:1, 2 * T:3 * T], span[:, 2:3], before[:], start=True,
                                  stop=True).then_inc(pe_pre, 1)
                        pe.wait_ge(peak_step, 4)
                        for k in range(2):
                            mm = pe.transpose(bank(3, 2 * P)[0:1, k * P:(k + 1) * P], peak[:, k:k + 1], ident[:])
                        mm.then_inc(peak_pe, 1)
                        pe.wait_ge(peak_step, 5)
                        pe.matmul(bank(4, 1), ones[0:1, :], peak_row[:, 0:1], start=True,
                                  stop=True).then_inc(peak_pe, 1)
                        pe.wait_ge(band_step, 3)
                        pe.wait_ge(dve, TABLE)
                        with pe.Fori(0, T // 2) as b2:
                            for r in range(2):
                                b = b2 * 2 + r
                                base = 4 * r
                                batches = pe.value_load(table[0:1, bass.ds(b + T, 1)], min_val=1, max_val=BATCHES)
                                past = pe.value_load(table[0:1, bass.ds(b + 2 * T, 1)], min_val=0,
                                                     max_val=T * BATCHES)
                                pe.wait_ge(logged, b * 2 + 2)
                                for a, z in CHUNKS:
                                    pe.matmul(ps[:, base * BANK + a:base * BANK + z], zeros[:], iota[:, a:z],
                                              start=True, stop=False, skip_group_check=True)
                                with pe.Fori(0, batches) as j:
                                    for k in range(BATCH):
                                        pe.wait_ge(hot_ready, (past + j) * BATCH + (k + 1))
                                        for a, z in CHUNKS:
                                            mm = pe.matmul(ps[:, base * BANK + a:base * BANK + z], hot_dst[:, k],
                                                           hot_src[:, k, a:z], start=False, stop=False,
                                                           skip_group_check=True)
                                        mm.then_inc(hot_free, 1)
                                for a, z in CHUNKS:
                                    mm = pe.matmul(ps[:, base * BANK + a:base * BANK + z], zeros[:], iota[:, a:z],
                                                   start=False, stop=True, skip_group_check=True)
                                mm.then_inc(block_done, 1)

                    @block.scalar
                    def _(act):
                        def weigh(i):
                            if i == 0:
                                act.wait_ge(peak_step, PEAK)
                            act.wait_ge(msgs, i + 1)
                            if i:
                                act.wait_ge(los, i)
                            act.activation(both[:, 0:D], msg[:], ACT.Exp, bias=shift[:],
                                           scale=tcol[:]).then_inc(exps, 1)
                            act.wait_ge(prods, i + 1)
                            act.activation(hi[:, i], both[:], ACT.Copy).then_inc(his, 1)

                        act.sem_inc(logged, 4)
                        weigh(0)
                        weigh(1)
                        for b in range(T):
                            of = ps[:, 4 * (b % 2) * BANK:4 * (b % 2) * BANK + NP]
                            act.wait_ge(block_done, b + 1)
                            act.activation(count[:, b], of, ACT.Copy)
                            if b:
                                act.wait_ge(logged, 4 + 2 * b)
                            act.activation(looped[:], of[:, b * P:(b + 1) * P], ACT.Copy).then_inc(counted, 1)
                            act.wait_ge(loops_in, b + 1)
                            if b:
                                act.wait_ge(rows_stored, 48 * b)
                            act.activation(mask[:, NP:WITH_LOOPS], looped[:], ACT.Copy, scale=-2 * NO_EDGE,
                                           bias=NO_EDGE)
                            act.activation(mask[:, 0:NP], of, ACT.Copy, scale=-2 * NO_EDGE,
                                           bias=NO_EDGE).then_inc(logged, 1)
                            act.activation(logs[:, NP:WITH_LOOPS], looped[:], ACT.Ln, bias=tiny[:])
                            act.activation(logs[:, 0:NP], of, ACT.Ln, bias=tiny[:]).then_inc(logged, 1)
                            if b + 2 < T:
                                weigh(b + 2)

        def channel_softmax(name, x, count, hi, lo, in_bands=False, beside=None):
            wide_chunks = [(a, min(a + BANK, WIDE)) for a in range(0, WIDE, BANK)]
            NC = len(wide_chunks)
            OUT0 = 4
            with ExitStack() as ctx:
                countf = sb(ctx, f"{name}_countf", [P, NP], F32)
                count_t = sb(ctx, f"{name}_count_t", [P, 2, T, P], F32R)
                sums = sb(ctx, f"{name}_sums", [P, WIDE], F32)
                if in_bands:
                    is_open = sb(ctx, "is_open", [P, D], F32)
                    found = sb(ctx, "found", [P, D], F32)
                    open_in, open_out = sem(f"{name}_open_in"), sem(f"{name}_open_out")
                x_in, zeroed = sem(f"{name}_x_in"), sem(f"{name}_zeroed")
                copied, turned, count_in = sem(f"{name}_copied"), sem(f"{name}_turned"), sem(f"{name}_count_in")
                summed, saved = sem(f"{name}_summed"), sem(f"{name}_saved")
                added, chain = sem(f"{name}_added"), sem(f"{name}_chain")
                with nc.Block() as block:
                    @block.gpsimd
                    def _(pool):
                        pool.sem_inc(added, 1)
                        pool.sem_inc(saved, NC)
                        pool.sem_inc(turned, 2)
                        if not in_bands:
                            pool.memset(x[:, T - 1], 0.0).then_inc(zeroed, 1)
                        with pool.Fori(0, T) as i:
                            pool.wait_ge(turned, i * 2 + 2)
                            pool.tensor_copy(countf[:], tile_of(count, i)).then_inc(copied, 1)

                    @block.sync
                    def _(sp):
                        if in_bands:
                            for i in range(T):
                                if i:
                                    sp.wait_ge(added, 2 * i + 1)
                                    sp.dma_start(open_d[:, i - 1], is_open[:]).then_inc(open_out, 16)
                                    sp.wait_ge(open_out, 16 * i)
                                sp.dma_start(is_open[:], open_d[:, i]).then_inc(open_in, 16)
                            sp.wait_ge(added, 2 * T + 1)
                            sp.dma_start(open_d[:, T - 1], is_open[:]).then_inc(open_out, 16)
                            sp.wait_ge(open_out, 16 * T)
                            return
                        sp.dma_start(x[:, 0:T - 1], x_d[0:(T - 1) * P, :].rearrange("(t p) c -> p t c", p=P)
                                     ).then_inc(x_in, 16)
                        sp.wait_ge(zeroed, 1)
                        sp.dma_start(x[0:LAST, T - 1], x_d[(T - 1) * P:N, :]).then_inc(x_in, 16)
                        if beside:
                            beside["sync"](sp)

                    @block.tensor
                    def _(pe):
                        def turn(i, r):
                            pe.wait_ge(copied, i + 1)
                            if not isinstance(i, int) or i > 0:
                                pe.wait_ge(count_in, i * 2)
                            for g in range(2):
                                for k in range(HB):
                                    mm = pe.transpose(ps[:, 2 * g * BANK + k * P:2 * g * BANK + (k + 1) * P],
                                                      countf[:, (g * HB + k) * P:(g * HB + k + 1) * P], ident[:])
                                mm.then_inc(turned, 1)

                        def products(i, r):
                            pe.wait_ge(count_in, i * 2 + 2)
                            for c, (a, z) in enumerate(wide_chunks):
                                pe.wait_ge(saved, i * NC + (c + 1))
                                for k in range(T):
                                    for h, half in enumerate((hi, lo)):
                                        mm = pe.matmul(ps[:, OUT0 * BANK + a:OUT0 * BANK + z], count_t[:, r, k],
                                                       half[:, k, a:z], start=(k == 0 and h == 0),
                                                       stop=(k == T - 1 and h == 1))
                                mm.then_inc(summed, 1)

                        def body(i, r):
                            turn(i + 1, 1 - r)
                            products(i, r)

                        turn(0, 0)
                        body(0, 0)
                        in_pairs(pe, body, 1, T - 1)
                        products(T - 1, 1)

                    @block.scalar
                    def _(act):
                        def take(i, r):
                            if not isinstance(i, int) or i >= 2:
                                act.wait_ge(summed, (i - 1) * NC)
                            for g in range(2):
                                act.wait_ge(turned, i * 2 + (g + 3))
                                act.activation(count_t[:, r, g * HB:(g + 1) * HB].rearrange("p k s -> p (k s)"),
                                               ps[:, 2 * g * BANK:2 * g * BANK + HALF], ACT.Copy).then_inc(count_in, 1)

                        def save(i, r):
                            act.wait_ge(added, i * (1 + in_bands) + 1)
                            for c, (a, z) in enumerate(wide_chunks):
                                act.wait_ge(summed, i * NC + (c + 1))
                                act.activation(sums[:, a:z], ps[:, OUT0 * BANK + a:OUT0 * BANK + z],
                                               ACT.Copy).then_inc(saved, 1)

                        def body(i, r):
                            take(i + 1, 1 - r)
                            save(i, r)

                        if beside:
                            beside["scalar"](act)
                        take(0, 0)
                        body(0, 0)
                        in_pairs(act, body, 1, T - 1)
                        save(T - 1, 1)

                    @block.vector
                    def _(v):
                        if beside:
                            beside["vector"](v)
                        if not in_bands:
                            v.wait_ge(x_in, 32)
                        STEPS = 6 if in_bands else 3
                        with v.Fori(0, T) as i:
                            done = [0]

                            def step(ins_):
                                done[0] += 1
                                ins_.then_inc(chain, 1)
                                v.wait_ge(chain, i * STEPS + done[0])

                            v.wait_ge(saved, i * NC + 2 * NC)
                            if in_bands:
                                v.wait_ge(open_in, i * 16 + 16)
                                step(v.tensor_scalar(found[:], sums[:, 0:D], 0.5 * float(np.exp(-BAND)), None,
                                                     ALU.is_ge))
                                step(v.tensor_tensor(found[:], found[:], is_open[:], ALU.mult))
                            step(v.tensor_scalar(sums[:, 0:D], sums[:, 0:D], 1e-37, None, ALU.max))
                            step(v.reciprocal(sums[:, 0:D], sums[:, 0:D]))
                            step(v.tensor_tensor(sums[:, D:WIDE], sums[:, D:WIDE], sums[:, 0:D], ALU.mult))
                            if in_bands:
                                step(v.tensor_tensor(sums[:, D:WIDE], sums[:, D:WIDE], found[:], ALU.mult))
                                v.tensor_tensor(is_open[:], is_open[:], found[:], ALU.subtract).then_inc(added, 1)
                            v.tensor_tensor(tile_of(x, i), tile_of(x, i), sums[:, D:WIDE], ALU.add).then_inc(added, 1)

        def softmax_in_bands(x, count, hi, lo, tcol, shift, bands):
            outer = len(in_use)
            with ExitStack() as ctx:
                all_open = sb(ctx, "all_open", [P, D], F32)
                zeroed, x_in, opened = sem("b_zeroed"), sem("b_x_in"), sem("b_opened")
                with nc.Block() as block:
                    @block.gpsimd
                    def _(pool):
                        pool.memset(all_open[:], 1.0).then_inc(zeroed, 1)
                        pool.memset(x[:, T - 1], 0.0).then_inc(zeroed, 1)

                    @block.sync
                    def _(sp):
                        sp.dma_start(x[:, 0:T - 1], x_d[0:(T - 1) * P, :].rearrange("(t p) c -> p t c", p=P)
                                     ).then_inc(x_in, 16)
                        sp.wait_ge(zeroed, 2)
                        sp.dma_start(x[0:LAST, T - 1], x_d[(T - 1) * P:N, :]).then_inc(x_in, 16)
                        for i in range(T):
                            sp.dma_start(open_d[:, i], all_open[:]).then_inc(opened, 16)
                        sp.wait_ge(x_in, 32)
                        sp.wait_ge(opened, 16 * T)

                    @block.tensor
                    def _(pe):
                        pe.wait_ge(x_in, 32)

                    @block.scalar
                    def _(act):
                        act.wait_ge(x_in, 32)

                    @block.vector
                    def _(v):
                        v.wait_ge(x_in, 32)
            recycle_semaphores(outer)

            number = nc.values_load(bands[0:1, 0:1], min_val=1, max_val=10 ** 6)
            with nc.Fori(0, number):
                with ExitStack() as ctx:
                    xr = sb(ctx, "b_xr", [P, D], F32)
                    msg = sb(ctx, "b_msg", [P, D], F32)
                    both = sb(ctx, "b_both", [P, WIDE], F32)
                    x_in, x_used, chain = sem("b_row_in"), sem("b_x_used"), sem("b_chain")
                    args, exps, prods = sem("b_args"), sem("b_exps"), sem("b_prods")
                    his, los, moved = sem("b_his"), sem("b_los"), sem("b_moved")
                    with nc.Block() as block:
                        @block.sync
                        def _(sp):
                            for i in range(T):
                                if i:
                                    sp.wait_ge(x_used, i)
                                rows = P if i < T - 1 else LAST
                                sp.dma_start(xr[0:rows], x_d[i * P:i * P + rows, :]).then_inc(x_in, 16)

                        @block.vector
                        def _(v):
                            for i in range(T):
                                v.wait_ge(x_in, 16 * (i + 1))
                                if i:
                                    v.wait_ge(los, i)
                                v.tensor_scalar(msg[:], xr[:], 0.0, EPS_MSG, ALU.max, ALU.add).then_inc(x_used, 1)
                                v.wait_ge(x_used, i + 1)
                                v.tensor_scalar(both[:, 0:D], msg[:], tcol[:], shift[:], ALU.mult,
                                                ALU.add).then_inc(chain, 1)
                                v.wait_ge(chain, i + 1)
                                v.tensor_scalar(both[:, 0:D], both[:, 0:D], 0.0, None, ALU.min).then_inc(args, 1)
                                v.wait_ge(exps, i + 1)
                                v.tensor_tensor(both[:, D:WIDE], both[:, 0:D], msg[:], ALU.mult).then_inc(prods, 1)
                                v.wait_ge(his, i + 1)
                                v.tensor_tensor(lo[:, i], both[:], hi[:, i].bitcast(F32), ALU.subtract
                                                ).then_inc(los, 1)
                            v.tensor_scalar(shift[:], shift[:], BAND, None, ALU.add).then_inc(moved, 1)
                            v.wait_ge(moved, 1)

                        @block.scalar
                        def _(act):
                            for i in range(T):
                                act.wait_ge(args, i + 1)
                                act.activation(both[:, 0:D], both[:, 0:D], ACT.Exp).then_inc(exps, 1)
                                act.wait_ge(prods, i + 1)
                                act.activation(hi[:, i], both[:], ACT.Copy).then_inc(his, 1)

                channel_softmax("mb", x, count, hi, lo, in_bands=True)
                recycle_semaphores(outer)

        def linear(name, pieces, K, w_d, F, *, out_hi=None, out_lo=None, out=None, finish=None, rows=(), turned_w=False,
                   elu=False, relu=False, heads=0, att=None, scores=None, room=None,
                   w_room=None, w_ring=4, junk_room=None,
                   beside=None):
            blocks = [(a, min(a + P, K)) for a in range(0, K, P)]
            KT = len(blocks)
            GROUP = 8
            groups = [range(g, min(g + GROUP, KT)) for g in range(0, KT, GROUP)]
            NG = len(groups)
            assert NG <= 2
            chunks = [(a, min(a + BANK, F)) for a in range(0, F, BANK)]
            NC = len(chunks) + bool(heads)
            RING = 4 if NC % 2 == 0 else 2
            OUT0 = 4
            S = 2 * heads
            C = F // heads if heads else 0
            with ExitStack() as ctx:
                w_hi = sb(ctx, f"{name}_w_hi", [P, KT, F], F16)
                w_lo = sb(ctx, f"{name}_w_lo", [P, KT, F], F16)
                if heads:
                    a_hi = sb(ctx, f"{name}_a_hi", [P, KT, S], F16)
                    a_lo = sb(ctx, f"{name}_a_lo", [P, KT, S], F16)
                if turned_w:
                    if w_room is not None:
                        w_nat = w_room[:, 0:F // P * K].rearrange("p (f k) -> p f k", k=K)
                    else:
                        w_nat = sb(ctx, f"{name}_w_nat", [P, F // P, K], F32)
                elif w_room is not None:
                    w_in = w_room[:, 0:w_ring * F].rearrange("p (r f) -> p r f", f=F)
                else:
                    w_in = sb(ctx, f"{name}_w_in", [P, w_ring, F], F32)
                if heads:
                    a_w = sb(ctx, f"{name}_a_w", [P, KT, S], F32)
                    att_row = sb(ctx, f"{name}_att_row", [P, 2, F], F32)
                    if junk_room is not None:
                        junk = junk_room[:, 0:2 * C].rearrange("p (r c) -> p r c", c=C)
                    else:
                        junk = sb(ctx, f"{name}_junk", [P, 2, C], F32)

                w_loaded = [sem(f"{name}_w_loaded{r}") for r in range(KT if turned_w else w_ring)]
                rows_in, w_turned = sem(f"{name}_rows_in"), sem(f"{name}_w_turned")
                w_high, w_split = sem(f"{name}_w_high"), sem(f"{name}_w_split")
                a_step = sem(f"{name}_a_step")

                def raw(k):
                    a, z = blocks[k]
                    if turned_w:
                        at = (OUT0 + 2 * (k % 2)) * BANK
                        return ps[:, at:at + F]
                    return w_in[0:z - a, k % w_ring]

                def load_weights(sp):
                    if turned_w:
                        for k, (a, z) in enumerate(blocks):
                            sp.dma_start(w_nat[:, :, a:z], w_d[:, a:z].rearrange("(t p) k -> p t k", p=P)
                                         ).then_inc(w_loaded[k], 16)
                    else:
                        for k, (a, z) in enumerate(blocks):
                            if k >= w_ring:
                                sp.wait_ge(w_split, k - w_ring + 1)
                            sp.dma_start(w_in[0:z - a, k % w_ring], w_d[a:z, :]
                                         ).then_inc(w_loaded[k % w_ring], 16)

                    if beside and "sync" in beside:
                        beside["sync"](sp)

                def load_rows(pool):
                    if beside and "gpsimd" in beside:
                        beside["gpsimd"](pool)
                    if heads:
                        for j in range(2):
                            pool.dma_start(att_row[:, j], over_partitions(att[j].rearrange("h c -> (h c)"))
                                           ).then_inc(rows_in, 16)
                    for to, ap in rows:
                        pool.dma_start(to, over_partitions(ap)).then_inc(rows_in, 16)

                def turn_weights(pe):
                    if turned_w:
                        for k in range(KT):
                            pe.wait_ge(w_loaded[k], 16)
                            if k >= 2:
                                pe.wait_ge(w_split, k - 1)
                            for f in range(F // P):
                                mm = pe.transpose(raw(k)[:, f * P:(f + 1) * P], w_nat[:, f, k * P:(k + 1) * P],
                                                  ident[:])
                            mm.then_inc(w_turned, 1)

                def weights_in(eng, k):
                    if turned_w:
                        eng.wait_ge(w_turned, k + 1)
                    else:
                        eng.wait_ge(w_loaded[k % w_ring], 16 * (k // w_ring + 1))

                def high_weights(act, first=0, last=KT):
                    for k in range(first, last):
                        a, z = blocks[k]
                        weights_in(act, k)
                        act.activation(w_hi[0:z - a, k], raw(k), ACT.Copy, scale=W_SCALE).then_inc(w_high, 1)

                def wait_rows(v):
                    if heads or rows:
                        v.wait_ge(rows_in, 16 * (2 * bool(heads) + len(rows)))

                def score_weights(v, k):
                    for j in range(S):
                        h, n = j % heads, k * S + j
                        if n >= 2:
                            v.wait_ge(a_step, n - 1)
                        v.tensor_tensor_reduce(junk[:, n % 2], raw(k)[:, h * C:(h + 1) * C],
                                               att_row[:, j // heads, h * C:(h + 1) * C], 1.0, 0.0,
                                               ALU.mult, ALU.add, a_w[:, k, j:j + 1]).then_inc(a_step, 1)

                def split_weights(v, first=0, last=KT):
                    at_once = w_ring < KT or turned_w
                    if at_once and first == 0:
                        wait_rows(v)
                    for k in range(first, last):
                        a, z = blocks[k]
                        weights_in(v, k)
                        v.wait_ge(w_high, k + 1)
                        if at_once:
                            score_weights(v, k)
                        v.scalar_tensor_tensor(out=w_lo[0:z - a, k], in0=raw(k), scalar=W_SCALE,
                                               in1=w_hi[0:z - a, k], op0=ALU.mult,
                                               op1=ALU.subtract).then_inc(w_split, 1)
                    if last < KT:
                        return
                    if not at_once:
                        wait_rows(v)
                        for k in range(KT):
                            score_weights(v, k)
                    if heads:
                        v.wait_ge(a_step, KT * S)
                        v.tensor_scalar(a_hi[:], a_w[:], W_SCALE, None, ALU.mult).then_inc(a_step, 1)
                        v.wait_ge(a_step, KT * S + 1)
                        v.scalar_tensor_tensor(out=a_lo[:].rearrange("p k s -> p (k s)"),
                                               in0=a_w[:].rearrange("p k s -> p (k s)"), scalar=W_SCALE,
                                               in1=a_hi[:].rearrange("p k s -> p (k s)"), op0=ALU.mult,
                                               op1=ALU.subtract).then_inc(a_step, 1)
                    if beside and "vector" in beside:
                        beside["vector"](v)

                stage = sb(ctx, f"{name}_stage", [P, 2, K], F32)
                if room:
                    xt_hi, xt_lo = (part[:, 0:2 * KT * P].rearrange("p (r k n) -> p r k n", r=2, n=P) for part in room)
                else:
                    xt_hi = sb(ctx, f"{name}_xt_hi", [P, 2, KT, P], F16)
                    xt_lo = sb(ctx, f"{name}_xt_lo", [P, 2, KT, P], F16)
                staged, turned, slot_free = sem(f"{name}_staged"), sem(f"{name}_turned"), sem(f"{name}_slot_free")
                xt_high, summed = sem(f"{name}_xt_high"), sem(f"{name}_summed")
                out_high, out_free = sem(f"{name}_out_high"), sem(f"{name}_out_free")
                below, expd, seen = sem(f"{name}_below"), sem(f"{name}_expd"), sem(f"{name}_seen")
                SLOTS = 2

                def slot(r, g):
                    return ((r * NG + g) % SLOTS) * 2 * BANK

                def out_bank(r, c, width):
                    return bank(OUT0 + (r * NC + c) % RING, width)

                def turned_parts(r, g, ks):
                    whole = [k for k in ks if blocks[k][1] - blocks[k][0] == P]
                    runs = [(P, whole[0], whole[-1] + 1)] if whole else []
                    runs += [(blocks[k][1] - blocks[k][0], k, k + 1) for k in ks if k not in whole]
                    for n, ka, kz in runs:
                        at = slot(r, g) + (ka - ks[0]) * P
                        yield n, ka, kz, ps[0:n, at:at + (kz - ka) * P]

                def stage_is_free(eng, i):
                    eng.wait_ge(slot_free, i * NG + (SLOTS - NG))

                NPC = len(pieces(0))
                EARLY = KT // 2 if elu else 0
                with nc.Block() as block:
                    @block.sync
                    def _(sp):
                        load_weights(sp)

                    @block.gpsimd
                    def _(pool):
                        load_rows(pool)
                        pool.sem_inc(slot_free, SLOTS)
                        pool.sem_inc(out_free, RING)

                        def body(i, r):
                            if elu:
                                pool.wait_ge(expd, (i + 1) * NPC)
                                pool.sem_inc(seen, 1)
                                pool.tensor_scalar(stage[:, r], stage[:, r], 1.0, -1.0, ALU.min,
                                                   ALU.add).then_inc(below, 1)
                                return
                            stage_is_free(pool, i)
                            for a, z, part in pieces(i):
                                pool.tensor_copy(stage[:, r, a:z], part).then_inc(staged, 1)

                        in_pairs(pool, body, 0, T)

                    @block.tensor
                    def _(pe):
                        def turn(i, r):
                            pe.wait_ge(staged, (i + 1) * NPC)
                            for g, ks in enumerate(groups):
                                pe.wait_ge(slot_free, i * NG + (g + 1))
                                for k in ks:
                                    a, z = blocks[k]
                                    at = slot(r, g) + (k - ks[0]) * P
                                    mm = pe.transpose(ps[0:z - a, at:at + P], stage[:, r, a:z], ident[:])
                                mm.then_inc(turned, 1)

                        def products(i, r):
                            pe.wait_ge(slot_free, i * NG + (NG + SLOTS))
                            for c in range(NC):
                                pe.wait_ge(out_free, i * NC + (c + 1))
                                if c < len(chunks):
                                    a, z = chunks[c]
                                    hi_w, lo_w = w_hi[:, :, a:z], w_lo[:, :, a:z]
                                else:
                                    a, z = 0, S
                                    hi_w, lo_w = a_hi[:], a_lo[:]
                                into = out_bank(r, c, z - a)
                                at_first = isinstance(i, int) and i == 0
                                if at_first and c == len(chunks):
                                    pe.wait_ge(a_step, KT * S + 2)
                                for k, (ka, kz) in enumerate(blocks):
                                    n = kz - ka
                                    if at_first and c == 0:
                                        pe.wait_ge(w_split, KT if turned_w else k + 1)
                                    pe.matmul(into, xt_hi[0:n, r, k], hi_w[0:n, k], start=(k == 0), stop=False)
                                    pe.matmul(into, xt_hi[0:n, r, k], lo_w[0:n, k], start=False, stop=False)
                                    mm = pe.matmul(into, xt_lo[0:n, r, k], hi_w[0:n, k], start=False,
                                                   stop=(k == KT - 1))
                                mm.then_inc(summed, 1)

                        def body(i, r):
                            turn(i + 1, 1 - r)
                            products(i, r)

                        turn(0, 0)
                        turn_weights(pe)
                        body(0, 0)
                        in_pairs(pe, body, 1, T - 1)
                        products(T - 1, 1)

                    @block.scalar
                    def _(act):
                        def exps(i, r):
                            if elu:
                                stage_is_free(act, i)
                                for a, z, part in pieces(i):
                                    act.activation(stage[:, r, a:z], part, ACT.Exp).then_inc(expd, 1)

                        def high(i, r):
                            if not isinstance(i, int) or i >= 2:
                                act.wait_ge(summed, (i - 1) * NC)
                            for g, ks in enumerate(groups):
                                act.wait_ge(turned, i * NG + (g + 1))
                                for n, ka, kz, of in turned_parts(r, g, ks):
                                    to = xt_hi[0:n, r, ka:kz].rearrange("p k n -> p (k n)")
                                    if relu:
                                        ins = act.activation(to, of, ACT.Relu)
                                    else:
                                        ins = act.activation(to, of, ACT.Copy)
                                ins.then_inc(xt_high, 1)

                        def outs(i, r):
                            if out_hi:
                                for c, (a, z) in enumerate(chunks):
                                    act.wait_ge(summed, i * NC + (c + 1))
                                    act.activation(out_hi(i, a, z), out_bank(r, c, z - a), ACT.Copy,
                                                   scale=1.0 / W_SCALE).then_inc(out_high, 1)
                            if out:
                                for c, (a, z) in enumerate(chunks):
                                    act.wait_ge(summed, i * NC + (c + 1))
                                    act.activation(out(i, a, z), out_bank(r, c, z - a), ACT.Copy,
                                                   scale=1.0 / W_SCALE).then_inc(out_free, 1)
                                act.wait_ge(summed, i * NC + NC)
                                act.activation(scores(i), out_bank(r, NC - 1, S).rearrange("p (e h) -> p e h", e=2),
                                               ACT.Copy, scale=1.0 / W_SCALE).then_inc(out_free, 1)

                        exps(0, 0)
                        exps(1, 1)
                        high_weights(act, 0, EARLY)
                        high(0, 0)
                        high_weights(act, EARLY)

                        def body(i, r):
                            exps(i + 2, r)
                            high(i + 1, 1 - r)
                            outs(i, r)

                        in_pairs(act, body, 0, T - 2)
                        high(T - 1, 1)
                        outs(T - 2, 0)
                        outs(T - 1, 1)

                    @block.vector
                    def _(v):
                        def join(i, r):
                            if elu:
                                v.wait_ge(below, i + 1)
                                for a, z, part in pieces(i):
                                    v.scalar_tensor_tensor(out=stage[:, r, a:z], in0=part, scalar=0.0,
                                                           in1=stage[:, r, a:z], op0=ALU.max,
                                                           op1=ALU.add).then_inc(staged, 1)

                        def split(i, r):
                            for g, ks in enumerate(groups):
                                v.wait_ge(xt_high, i * NG + (g + 1))
                                for n, ka, kz, of in turned_parts(r, g, ks):
                                    to = xt_lo[0:n, r, ka:kz].rearrange("p k n -> p (k n)")
                                    high = xt_hi[0:n, r, ka:kz].rearrange("p k n -> p (k n)")
                                    if relu:
                                        ins = v.scalar_tensor_tensor(out=to, in0=of, scalar=0.0, in1=high,
                                                                     op0=ALU.max, op1=ALU.subtract)
                                    else:
                                        ins = v.tensor_tensor(to, of, high, ALU.subtract)
                                ins.then_inc(slot_free, 1)

                        def outs(i, r):
                            if out:
                                return
                            for c, (a, z) in enumerate(chunks):
                                v.wait_ge(summed, i * NC + (c + 1))
                                of = out_bank(r, c, z - a)
                                if out_hi:
                                    v.wait_ge(out_high, i * len(chunks) + (c + 1))
                                    v.scalar_tensor_tensor(out=out_lo(i, a, z), in0=of, scalar=1.0 / W_SCALE,
                                                           in1=out_hi(i, a, z), op0=ALU.mult,
                                                           op1=ALU.subtract).then_inc(out_free, 1)
                                else:
                                    finish(v, i, a, z, of, out_free, i * NC + (c + 1 + RING))
                            if heads:
                                c = len(chunks)
                                v.wait_ge(summed, i * NC + (c + 1))
                                v.tensor_scalar(scores(i), out_bank(r, c, S).rearrange("p (e h) -> p e h", e=2),
                                                1.0 / W_SCALE, None, ALU.mult).then_inc(out_free, 1)

                        if elu:
                            split_weights(v, 0, EARLY // 2)
                        join(0, 0)
                        if elu:
                            split_weights(v, EARLY // 2, EARLY)
                        join(1, 1)
                        split(0, 0)
                        split_weights(v, EARLY)

                        def body(i, r):
                            split(i + 1, 1 - r)
                            join(i + 2, r)
                            outs(i, r)

                        in_pairs(v, body, 0, T - 2)
                        split(T - 1, 1)
                        outs(T - 2, 0)
                        outs(T - 1, 1)

        def each_unit(eng, body, first, last):
            H, left = divmod(last, T)
            if left < first:
                H, left = H - 1, left + T
            if H:
                with eng.Fori(0, H) as h:
                    for i in range(first, T):
                        body(h, i)
                    for i in range(first):
                        body(h + 1, i)
            for i in range(first, left):
                body(H + i // T, i % T)

        def attention(name, H, C, h_hi, h_lo, scores, logc, bias_d, put, *, load=None, residual=None,
                      load_residual=None, stats=None):
            U = H * T
            ROWS = 2 * H
            acc_chunks = [(a, min(a + BANK, C)) for a in range(0, C, BANK)]
            with ExitStack() as ctx:
                s_row = sb(ctx, f"{name}_s_row", [P, 2, NP], F32)
                s_row_fifth = sb(ctx, f"{name}_s_row_fifth", [P, 2, NP], F32)
                d_most = sb(ctx, f"{name}_d_most", [P, H, T], F32)
                logit = sb(ctx, f"{name}_logit", [P, 2, NP], F32)
                src_rows = logit[0:ROWS, 0]
                peak = sb(ctx, f"{name}_peak", [P, 2], F32)
                denom = sb(ctx, f"{name}_denom", [P, U], F32)
                inv = sb(ctx, f"{name}_inv", [P, 2], F32)
                pt_hi = sb(ctx, f"{name}_pt_hi", [P, 2, T, P], F16 if h_lo else F32)
                pt_lo = sb(ctx, f"{name}_pt_lo", [P, 2, T, P], F16) if h_lo else None
                bias = sb(ctx, f"{name}_bias", [P, H * C], F32)

                rows_turned, rows_saved = sem(f"{name}_rows_turned"), sem(f"{name}_rows_saved")
                rows_out, d_scaled = sem(f"{name}_rows_out"), sem(f"{name}_d_scaled")
                logc_in = [sem(f"{name}_logc_in{i}") for i in range(T)] if load else None
                residual_in, bias_in = sem(f"{name}_residual_in"), sem(f"{name}_bias_in")
                row_in = [sem(f"{name}_row_in{r}") for r in range(2)]
                row_ready = sem(f"{name}_row_ready")
                logit_up, logit_done, expd = sem(f"{name}_logit_up"), sem(f"{name}_logit_done"), sem(f"{name}_expd")
                turned, high, split = sem(f"{name}_turned"), sem(f"{name}_high"), sem(f"{name}_split")
                summed, acc_free, seen = sem(f"{name}_summed"), sem(f"{name}_acc_free"), sem(f"{name}_seen")
                inverted, biased = sem(f"{name}_inverted"), sem(f"{name}_biased")
                SETS = 2
                taken = split if h_lo else high

                def acc(r, a, z):
                    return ps[:, (4 + 2 * r) * BANK + a:(4 + 2 * r) * BANK + z]

                with nc.Block() as block:
                    @block.sync
                    def _(sp):
                        sp.wait_ge(rows_saved, 1)
                        sp.dma_start(src_rows_d[0:H, :], src_rows[0:H]).then_inc(rows_out, 16)
                        sp.wait_ge(rows_out, 16)
                        for h in range(H):
                            if h >= 2:
                                sp.wait_ge(logit_up, (h - 1) * T)
                            sp.dma_start(s_row[:, h % 2], over_partitions(src_rows_d[h])).then_inc(row_in[h % 2], 16)
                            if h == min(1, H - 1):
                                for i in range(T if load else 0):
                                    load(sp, i, logc_in[i])
                                if load_residual:
                                    load_residual(sp, residual_in)

                    @block.gpsimd
                    def _(pool):
                        pool.sem_inc(summed, SETS)
                        pool.sem_inc(acc_free, SETS)
                        pool.dma_start(bias[:], over_partitions(bias_d)).then_inc(bias_in, 16)
                        for h in range(1, H):
                            pool.wait_ge(row_in[h % 2], 16 * (h // 2 + 1))
                            pool.wait_ge(row_ready, h)
                            pool.tensor_scalar(s_row_fifth[:, h % 2], s_row[:, h % 2], 0.2, None,
                                               ALU.mult).then_inc(row_ready, 1)
                        if residual is not None:
                            pool.wait_ge(bias_in, 16)
                            if load_residual:
                                pool.wait_ge(residual_in, 16)
                            for i in range(T):
                                pool.tensor_tensor(residual[:, i], residual[:, i], bias[:],
                                                   ALU.add).then_inc(biased, 1)

                    def after(h, i):
                        return (h, i + 1) if i + 1 < T else (h + 1, 0)

                    def before(h, i, n):
                        return (h, i - n) if i >= n else (h - 1, i + T - n)

                    @block.vector
                    def _(v):
                        def upper(h, i):
                            u, r = h * T + i, i % 2
                            v.wait_ge(row_ready, h + 1)
                            if not isinstance(u, int) or u >= 2:
                                v.wait_ge(turned, (u - 1) * 2)
                            row = h % 2
                            v.scalar_tensor_tensor(out=logit[:, r], in0=tile_of(s_row, row),
                                                   scalar=d_most[:].rearrange("p h t -> p (h t)")[:, bass.ds(u, 1)],
                                                   in1=tile_of(s_row_fifth, row), op0=ALU.add,
                                                   op1=ALU.max).then_inc(logit_up, 1)

                        def greatest(h, i):
                            u, r = h * T + i, i % 2
                            if load:
                                v.wait_ge(logc_in[i], 16)
                            v.wait_ge(logit_up, u + 1)
                            v.sem_inc(seen, 1)
                            v.tensor_tensor_reduce(logit[:, r], logit[:, r], logc[:, i], -1.0, -NO_EDGE / 10,
                                                   ALU.add, ALU.min, peak[:, r:r + 1]).then_inc(logit_done, 1)

                        def low(h, i):
                            u, r = h * T + i, i % 2
                            for g in range(2 if h_lo else 0):
                                v.wait_ge(high, u * 2 + (g + 1))
                                v.tensor_tensor(pt_lo[:, r, g * HB:(g + 1) * HB].rearrange("p k n -> p (k n)"),
                                                ps[:, 2 * g * BANK:2 * g * BANK + HALF],
                                                pt_hi[:, r, g * HB:(g + 1) * HB].rearrange("p k n -> p (k n)"),
                                                ALU.subtract).then_inc(split, 1)

                        def clamp(h, i):
                            u, r = h * T + i, i % 2
                            v.wait_ge(expd, u + 1)
                            v.tensor_scalar(inv[:, r:r + 1], denom[:, bass.ds(u, 1)], 1e-37, None,
                                            ALU.max).then_inc(inverted, 1)

                        def invert(h, i):
                            u, r = h * T + i, i % 2
                            v.wait_ge(inverted, u * 2 + 1)
                            v.reciprocal(inv[:, r:r + 1], inv[:, r:r + 1]).then_inc(inverted, 1)

                        def finish(h, i):
                            u, r = h * T + i, i % 2
                            v.wait_ge(inverted, u * 2 + 2)
                            v.wait_ge(summed, u + (1 + SETS))
                            if residual is not None:
                                v.wait_ge(biased, i + 1)
                                other = residual[:, i]
                            else:
                                other = bias[:, bass.ds(h * C, C)]
                            v.scalar_tensor_tensor(out=put(h, i), in0=acc(r, 0, C), scalar=inv[:, r:r + 1],
                                                   in1=other, op0=ALU.mult, op1=ALU.add).then_inc(acc_free, 1)
                            if stats is not None:
                                v.wait_ge(acc_free, u + (1 + SETS))
                                row_stats(v, stats, i, put(h, i))

                        v.tensor_scalar(d_most[:].rearrange("p h t -> p t h"), scores[:, :, 1], 0.8, None,
                                        ALU.mult).then_inc(d_scaled, 1)
                        v.wait_ge(d_scaled, 1)
                        for i in range(2):
                            upper(0, i)
                            greatest(0, i)
                        low(0, 0)
                        upper(0, 2)
                        greatest(0, 2)
                        low(0, 1)

                        def body(h, i):
                            earlier, later = before(h, i, 2), after(h, i)
                            clamp(*earlier)
                            upper(*later)
                            invert(*earlier)
                            greatest(*later)
                            finish(*earlier)
                            low(h, i)

                        def close(h, i):
                            clamp(h, i)
                            invert(h, i)
                            finish(h, i)

                        v.wait_ge(bias_in, 16)
                        each_unit(v, body, 2, U - 1)
                        close(*before(H - 1, T - 1, 2))
                        low(H - 1, T - 1)
                        close(H - 1, T - 2)
                        close(H - 1, T - 1)

                    @block.scalar
                    def _(act):
                        def exps(h, i):
                            u, r = h * T + i, i % 2
                            act.wait_ge(logit_done, u + 1)
                            act.activation(logit[:, r], logit[:, r], ACT.Exp, bias=peak[:, r:r + 1], scale=-1.0,
                                           accum_out=denom[:, bass.ds(u, 1)]).then_inc(expd, 1)

                        def highs(h, i):
                            u, r = h * T + i, i % 2
                            act.wait_ge(summed, u + 1)
                            for g in range(2):
                                act.wait_ge(turned, u * 2 + (g + 1))
                                act.activation(pt_hi[:, r, g * HB:(g + 1) * HB].rearrange("p k n -> p (k n)"),
                                               ps[:, 2 * g * BANK:2 * g * BANK + HALF], ACT.Copy).then_inc(high, 1)

                        def body(h, i):
                            if h_lo:
                                highs(h, i)
                                exps(*after(h, i))
                            else:
                                exps(*after(h, i))
                                highs(h, i)

                        act.wait_ge(rows_turned, 1)
                        act.activation(src_rows, ps[0:ROWS, 0:NP], ACT.Copy).then_inc(rows_saved, 1)
                        act.wait_ge(row_in[0], 16)
                        act.activation(s_row_fifth[:, 0], s_row[:, 0], ACT.Copy, scale=0.2).then_inc(row_ready, 1)
                        exps(0, 0)
                        body(0, 0)
                        each_unit(act, body, 1, U - 1)
                        highs(H - 1, T - 1)

                    @block.tensor
                    def _(pe):
                        def turn(h, i):
                            u, r = h * T + i, i % 2
                            pe.wait_ge(expd, u + 1)
                            for g in range(2):
                                if not isinstance(u, int) or u > 0:
                                    pe.wait_ge(taken, u * 2 + g - 1)
                                for k in range(HB):
                                    at = 2 * g * BANK + k * P
                                    mm = pe.transpose(ps[:, at:at + P],
                                                      logit[:, r, (g * HB + k) * P:(g * HB + k + 1) * P], ident[:])
                                mm.then_inc(turned, 1)

                        def sums(h, i):
                            u, r = h * T + i, i % 2
                            pe.wait_ge(acc_free, u + 1)
                            for a, z in acc_chunks:
                                for k in range(T):
                                    if a == 0 and k in (0, HB):
                                        pe.wait_ge(taken, u * 2 + (k // HB + 1))
                                    into = acc(r, a, z)
                                    if not h_lo:
                                        mm = pe.matmul(into, pt_hi[:, r, k], h_hi(k, h, a, z), start=(k == 0),
                                                       stop=(k == T - 1))
                                        continue
                                    pe.matmul(into, pt_hi[:, r, k], h_hi(k, h, a, z), start=(k == 0), stop=False)
                                    pe.matmul(into, pt_hi[:, r, k], h_lo(k, h, a, z), start=False, stop=False)
                                    mm = pe.matmul(into, pt_lo[:, r, k], h_hi(k, h, a, z), start=False,
                                                   stop=(k == T - 1))
                            mm.then_inc(summed, 1)

                        def body(h, i):
                            turn(*after(h, i))
                            sums(h, i)

                        for i in range(T):
                            mm = pe.transpose(ps[0:ROWS, i * P:(i + 1) * P],
                                              scores[:, i].rearrange("p e h -> p (e h)"), ident[:])
                        mm.then_inc(rows_turned, 1)
                        turn(0, 0)
                        body(0, 0)
                        each_unit(pe, body, 1, U - 1)
                        sums(H - 1, T - 1)

        def row_stats(v, stats, i, row):
            for h in range(2):
                ins_ = v.bn_stats(stats[:, bass.ds(i, 1), h].rearrange("p o s -> p (o s)"),
                                  row[:, h * (D // 2):(h + 1) * (D // 2)])
            return ins_

        def layer_norm(name, x, to=None, affine=None, store=None, stats=None):
            to = x if to is None else to
            with ExitStack() as ctx:
                known = stats is not None
                if not known:
                    stats = sb(ctx, f"{name}_stats", [P, T, 2, 6], F32)
                mean_var = sb(ctx, f"{name}_mean_var", [P, T, 2], F32)
                std = sb(ctx, f"{name}_std", [P, T], F32)
                offset = sb(ctx, f"{name}_offset", [P, T], F32)
                rows = sb(ctx, f"{name}_rows", [P, 2, D], F32) if affine else None
                dve, rooted, rows_in = sem(f"{name}_dve"), sem(f"{name}_rooted"), sem(f"{name}_rows_in")
                known_stats = sem(f"{name}_known_stats")
                on_act = [i for i in range(T) if i % 2 and not affine]
                on_dve = [i for i in range(T) if i not in on_act]
                act_normed, dve_normed = sem(f"{name}_act_normed"), sem(f"{name}_dve_normed")
                with nc.Block() as block:
                    @block.vector
                    def _(v):
                        if not known:
                            for i in range(T):
                                row_stats(v, stats, i, x[:, i]).then_inc(known_stats, 1)
                            v.wait_ge(known_stats, T)
                        for i in range(T):
                            v.bn_aggr(mean_var[:, i], stats[:, i].rearrange("p a b -> p (a b)")).then_inc(dve, 1)
                        v.wait_ge(dve, T)
                        v.tensor_scalar(std[:], mean_var[:, :, 1], LN_EPS, None, ALU.add).then_inc(dve, 1)
                        v.wait_ge(rooted, 1)
                        v.reciprocal(std[:], std[:]).then_inc(dve, 1)
                        v.wait_ge(dve, T + 2)
                        v.scalar_tensor_tensor(out=offset[:], in0=mean_var[:, :, 0], scalar=-1.0, in1=std[:],
                                               op0=ALU.mult, op1=ALU.mult).then_inc(dve, 1)
                        if affine:
                            v.wait_ge(rows_in, 32)
                            for i in on_dve:
                                v.scalar_tensor_tensor(out=to[:, i], in0=x[:, i], scalar=mean_var[:, i, 0:1],
                                                       in1=rows[:, 0], op0=ALU.subtract,
                                                       op1=ALU.mult).then_inc(dve, 1)
                            for i in on_dve:
                                v.wait_ge(dve, T + 4 + i)
                                v.scalar_tensor_tensor(out=to[:, i], in0=to[:, i], scalar=std[:, i:i + 1],
                                                       in1=rows[:, 1], op0=ALU.mult,
                                                       op1=ALU.add).then_inc(dve_normed, 1)
                        else:
                            for i in on_dve:
                                v.tensor_scalar(to[:, i], x[:, i], mean_var[:, i, 0:1], std[:, i:i + 1],
                                                ALU.subtract, ALU.mult).then_inc(dve_normed, 1)

                    @block.scalar
                    def _(act):
                        act.wait_ge(dve, T + 1)
                        act.activation(std[:], std[:], ACT.Sqrt).then_inc(rooted, 1)
                        act.wait_ge(dve, T + 3)
                        for i in on_act:
                            act.activation(to[:, i], x[:, i], ACT.Identity, bias=offset[:, i:i + 1],
                                           scale=std[:, i:i + 1]).then_inc(act_normed, 1)

                    @block.gpsimd
                    def _(pool):
                        if affine:
                            for k in range(2):
                                pool.dma_start(rows[:, k], over_partitions(affine[k])).then_inc(rows_in, 16)
                            pool.wait_ge(rows_in, 32)

                    @block.sync
                    def _(sp):
                        if store:
                            for i in range(T):
                                if i in on_act:
                                    sp.wait_ge(act_normed, on_act.index(i) + 1)
                                else:
                                    sp.wait_ge(dve_normed, on_dve.index(i) + 1)
                                store(sp, i)

        early = ExitStack()
        with ExitStack() as counting:
            count = counting.enter_context(nc.sbuf_tensor("count", [P, T, NP], U16, side="right"))
            hi = counting.enter_context(nc.sbuf_tensor("sm_hi", [P, T, WIDE], F32R, side="right"))
            lo = counting.enter_context(nc.sbuf_tensor("sm_lo", [P, T, WIDE], F32R, side="right"))
            tcol = counting.enter_context(nc.sbuf_tensor("tcol", [P, 1], F32, side="right"))
            shift = counting.enter_context(nc.sbuf_tensor("shift", [P, 1], F32, side="right"))
            bands = counting.enter_context(nc.sbuf_tensor("bands", [1, 1], I32, side="right"))
            count_and_weigh(count, hi, lo, tcol, shift, bands, ins["L0_gnn_t"])
            x = sb(early, "x0", [P, T, D], F32)

            BN = ins["L0_gnn_W1"].shape[1] // P
            bn_small = sb(counting, "bn_small", [BN, 5, P], F32)
            var, gamma, b1, mean, beta = (bn_small[:, k] for k in range(5))
            bn_given, bn_step, bn_root, bn_out = sem("bn_given"), sem("bn_step"), sem("bn_root"), sem("bn_out")

            def bn_load_and_store(sp):
                for k, key in enumerate(("bn_var", "bn_gamma", "b1", "bn_mean", "bn_beta")):
                    sp.dma_start(bn_small[:, k], ins[f"L0_gnn_{key}"].rearrange("(a b) -> a b", b=P)
                                 ).then_inc(bn_given, 16)
                sp.wait_ge(bn_step, 7)
                for k, part in enumerate((var, b1)):
                    sp.dma_start(bn_d[k].rearrange("(a b) -> a b", b=P), part).then_inc(bn_out, 16)
                sp.wait_ge(bn_out, 32)

            def bn_sqrt(act):
                act.wait_ge(bn_step, 1)
                act.activation(var, var, ACT.Sqrt).then_inc(bn_root, 1)

            def bn_work_out(v):
                done = [0]

                def step(ins_):
                    done[0] += 1
                    ins_.then_inc(bn_step, 1)
                    v.wait_ge(bn_step, done[0])

                v.wait_ge(bn_given, 5 * 16)
                step(v.tensor_scalar(var, var, LN_EPS, None, ALU.add))
                v.wait_ge(bn_root, 1)
                step(v.reciprocal(var, var))
                step(v.tensor_tensor(var, var, gamma, ALU.mult))
                step(v.tensor_tensor(b1, b1, mean, ALU.subtract))
                step(v.tensor_tensor(b1, b1, var, ALU.mult))
                step(v.tensor_tensor(b1, b1, beta, ALU.add))
                step(v.tensor_scalar(var, var, 1.0 / W_SCALE, None, ALU.mult))

            channel_softmax("m", x, count, hi, lo,
                            beside={"scalar": bn_sqrt, "vector": bn_work_out, "sync": bn_load_and_store})
            with nc.If(nc.values_load(bands[0:1, 0:1], min_val=1, max_val=10 ** 6) > 1):
                softmax_in_bands(x, count, hi, lo, tcol, shift, bands)
            nc.end_all_ifs()

        F0 = ins["L0_gnn_W1"].shape[1]
        with ExitStack() as ctx:
            z = sb(ctx, "z", [P, T, F0], F32)
            with ExitStack() as ctx2:
                bn = sb(ctx2, "bn", [P, 2, F0], F32)
                bn_in = sem("bn_in")

                def bn_load(pool):
                    for k in range(2):
                        pool.dma_start(bn[:, k], over_partitions(bn_d[k])).then_inc(bn_in, 16)

                def batch_norm(v, i, a, z_, of, of_free, first_done):
                    to = z[:, bass.ds(i, 1), a:z_].rearrange("p o c -> p (o c)")
                    v.tensor_tensor(to, of, bn[:, 0, a:z_], ALU.mult).then_inc(of_free, 1)
                    v.wait_ge(of_free, first_done)
                    v.tensor_tensor(to, to, bn[:, 1, a:z_], ALU.add)

                linear("l0a", lambda i: [(0, D, tile_of(x, i))], D, ins["L0_gnn_W1"], F0, finish=batch_norm,
                       beside={"gpsimd": bn_load, "vector": lambda v: v.wait_ge(bn_in, 32)})

            b2 = sb(ctx, "b2_0", [P, D], F32)
            summand = sb(ctx, "summand0", [P, 2, BANK], F32)
            again = sem("x_again")

            def x_again(sp):
                sp.dma_start(x[:, 0:T - 1], x_d[0:(T - 1) * P, :].rearrange("(t p) c -> p t c", p=P)
                             ).then_inc(again, 16)
                sp.dma_start(x[0:LAST, T - 1], x_d[(T - 1) * P:N, :]).then_inc(again, 16)

            def add_twice(times, row_done):
                def finish(v, i, a, z_, of, of_free, first_done):
                    tmp = summand[:, (a // BANK) % 2, 0:z_ - a]
                    v.scalar_tensor_tensor(out=tmp, in0=of, scalar=1.0 / W_SCALE, in1=b2[:, a:z_], op0=ALU.mult,
                                           op1=ALU.add).then_inc(of_free, 1)
                    v.wait_ge(of_free, first_done)
                    to = x[:, bass.ds(i, 1), a:z_].rearrange("p o c -> p (o c)")
                    ins_ = v.scalar_tensor_tensor(out=to, in0=to, scalar=times, in1=tmp, op0=ALU.mult, op1=ALU.add)
                    ins_.then_inc(row_done, 1)
                    if z_ == D:
                        v.wait_ge(row_done, (i + 1) * -(-D // BANK))
                        row_stats(v, stats, i, tile_of(x, i))
                return finish

            linear("l0b", lambda i: [(0, F0, tile_of(z, i))], F0, ins["L0_gnn_W2"], D,
                   finish=add_twice(2.0, sem("row_done0")), rows=[(b2[:], ins["L0_gnn_b2"])], relu=True,
                   beside={"sync": x_again, "vector": lambda v: v.wait_ge(again, 32)})

        x_away = nc.alloc_semaphore("x_away")

        def spill(sp, i):
            sp.dma_start(x_spill[:, i], x[:, i]).then_inc(x_away, 16)

        layer_norm("n0", x, store=spill, stats=stats)

        recycle_semaphores()

        H1, C1 = ins["L1_gnn_a1_src"].shape
        wide = ExitStack()
        slots = wide.enter_context(nc.sbuf_tensor("slots", [P, H1 + 1, T, C1], F32, side="right"))
        halves = slots[:].bitcast(F16).rearrange("p h t c -> p h (t c)")
        halves = halves.rearrange("p h (e t c) -> p h e t c", e=2, t=T)
        scores1 = wide.enter_context(nc.sbuf_tensor("scores1", [P, T, 2, H1], F32, side="right"))
        HH = H1 // 2

        def slot_half(e, first):
            def where(i, a, z_):
                h = first + a // C1
                return halves[:, h + 1, e, bass.ds(i, 1), :].rearrange("p o c -> p (o c)")
            return where

        for part in range(2):
            first = part * HH
            linear(f"l1a{part}", lambda i: [(0, D, tile_of(x, i))], D,
                   ins["L1_gnn_W1"][:, first * C1:(first + HH) * C1], HH * C1, out_hi=slot_half(0, first),
                   out_lo=slot_half(1, first), heads=HH,
                   att=[ins["L1_gnn_a1_src"][first:first + HH, :], ins["L1_gnn_a1_dst"][first:first + HH, :]],
               w_ring=-(-D // P),
                   scores=lambda i, first=first: scores1[:, bass.ds(i, 1), :, first:first + HH]
                   .rearrange("p o e h -> p (o e) h"))
        early.close()

        def load_logs(logc):
            return lambda sp, i, loaded: sp.dma_start(logc[:, i], logc_d[:, i]).then_inc(loaded, 16)

        def load_diagonal(sp, i, loaded):
            sp.dma_start(logc[:, i, i * P:(i + 1) * P], logc_diag_d[:, i]).then_inc(loaded, 16)

        def head_half(e):
            return lambda k, h, a, z_: halves[:, bass.ds(h + 1, 1), e, k, a:z_].rearrange("p o c -> p (o c)")

        with ExitStack() as ctx:
            logc = sb(ctx, "logc1", [P, T, NP], F32)
            attention("t1a", H1, C1, head_half(0), head_half(1), scores1, logc, ins["L1_gnn_b1"],
                      lambda h, i: slots[:, bass.ds(h, 1), bass.ds(i, 1), :].rearrange("p a b c -> p (a b c)"),
                      load=load_logs(logc))

        mid = ExitStack()
        feat_hi = sb(mid, "feat1_hi", [P, T, D], F16)
        feat_lo = sb(mid, "feat1_lo", [P, T, D], F16)
        scores2 = sb(mid, "scores2", [P, T, 2, 1], F32)

        def tile_half(t):
            return lambda i, a, z_: t[:, bass.ds(i, 1), a:z_].rearrange("p o c -> p (o c)")

        def feature_half(t, C):
            return lambda k, h, a, z_: (t[:, k, a:z_] if isinstance(h, int) and h == 0 else
                                        t[:, k, bass.ds(h * C + a, z_ - a)])

        def tile_scores(s):
            return lambda i: s[:, bass.ds(i, 1)].rearrange("p o e h -> p (o e) h")

        linear("l1b", lambda i: [(h * C1, (h + 1) * C1, slots[:, h, bass.ds(i, 1), :].rearrange("p o c -> p (o c)"))
                                 for h in range(H1)],
               H1 * C1, ins["L1_gnn_W2"], D, out_hi=tile_half(feat_hi), out_lo=tile_half(feat_lo), elu=True, heads=1,
               att=[ins["L1_gnn_a2_src"], ins["L1_gnn_a2_dst"]], scores=tile_scores(scores2),
               w_room=feat_lo[:].rearrange("p t c -> p (t c)").bitcast(F32), w_ring=5,
               junk_room=feat_hi[:].rearrange("p t c -> p (t c)").bitcast(F32),
               room=[halves[:, H1, e].rearrange("p t c -> p (t c)") for e in range(2)])
        wide.close()

        x = root.enter_context(nc.sbuf_tensor("x1", [P, T, D], F32, side="right"))
        logc = root.enter_context(nc.sbuf_tensor("logc", [P, T, NP], F32, side="right"))

        def load_x(sp, loaded):
            sp.wait_ge(x_away, 16 * T)
            sp.dma_start(x[:], x_spill).then_inc(loaded, 16)

        attention("t1b", 1, D, feature_half(feat_hi, D), feature_half(feat_lo, D), scores2, logc, ins["L1_gnn_b2"],
                  lambda h, i: tile_of(x, i), load=load_logs(logc), residual=x,
                  load_residual=load_x, stats=stats)
        mid.close()
        layer_norm("n1", x, stats=stats)

        recycle_semaphores()

        H2, C2 = ins["L2_gnn_a_src1"].shape
        H3, C3 = ins["L2_gnn_a_src2"].shape
        FB = H3 * C3
        with ExitStack() as ctx:
            out2 = sb(ctx, "out2", [P, T, FB], F32)
            with ExitStack() as ctx2:
                out1 = sb(ctx2, "out1", [P, T, H2 * C2], F32)
                with ExitStack() as ctx3:
                    layer_norm("n2", x, to=out1, affine=[ins["L2_gnn_norm_g"], ins["L2_gnn_norm_b"]])
                    feat = sb(ctx3, "feat2", [P, T, H2 * C2], F32)
                    sc = sb(ctx3, "scores3", [P, T, 2, H2], F32)
                    linear("l2a", lambda i: [(0, D, tile_of(out1, i))], D, ins["L2_gnn_W1"], H2 * C2,
                           out=tile_half(feat), heads=H2,
                           att=[ins["L2_gnn_a_src1"], ins["L2_gnn_a_dst1"]], scores=tile_scores(sc))
                    attention("t2a", H2, C2, feature_half(feat, C2), None, sc, logc,
                              ins["L2_gnn_b1"],
                              lambda h, i: out1[:, bass.ds(i, 1), bass.ds(h * C2, C2)].rearrange("p o c -> p (o c)"))
                feat = sb(ctx2, "feat3", [P, T, FB], F32)
                sc = sb(ctx2, "scores4", [P, T, 2, H3], F32)
                linear("l2b", lambda i: [(0, H2 * C2, tile_of(out1, i))], H2 * C2, ins["L2_gnn_W2"], FB,
                       w_ring=-(-H2 * C2 // P),
                       out=tile_half(feat), heads=H3,
                       att=[ins["L2_gnn_a_src2"], ins["L2_gnn_a_dst2"]], scores=tile_scores(sc))
                attention("t2b", H3, C3, feature_half(feat, C3), None, sc, logc,
                          ins["L2_gnn_b2"],
                          lambda h, i: out2[:, bass.ds(i, 1), bass.ds(h * C3, C3)].rearrange("p o c -> p (o c)"))
            b2 = sb(ctx, "b2_2", [P, D], F32)
            summand = sb(ctx, "summand2", [P, 2, BANK], F32)
            linear("l2c", lambda i: [(0, D, tile_of(x, i)), (D, D + FB, tile_of(out2, i))], D + FB,
                   ins["L2_gnn_Wu"], D, finish=add_twice(1.0, sem("row_done2")), rows=[(b2[:], ins["L2_gnn_bu"])])
        layer_norm("n3", x, stats=stats)

        recycle_semaphores()

        H4, C4 = ins["L3_gnn_att_src1"].shape
        with ExitStack() as ctx:
            out3 = sb(ctx, "out3", [P, T, H4 * C4], F32)
            with ExitStack() as ctx2:
                feat = sb(ctx2, "feat4", [P, T, H4 * C4], F32)
                sc = sb(ctx2, "scores5", [P, T, 2, H4], F32)
                linear("l3a", lambda i: [(0, D, tile_of(x, i))], D, ins["L3_gnn_W1"], H4 * C4,
                       out=tile_half(feat), turned_w=True, heads=H4,
                       att=[ins["L3_gnn_att_src1"], ins["L3_gnn_att_dst1"]], scores=tile_scores(sc),
                       w_room=out3[:].rearrange("p t c -> p (t c)"))
                attention("t3a", H4, C4, feature_half(feat, C4), None, sc, logc,
                          ins["L3_gnn_b1"],
                          lambda h, i: out3[:, bass.ds(i, 1), bass.ds(h * C4, C4)].rearrange("p o c -> p (o c)"),
                          load=load_diagonal)
            feat = sb(ctx, "feat5", [P, 2, T, D], F16)
            f_hi, f_lo = feat[:, 0], feat[:, 1]
            sc = sb(ctx, "scores6", [P, T, 2, 1], F32)
            linear("l3b", lambda i: [(0, H4 * C4, tile_of(out3, i))], H4 * C4, ins["L3_gnn_W2"], D,
                   out_hi=tile_half(f_hi), out_lo=tile_half(f_lo), turned_w=True, relu=True, heads=1,
                   att=[ins["L3_gnn_att_src2"], ins["L3_gnn_att_dst2"]], scores=tile_scores(sc),
                   w_room=feat[:].rearrange("p e t c -> p (e t c)").bitcast(F32))
            attention("t3b", 1, D, feature_half(f_hi, D), feature_half(f_lo, D), sc, logc, ins["L3_gnn_b2"],
                      lambda h, i: tile_of(x, i), residual=x, stats=stats)

        out_stored = sem("out_stored")

        def store_out(sp, i):
            rows = P if i < T - 1 else LAST
            sp.dma_start(out[i * P:i * P + rows, :], x[0:rows, i]).then_inc(out_stored, 16)
            if i == T - 1:
                sp.wait_ge(out_stored, 16 * T)

        layer_norm("n4", x, store=store_out, stats=stats)


_INS = ["x", "src", "dst", "L0_gnn_t", "L0_gnn_W1", "L0_gnn_b1", "L0_gnn_bn_gamma", "L0_gnn_bn_beta",
        "L0_gnn_bn_mean", "L0_gnn_bn_var", "L0_gnn_W2", "L0_gnn_b2", "L1_gnn_W1", "L1_gnn_a1_src", "L1_gnn_a1_dst",
        "L1_gnn_b1", "L1_gnn_W2", "L1_gnn_a2_src", "L1_gnn_a2_dst", "L1_gnn_b2", "L2_gnn_norm_g", "L2_gnn_norm_b",
        "L2_gnn_W1", "L2_gnn_a_src1", "L2_gnn_a_dst1", "L2_gnn_b1", "L2_gnn_W2", "L2_gnn_a_src2", "L2_gnn_a_dst2",
        "L2_gnn_b2", "L2_gnn_Wu", "L2_gnn_bu", "L3_gnn_W1", "L3_gnn_att_src1", "L3_gnn_att_dst1", "L3_gnn_b1",
        "L3_gnn_W2", "L3_gnn_att_src2", "L3_gnn_att_dst2", "L3_gnn_b2"]


def kernel(**inputs):
    import numpy as _np
    import concourse.bacc as _bacc
    from concourse import mybir as _mybir
    from concourse.bass_utils import run_bass_kernel_spmd as _run

    nc = _bacc.Bacc("TRN2", target_bir_lowering=False, num_devices=1)
    arrays, args = {}, {}
    for name in _INS:
        a = _np.ascontiguousarray(inputs[name])
        if a.ndim == 0:
            a = a.reshape(1)
        arrays[f"in_{name}_dram"] = a
        args[name] = nc.dram_tensor(f"in_{name}_dram", a.shape, _mybir.dt.from_np(a.dtype), kind="ExternalInput").ap()
    out = nc.dram_tensor("out_dram", inputs["x"].shape, _mybir.dt.float32, kind="ExternalOutput").ap()
    bass_gnn_kernel(nc, args, out)
    r = _run(nc, [arrays], core_ids=[0])
    return r.results[0]["out_dram"]
```
